# Optimizing a Trainium2 kernel written in Bass

```python
import numpy as np
import jax
import jax.numpy as jnp

def _softmax(x, axis=-1):
    return jax.nn.softmax(x, axis=axis)

def _gelu(x):
    return jax.nn.gelu(x, approximate=True)

def _silu(x):
    return jax.nn.silu(x)

def _sigmoid(x):
    return jax.nn.sigmoid(x)

def _layernorm(x, axis=-1, eps=1e-05):
    m = jnp.mean(x, axis=axis, keepdims=True)
    v = jnp.var(x, axis=axis, keepdims=True)
    return (x - m) / jnp.sqrt(v + eps)

def _scatter_add(tgt, idx, src, axis=0):
    return tgt.at[idx].add(src)

def _segment_sum(src, seg, n):
    return jax.ops.segment_sum(src, seg, n)
kernel_name = 'mk_decoder_postln_d2_seqx_r4_780644'

def setup_inputs(seed: int=0):
    np.random.seed(seed)
    _w = jnp.asarray

    def _rec_inputs():
        import jax
        import jax.numpy as jnp
        _rk = jax.random.key(seed)
        x = 7.22e-05 + 1 * jax.random.normal(jax.random.fold_in(_rk, 1), (2, 1024, 256), jnp.float32)
        _lenS = 1024 - jax.random.randint(jax.random.fold_in(_rk, 7), (2,), 0, max(1, 1024 // 4) + 1, jnp.int32)
        _lenS2 = 77 - jax.random.randint(jax.random.fold_in(_rk, 8), (2,), 0, max(1, 77 // 4) + 1, jnp.int32)
        _ctx_1024P = jax.random.normal(jax.random.fold_in(_rk, 11), (2, 16, 256), jnp.float32)
        _ctx_1024c = jax.random.dirichlet(jax.random.fold_in(_rk, 511), 0.3 * jnp.ones((16,), jnp.float32), (2, 77))
        _ctx_1024t = jnp.einsum('bsk,bkd->bsd', _ctx_1024c, _ctx_1024P)
        _ctx_1024t = _ctx_1024t * jax.lax.rsqrt(jnp.mean(jnp.square(_ctx_1024t)) + 1e-12) * 0.953939
        ctx_1024 = 4.13588e-05 + 0.999923 * (_ctx_1024t + 0.3 * jax.random.normal(jax.random.fold_in(_rk, 611), (2, 77, 256), jnp.float32))
        fside_1x16xSxS2_0 = 8.74812e-05 + 1.00005 * jax.random.normal(jax.random.fold_in(_rk, 12), (1, 16, 1024, 77), jnp.float32)
        _validS = jnp.arange(1024)[None, :] < _lenS[:, None]
        _validS2 = jnp.arange(77)[None, :] < _lenS2[:, None]
        _causal = jnp.tril(jnp.ones((1024, 1024), dtype=bool))
        mask_Bx1x1xS2_ff0 = jnp.where(jnp.ones((2, 1, 1, 77), dtype=bool), 0.0, -1000000000.0).astype(jnp.float32)
        return (x, ctx_1024, fside_1x16xSxS2_0, mask_Bx1x1xS2_ff0)
    x, ctx_1024, fside_1x16xSxS2_0, mask_Bx1x1xS2_ff0 = _rec_inputs()

    def _L0_attn_setup():
        import jax, jax.numpy as jnp
        import numpy as np
        NUM_HEADS = 16
        key = jax.random.key(seed)
        ks = jax.random.split(key, 6)
        B, S, D = (2, 512, 256)
        x = jax.random.normal(ks[0], (B, S, D), dtype=jnp.float32)
        s = 1.0 / np.sqrt(D)
        Wq = jax.random.normal(ks[1], (D, D), dtype=jnp.float32) * s
        Wk = jax.random.normal(ks[2], (D, D), dtype=jnp.float32) * s
        Wv = jax.random.normal(ks[3], (D, D), dtype=jnp.float32) * s
        Wff = jax.random.normal(ks[4], (D, D), dtype=jnp.float32) * s
        bff = jax.random.normal(ks[5], (D,), dtype=jnp.float32) * 0.01
        return {'x': x, 'Wq': Wq, 'Wk': Wk, 'Wv': Wv, 'Wff': Wff, 'bff': bff}
    _L0_attn_all = _L0_attn_setup()
    _L0_attn_in = {k: v for k, v in _L0_attn_all.items() if k in ('Wq', 'Wk', 'Wv', 'Wff', 'bff')}
    del _L0_attn_all

    def _L0_xattn_setup():
        import jax, jax.numpy as jnp
        import numpy as np
        DIM = 256
        HEADS = 16
        DIM_HEAD = 64
        INNER = HEADS * DIM_HEAD
        SCALE = DIM_HEAD ** (-0.5)
        B, N = (4, 512)

        def _split_heads(t):
            b, n, _ = t.shape
            return t.reshape(b, n, HEADS, DIM_HEAD).transpose(0, 2, 1, 3)

        def _attn_block(q_src, k_src, v_src, Wq, Wk, Wv, Wo, bo):
            q = _split_heads(q_src @ Wq)
            k = _split_heads(k_src @ Wk)
            v = _split_heads(v_src @ Wv)
            dots = jnp.einsum('bhid,bhjd->bhij', q, k) * SCALE
            attn = jax.nn.softmax(dots, axis=-1)
            out = jnp.einsum('bhij,bhjd->bhid', attn, v)
            out = out.transpose(0, 2, 1, 3).reshape(q_src.shape[0], q_src.shape[1], INNER)
            return out @ Wo + bo
        key = jax.random.key(seed)
        ks = jax.random.split(key, 7)
        s = DIM ** (-0.5)
        return {'x1': jax.random.normal(ks[0], (B, N, DIM), jnp.float32), 'x2': jax.random.normal(ks[1], (B, N, DIM), jnp.float32), 'Wq': jax.random.normal(ks[2], (DIM, INNER), jnp.float32) * s, 'Wk': jax.random.normal(ks[3], (DIM, INNER), jnp.float32) * s, 'Wv': jax.random.normal(ks[4], (DIM, INNER), jnp.float32) * s, 'Wo': jax.random.normal(ks[5], (INNER, DIM), jnp.float32) * INNER ** (-0.5), 'bo': jnp.zeros((DIM,), jnp.float32)}
    _L0_xattn_all = _L0_xattn_setup()
    _L0_xattn_in = {k: v for k, v in _L0_xattn_all.items() if k in ('Wq', 'Wk', 'Wv', 'Wo', 'bo')}
    del _L0_xattn_all

    def _L0_ffn_setup():
        import jax, jax.numpy as jnp
        import numpy as np
        MICRO_BATCHES = 2
        TOP_K = 2
        LN_EPS = 1e-05
        B, S, D = (4, 1024, 256)
        E = 8
        DFF = 4 * D

        def _layernorm(x, g, b):
            mu = jnp.mean(x, axis=-1, keepdims=True)
            var = jnp.mean(jnp.square(x - mu), axis=-1, keepdims=True)
            return (x - mu) * jax.lax.rsqrt(var + LN_EPS) * g + b
        key = jax.random.key(seed)
        ks = jax.random.split(key, 12)
        sd = 1.0 / np.sqrt(D)
        sf = 1.0 / np.sqrt(DFF)
        return {'x': jax.random.normal(ks[0], (B, S, D), dtype=jnp.float32), 'ln_g': jnp.ones((D,), jnp.float32), 'ln_b': jnp.zeros((D,), jnp.float32), 'attn_w': jax.random.normal(ks[1], (D, D), jnp.float32) * sd, 'attn_b': jnp.zeros((D,), jnp.float32), 'gate_w': jax.random.normal(ks[2], (D, E), jnp.float32) * sd, 'w1': jax.random.normal(ks[3], (E, D, DFF), jnp.float32) * sd, 'b1': jnp.zeros((E, DFF), jnp.float32), 'w2': jax.random.normal(ks[4], (E, DFF, D), jnp.float32) * sf, 'b2': jnp.zeros((E, D), jnp.float32), 'next_w': jax.random.normal(ks[5], (D, D), jnp.float32) * sd, 'next_b': jnp.zeros((D,), jnp.float32)}
    _L0_ffn_all = _L0_ffn_setup()
    _L0_ffn_in = {k: v for k, v in _L0_ffn_all.items() if k in ('ln_g', 'ln_b', 'attn_w', 'attn_b', 'gate_w', 'w1', 'b1', 'w2', 'b2', 'next_w', 'next_b')}
    del _L0_ffn_all

    def _L1_attn_setup():
        import jax, jax.numpy as jnp
        import numpy as np
        HEADS, DIM_HEAD, LANDMARKS, PINV_ITERS = (8, 64, 64, 6)
        WQK_DIM = 64
        CONV_K = 33

        def moore_penrose_pinv(x, iters):
            I = jnp.eye(x.shape[-1], dtype=x.dtype)
            abs_x = jnp.abs(x)
            scale = jnp.max(abs_x.sum(-1)) * jnp.max(abs_x.sum(-2))
            z = jnp.swapaxes(x, -1, -2) / scale
            for _ in range(iters):
                xz = x @ z
                z = 0.25 * z @ (13 * I - xz @ (15 * I - xz @ (7 * I - xz)))
            return z

        def nystrom_attention(x, qkv_w, out_w, out_b, conv_w):
            b, n, d = x.shape
            h, dh, m = (HEADS, DIM_HEAD, LANDMARKS)
            scale = dh ** (-0.5)
            qkv = x @ qkv_w
            q, k, v = jnp.split(qkv, 3, axis=-1)
            split = lambda t: t.reshape(b, n, h, dh).transpose(0, 2, 1, 3)
            q, k, v = (split(q) * scale, split(k), split(v))
            l = n // m
            q_l = q.reshape(b, h, m, l, dh).mean(axis=3)
            k_l = k.reshape(b, h, m, l, dh).mean(axis=3)
            attn1 = jax.nn.softmax(jnp.einsum('bhid,bhjd->bhij', q, k_l), axis=-1)
            attn2 = jax.nn.softmax(jnp.einsum('bhid,bhjd->bhij', q_l, k_l), axis=-1)
            attn3 = jax.nn.softmax(jnp.einsum('bhid,bhjd->bhij', q_l, k), axis=-1)
            attn2_inv = moore_penrose_pinv(attn2, PINV_ITERS)
            out = attn1 @ (attn2_inv @ (attn3 @ v))
            pad = CONV_K // 2
            res = jax.lax.conv_general_dilated(v, conv_w, window_strides=(1, 1), padding=((pad, pad), (0, 0)), dimension_numbers=('NCHW', 'OIHW', 'NCHW'), feature_group_count=h)
            out = out + res
            out = out.transpose(0, 2, 1, 3).reshape(b, n, h * dh)
            return out @ out_w + out_b

        def _reference_tuple_inner(dense, adj_rows, adj_cols, adj_vals, wq, wk, wv_w, wv_b, qkv_w, out_w, out_b, conv_w):
            b, n, d = dense.shape
            xg = nystrom_attention(dense, qkv_w, out_w, out_b, conv_w)
            enc = xg[0] + dense
            q = enc @ wq
            k = enc @ wk
            scores = jnp.einsum('bid,bjd->bij', q, k) / jnp.sqrt(jnp.float32(WQK_DIM))
            data = scores[0]
            contrib = adj_vals * data[adj_rows, adj_cols]
            A_raw = jax.ops.segment_sum(contrib, adj_rows, num_segments=n)
            alpha = jax.nn.softmax(A_raw)
            value = dense @ wv_w + wv_b
            xl = alpha[:, None] * value
            wei = jax.nn.sigmoid(-xl)
            sw = wei * wei
            xo = xl * 2 * sw + 2 * enc * (1 - sw)
            return (xo, A_raw)
        key = jax.random.key(seed)
        ks = jax.random.split(key, 12)
        n, d, E = (2048, 256, 32768)
        inner = HEADS * DIM_HEAD
        s = lambda fan: (1.0 / np.sqrt(fan)).astype(np.float32) if isinstance(fan, np.ndarray) else np.float32(1.0 / np.sqrt(fan))
        return {'dense': jax.random.normal(ks[0], (1, n, d), jnp.float32), 'adj_rows': jax.random.randint(ks[1], (E,), 0, n), 'adj_cols': jax.random.randint(ks[2], (E,), 0, n), 'adj_vals': jax.random.uniform(ks[3], (E,), jnp.float32), 'wq': jax.random.normal(ks[4], (d, WQK_DIM), jnp.float32) * s(d), 'wk': jax.random.normal(ks[5], (d, WQK_DIM), jnp.float32) * s(d), 'wv_w': jax.random.normal(ks[6], (d, d), jnp.float32) * s(d), 'wv_b': jnp.zeros((d,), jnp.float32), 'qkv_w': jax.random.normal(ks[7], (d, 3 * inner), jnp.float32) * s(d), 'out_w': jax.random.normal(ks[8], (inner, d), jnp.float32) * s(inner), 'out_b': jnp.zeros((d,), jnp.float32), 'conv_w': jax.random.normal(ks[9], (HEADS, 1, CONV_K, 1), jnp.float32) * s(CONV_K)}
    _L1_attn_all = _L1_attn_setup()
    _L1_attn_in = {k: v for k, v in _L1_attn_all.items() if k in ('adj_rows', 'adj_cols', 'adj_vals', 'wq', 'wk', 'wv_w', 'wv_b', 'qkv_w', 'out_w', 'out_b', 'conv_w')}
    del _L1_attn_all

    def _L1_xattn_setup():
        import jax, jax.numpy as jnp
        import numpy as np
        HIDDEN = 256
        NUM_HEADS = 16
        HEAD_DIM = 64
        key = jax.random.key(seed)
        ks = jax.random.split(key, 8)
        B, Sq, Skv = (4, 512, 512)
        scale = 1.0 / np.sqrt(HIDDEN)
        inp = {'q_hidden_states': jax.random.normal(ks[0], (B, Sq, HIDDEN), jnp.float32), 'kv_hidden_states': jax.random.normal(ks[1], (B, Skv, HIDDEN), jnp.float32), 'attention_bias': jax.random.normal(ks[2], (1, NUM_HEADS, Sq, Skv), jnp.float32), 'attention_mask': jnp.zeros((B, 1, 1, Skv), jnp.float32), 'Wq': jax.random.normal(ks[3], (HIDDEN, NUM_HEADS * HEAD_DIM), jnp.float32) * scale, 'Wk': jax.random.normal(ks[4], (HIDDEN, NUM_HEADS * HEAD_DIM), jnp.float32) * scale, 'Wv': jax.random.normal(ks[5], (HIDDEN, NUM_HEADS * HEAD_DIM), jnp.float32) * scale, 'Wo': jax.random.normal(ks[6], (NUM_HEADS * HEAD_DIM, HIDDEN), jnp.float32) * scale}
        return inp
    _L1_xattn_all = _L1_xattn_setup()
    _L1_xattn_in = {k: v for k, v in _L1_xattn_all.items() if k in ('Wq', 'Wk', 'Wv', 'Wo')}
    del _L1_xattn_all

    def _L1_ffn_setup():
        import jax, jax.numpy as jnp
        import numpy as np
        import math
        GOLDEN_CENTER = 1.0 / math.e
        GOLDEN_LOWER = 0.5 - math.log(4.0 / 3.0)
        GOLDEN_UPPER = 0.5
        B, T, D = (4, 512, 256)
        E = 8
        I = 1024 // (E // 2)

        def _routing_weights(x, Wr, temperature):
            inh = jax.nn.sigmoid(x @ Wr / temperature)
            in_zone = (inh >= GOLDEN_LOWER) & (inh <= GOLDEN_UPPER)
            dist = jnp.abs(inh - GOLDEN_CENTER)
            w = jnp.exp(-dist / 0.1) * in_zone.astype(x.dtype)
            wsum = w.sum(axis=-1, keepdims=True)
            no_expert = wsum < 1e-08
            fb = jnp.exp(-dist / 0.3)
            _, top2 = jax.lax.top_k(fb, 2)
            fb_mask = jax.nn.one_hot(top2, E, dtype=x.dtype).sum(axis=-2)
            fb_w = fb * fb_mask
            fb_w = fb_w / jnp.clip(fb_w.sum(axis=-1, keepdims=True), 1e-08)
            w = jnp.where(no_expert, fb_w, w)
            wsum = w.sum(axis=-1, keepdims=True)
            return w / jnp.clip(wsum, 1e-08)
        key = jax.random.key(seed)
        k = jax.random.split(key, 6)
        s_d = 1.0 / math.sqrt(D)
        s_i = 1.0 / math.sqrt(I)
        return {'x': jax.random.normal(k[0], (B, T, D), jnp.float32), 'Wg': jax.random.normal(k[1], (E, D, I), jnp.float32) * s_d, 'Wu': jax.random.normal(k[2], (E, D, I), jnp.float32) * s_d, 'Wd': jax.random.normal(k[3], (E, I, D), jnp.float32) * s_i, 'Wr': jax.random.normal(k[4], (D, E), jnp.float32) * s_d, 'temperature': jnp.ones((1,), jnp.float32)}
    _L1_ffn_all = _L1_ffn_setup()
    _L1_ffn_in = {k: v for k, v in _L1_ffn_all.items() if k in ('Wg', 'Wu', 'Wd', 'Wr', 'temperature')}
    del _L1_ffn_all
    return {'x': x, 'ctx_1024': ctx_1024, 'fside_1x16xSxS2_0': fside_1x16xSxS2_0, 'mask_Bx1x1xS2_ff0': mask_Bx1x1xS2_ff0, 'L0_attn_Wq': _L0_attn_in['Wq'], 'L0_attn_Wk': _L0_attn_in['Wk'], 'L0_attn_Wv': _L0_attn_in['Wv'], 'L0_attn_Wff': _L0_attn_in['Wff'], 'L0_attn_bff': _L0_attn_in['bff'], 'L0_xattn_Wq': _L0_xattn_in['Wq'], 'L0_xattn_Wk': _L0_xattn_in['Wk'], 'L0_xattn_Wv': _L0_xattn_in['Wv'], 'L0_xattn_Wo': _L0_xattn_in['Wo'], 'L0_xattn_bo': _L0_xattn_in['bo'], 'L0_ffn_ln_g': _L0_ffn_in['ln_g'], 'L0_ffn_ln_b': _L0_ffn_in['ln_b'], 'L0_ffn_attn_w': _L0_ffn_in['attn_w'], 'L0_ffn_attn_b': _L0_ffn_in['attn_b'], 'L0_ffn_gate_w': _L0_ffn_in['gate_w'], 'L0_ffn_w1': _L0_ffn_in['w1'], 'L0_ffn_b1': _L0_ffn_in['b1'], 'L0_ffn_w2': _L0_ffn_in['w2'], 'L0_ffn_b2': _L0_ffn_in['b2'], 'L0_ffn_next_w': _L0_ffn_in['next_w'], 'L0_ffn_next_b': _L0_ffn_in['next_b'], 'L1_attn_adj_rows': _L1_attn_in['adj_rows'], 'L1_attn_adj_cols': _L1_attn_in['adj_cols'], 'L1_attn_adj_vals': _L1_attn_in['adj_vals'], 'L1_attn_wq': _L1_attn_in['wq'], 'L1_attn_wk': _L1_attn_in['wk'], 'L1_attn_wv_w': _L1_attn_in['wv_w'], 'L1_attn_wv_b': _L1_attn_in['wv_b'], 'L1_attn_qkv_w': _L1_attn_in['qkv_w'], 'L1_attn_out_w': _L1_attn_in['out_w'], 'L1_attn_out_b': _L1_attn_in['out_b'], 'L1_attn_conv_w': _L1_attn_in['conv_w'], 'L1_xattn_Wq': _L1_xattn_in['Wq'], 'L1_xattn_Wk': _L1_xattn_in['Wk'], 'L1_xattn_Wv': _L1_xattn_in['Wv'], 'L1_xattn_Wo': _L1_xattn_in['Wo'], 'L1_ffn_Wg': _L1_ffn_in['Wg'], 'L1_ffn_Wu': _L1_ffn_in['Wu'], 'L1_ffn_Wd': _L1_ffn_in['Wd'], 'L1_ffn_Wr': _L1_ffn_in['Wr'], 'L1_ffn_temperature': _L1_ffn_in['temperature']}

def reference(x, ctx_1024, fside_1x16xSxS2_0, mask_Bx1x1xS2_ff0, L0_attn_Wq, L0_attn_Wk, L0_attn_Wv, L0_attn_Wff, L0_attn_bff, L0_xattn_Wq, L0_xattn_Wk, L0_xattn_Wv, L0_xattn_Wo, L0_xattn_bo, L0_ffn_ln_g, L0_ffn_ln_b, L0_ffn_attn_w, L0_ffn_attn_b, L0_ffn_gate_w, L0_ffn_w1, L0_ffn_b1, L0_ffn_w2, L0_ffn_b2, L0_ffn_next_w, L0_ffn_next_b, L1_attn_adj_rows, L1_attn_adj_cols, L1_attn_adj_vals, L1_attn_wq, L1_attn_wk, L1_attn_wv_w, L1_attn_wv_b, L1_attn_qkv_w, L1_attn_out_w, L1_attn_out_b, L1_attn_conv_w, L1_xattn_Wq, L1_xattn_Wk, L1_xattn_Wv, L1_xattn_Wo, L1_ffn_Wg, L1_ffn_Wu, L1_ffn_Wd, L1_ffn_Wr, L1_ffn_temperature):
    import jax
    import jax.numpy as jnp

    def _L0_attn_ref(x, Wq, Wk, Wv, Wff, bff):
        import jax, jax.numpy as jnp
        import numpy as np
        NUM_HEADS = 16
        B, S, D = x.shape
        H = NUM_HEADS
        Dh = D // H
        q = x @ Wq.T * (1.0 / jnp.sqrt(jnp.asarray(D, x.dtype)))
        k = x @ Wk.T
        v = x @ Wv.T
        q = q.reshape(B, S, H, Dh)
        k = k.reshape(B, S, H, Dh)
        v = v.reshape(B, S, H, Dh)
        scores = jnp.einsum('bqhd,bkhd->bhqk', q, k)
        attn = jax.nn.softmax(scores, axis=-1)
        out = jnp.einsum('bhqk,bkhd->bqhd', attn, v).reshape(B, S, D)
        return out @ Wff.T + bff

    def _L0_xattn_ref(x1, x2, Wq, Wk, Wv, Wo, bo):
        import jax, jax.numpy as jnp
        import numpy as np
        DIM = 256
        HEADS = 16
        DIM_HEAD = 64
        INNER = HEADS * DIM_HEAD
        SCALE = DIM_HEAD ** (-0.5)
        B, N = (4, 512)

        def _split_heads(t):
            b, n, _ = t.shape
            return t.reshape(b, n, HEADS, DIM_HEAD).transpose(0, 2, 1, 3)

        def _attn_block(q_src, k_src, v_src, Wq, Wk, Wv, Wo, bo):
            q = _split_heads(q_src @ Wq)
            k = _split_heads(k_src @ Wk)
            v = _split_heads(v_src @ Wv)
            dots = jnp.einsum('bhid,bhjd->bhij', q, k) * SCALE
            attn = jax.nn.softmax(dots, axis=-1)
            out = jnp.einsum('bhij,bhjd->bhid', attn, v)
            out = out.transpose(0, 2, 1, 3).reshape(q_src.shape[0], q_src.shape[1], INNER)
            return out @ Wo + bo
        out = x1 + _attn_block(x1, x2, x2, Wq, Wk, Wv, Wo, bo)
        return _attn_block(out, out, x1, Wq, Wk, Wv, Wo, bo)

    def _L0_ffn_ref(x, ln_g, ln_b, attn_w, attn_b, gate_w, w1, b1, w2, b2, next_w, next_b):
        import jax, jax.numpy as jnp
        import numpy as np
        MICRO_BATCHES = 2
        TOP_K = 2
        LN_EPS = 1e-05
        B, S, D = (4, 1024, 256)
        E = 8
        DFF = 4 * D

        def _layernorm(x, g, b):
            mu = jnp.mean(x, axis=-1, keepdims=True)
            var = jnp.mean(jnp.square(x - mu), axis=-1, keepdims=True)
            return (x - mu) * jax.lax.rsqrt(var + LN_EPS) * g + b
        Bx, Sx, Dx = x.shape
        N = Bx * Sx
        x_flat = x.reshape(N, Dx)
        x_attn = _layernorm(x_flat, ln_g, ln_b) @ attn_w + attn_b + x_flat
        logits = x_attn @ gate_w
        _ = jax.lax.top_k(logits, TOP_K)
        tpe = N // (MICRO_BATCHES * E)
        g = x_attn.reshape(MICRO_BATCHES, E, tpe, Dx)
        h = jax.nn.gelu(jnp.einsum('metd,edf->metf', g, w1) + b1[None, :, None, :], approximate=False)
        y = jnp.einsum('metf,efd->metd', h, w2) + b2[None, :, None, :]
        out = jax.nn.gelu(y @ next_w + next_b, approximate=False)
        return out.reshape(Bx, Sx, Dx)

    def _L1_attn_ref(dense, adj_rows, adj_cols, adj_vals, wq, wk, wv_w, wv_b, qkv_w, out_w, out_b, conv_w):
        import jax, jax.numpy as jnp
        import numpy as np
        HEADS, DIM_HEAD, LANDMARKS, PINV_ITERS = (8, 64, 64, 6)
        WQK_DIM = 64
        CONV_K = 33

        def moore_penrose_pinv(x, iters):
            I = jnp.eye(x.shape[-1], dtype=x.dtype)
            abs_x = jnp.abs(x)
            scale = jnp.max(abs_x.sum(-1)) * jnp.max(abs_x.sum(-2))
            z = jnp.swapaxes(x, -1, -2) / scale
            for _ in range(iters):
                xz = x @ z
                z = 0.25 * z @ (13 * I - xz @ (15 * I - xz @ (7 * I - xz)))
            return z

        def nystrom_attention(x, qkv_w, out_w, out_b, conv_w):
            b, n, d = x.shape
            h, dh, m = (HEADS, DIM_HEAD, LANDMARKS)
            scale = dh ** (-0.5)
            qkv = x @ qkv_w
            q, k, v = jnp.split(qkv, 3, axis=-1)
            split = lambda t: t.reshape(b, n, h, dh).transpose(0, 2, 1, 3)
            q, k, v = (split(q) * scale, split(k), split(v))
            l = n // m
            q_l = q.reshape(b, h, m, l, dh).mean(axis=3)
            k_l = k.reshape(b, h, m, l, dh).mean(axis=3)
            attn1 = jax.nn.softmax(jnp.einsum('bhid,bhjd->bhij', q, k_l), axis=-1)
            attn2 = jax.nn.softmax(jnp.einsum('bhid,bhjd->bhij', q_l, k_l), axis=-1)
            attn3 = jax.nn.softmax(jnp.einsum('bhid,bhjd->bhij', q_l, k), axis=-1)
            attn2_inv = moore_penrose_pinv(attn2, PINV_ITERS)
            out = attn1 @ (attn2_inv @ (attn3 @ v))
            pad = CONV_K // 2
            res = jax.lax.conv_general_dilated(v, conv_w, window_strides=(1, 1), padding=((pad, pad), (0, 0)), dimension_numbers=('NCHW', 'OIHW', 'NCHW'), feature_group_count=h)
            out = out + res
            out = out.transpose(0, 2, 1, 3).reshape(b, n, h * dh)
            return out @ out_w + out_b

        def _reference_tuple_inner(dense, adj_rows, adj_cols, adj_vals, wq, wk, wv_w, wv_b, qkv_w, out_w, out_b, conv_w):
            b, n, d = dense.shape
            xg = nystrom_attention(dense, qkv_w, out_w, out_b, conv_w)
            enc = xg[0] + dense
            q = enc @ wq
            k = enc @ wk
            scores = jnp.einsum('bid,bjd->bij', q, k) / jnp.sqrt(jnp.float32(WQK_DIM))
            data = scores[0]
            contrib = adj_vals * data[adj_rows, adj_cols]
            A_raw = jax.ops.segment_sum(contrib, adj_rows, num_segments=n)
            alpha = jax.nn.softmax(A_raw)
            value = dense @ wv_w + wv_b
            xl = alpha[:, None] * value
            wei = jax.nn.sigmoid(-xl)
            sw = wei * wei
            xo = xl * 2 * sw + 2 * enc * (1 - sw)
            return (xo, A_raw)
        return _reference_tuple_inner(dense, adj_rows, adj_cols, adj_vals, wq, wk, wv_w, wv_b, qkv_w, out_w, out_b, conv_w)[0]

    def _L1_xattn_ref(q_hidden_states, kv_hidden_states, attention_bias, attention_mask, Wq, Wk, Wv, Wo):
        import jax, jax.numpy as jnp
        import numpy as np
        HIDDEN = 256
        NUM_HEADS = 16
        HEAD_DIM = 64
        B, Sq, D = q_hidden_states.shape
        Skv = kv_hidden_states.shape[1]
        H, Dh = (NUM_HEADS, HEAD_DIM)
        q = (q_hidden_states @ Wq).reshape(B, Sq, H, Dh)
        k = (kv_hidden_states @ Wk).reshape(B, Skv, H, Dh)
        v = (kv_hidden_states @ Wv).reshape(B, Skv, H, Dh)
        bias = attention_bias + attention_mask
        scores = jnp.einsum('bqhd,bkhd->bhqk', q, k) + bias
        probs = jax.nn.softmax(scores, axis=-1)
        attn = jnp.einsum('bhqk,bkhd->bqhd', probs, v)
        attn = attn.reshape(B, Sq, H * Dh)
        return attn @ Wo

    def _L1_ffn_ref(x, Wg, Wu, Wd, Wr, temperature):
        import jax, jax.numpy as jnp
        import numpy as np
        import math
        GOLDEN_CENTER = 1.0 / math.e
        GOLDEN_LOWER = 0.5 - math.log(4.0 / 3.0)
        GOLDEN_UPPER = 0.5
        B, T, D = (4, 512, 256)
        E = 8
        I = 1024 // (E // 2)

        def _routing_weights(x, Wr, temperature):
            inh = jax.nn.sigmoid(x @ Wr / temperature)
            in_zone = (inh >= GOLDEN_LOWER) & (inh <= GOLDEN_UPPER)
            dist = jnp.abs(inh - GOLDEN_CENTER)
            w = jnp.exp(-dist / 0.1) * in_zone.astype(x.dtype)
            wsum = w.sum(axis=-1, keepdims=True)
            no_expert = wsum < 1e-08
            fb = jnp.exp(-dist / 0.3)
            _, top2 = jax.lax.top_k(fb, 2)
            fb_mask = jax.nn.one_hot(top2, E, dtype=x.dtype).sum(axis=-2)
            fb_w = fb * fb_mask
            fb_w = fb_w / jnp.clip(fb_w.sum(axis=-1, keepdims=True), 1e-08)
            w = jnp.where(no_expert, fb_w, w)
            wsum = w.sum(axis=-1, keepdims=True)
            return w / jnp.clip(wsum, 1e-08)
        weights = _routing_weights(x, Wr, temperature)
        gate = jnp.einsum('btd,edi->beti', x, Wg)
        up = jnp.einsum('btd,edi->beti', x, Wu)
        h = jax.nn.silu(gate) * up
        e_out = jnp.einsum('beti,eid->betd', h, Wd)
        out = jnp.einsum('bte,betd->btd', weights, e_out)
        return out
    x = _layernorm(x + _L0_attn_ref(x, L0_attn_Wq, L0_attn_Wk, L0_attn_Wv, L0_attn_Wff, L0_attn_bff), axis=-1)
    x = _layernorm(x + _L0_xattn_ref(x, ctx_1024, L0_xattn_Wq, L0_xattn_Wk, L0_xattn_Wv, L0_xattn_Wo, L0_xattn_bo), axis=-1)
    x = _layernorm(x + _L0_ffn_ref(x, L0_ffn_ln_g, L0_ffn_ln_b, L0_ffn_attn_w, L0_ffn_attn_b, L0_ffn_gate_w, L0_ffn_w1, L0_ffn_b1, L0_ffn_w2, L0_ffn_b2, L0_ffn_next_w, L0_ffn_next_b), axis=-1)
    x = _layernorm(x + _L1_attn_ref(x, L1_attn_adj_rows, L1_attn_adj_cols, L1_attn_adj_vals, L1_attn_wq, L1_attn_wk, L1_attn_wv_w, L1_attn_wv_b, L1_attn_qkv_w, L1_attn_out_w, L1_attn_out_b, L1_attn_conv_w), axis=-1)
    x = _layernorm(x + _L1_xattn_ref(x, ctx_1024, fside_1x16xSxS2_0, mask_Bx1x1xS2_ff0, L1_xattn_Wq, L1_xattn_Wk, L1_xattn_Wv, L1_xattn_Wo), axis=-1)
    x = _layernorm(x + _L1_ffn_ref(x, L1_ffn_Wg, L1_ffn_Wu, L1_ffn_Wd, L1_ffn_Wr, L1_ffn_temperature), axis=-1)
    return x

_drawn_inputs = setup_inputs


def setup_inputs(seed=0):
    import zlib

    import numpy as np

    out = dict(_drawn_inputs(seed))
    spreads = {'L0_xattn_bo': (0.0, 0.1),
     'L0_ffn_ln_g': (1.0, 0.2),
     'L0_ffn_ln_b': (0.0, 0.1),
     'L0_ffn_attn_b': (0.0, 0.1),
     'L0_ffn_b1': (0.0, 0.1),
     'L0_ffn_b2': (0.0, 0.1),
     'L0_ffn_next_b': (0.0, 0.1),
     'L1_attn_wv_b': (0.0, 0.8),
     'L1_attn_out_b': (0.0, 0.1)}
    factors = {'L1_attn_adj_vals': 8.0, 'L1_attn_wq': 2.816, 'L1_attn_wk': 3.01, 'L1_attn_wv_w': 3.709}
    for name, (base, spread) in spreads.items():
        noise = np.random.default_rng([zlib.crc32(name.encode()), seed]).standard_normal(out[name].shape)
        drawn = base * np.exp(spread * noise) if base else spread * noise
        out[name] = jnp.asarray(drawn.astype(out[name].dtype))
    for name, factor in factors.items():
        out[name] = (out[name] * factor).astype(out[name].dtype)
    return out
```

```python
from contextlib import ExitStack

import numpy as np

import concourse.bass as bass
from concourse import mybir

F32 = mybir.dt.float32
F32R = mybir.dt.float32r
BF16 = mybir.dt.bfloat16
I32 = mybir.dt.int32
ALU = mybir.AluOpType
ACT = mybir.ActivationFunctionType
AX = mybir.AxisListType.X


class Queue:

    def __init__(self, sem, serial=False):
        self.sem, self.n, self.ops, self.passed, self.serial = sem, 0, [], {}, serial

    def wait(self, *tokens):
        for t in tokens:
            if isinstance(t, list):
                self.wait(*t)
            elif t is not None and self.passed.get(t[2], 0) < t[1]:
                self.passed[t[2]] = t[1]
                self.ops.append((lambda e, t=t: e.wait_ge(t[0], t[1]), None))

    def raw(self, fn):
        self.ops.append((fn, None))

    def do(self, fn, *tokens):
        self.wait(*tokens)
        if self.serial:
            self.wait(self.here())
        self.n += 1
        self.ops.append((fn, (self.sem, 1)))
        return (self.sem, self.n, id(self))

    def here(self):
        return (self.sem, self.n, id(self)) if self.n else None

    def run(self, e):
        for fn, inc in self.ops:
            ins = fn(e)
            if inc:
                ins.then_inc(*inc)


class Program:
    def __init__(self, nc, ctx):
        self.nc, self.ctx = nc, ctx
        self.PE, self.V, self.S, self.G, self.Y = [Queue(ctx.enter_context(nc.semaphore(n)), n == "pool") for n in
                                                   ("pe", "dve", "act", "pool", "sp")]
        self.dsem = [ctx.enter_context(nc.semaphore(f"dma{i}")) for i in range(96)]
        self.dcount = [0] * 96
        self.dnext = 0
        self.gsem = [ctx.enter_context(nc.semaphore(f"gather{i}")) for i in range(16)]
        self.gcount = [0] * 16
        self.gnext = 0

    def dma(self, q, out, in_, *tokens):
        if out.dtype == F32R:
            out = out.bitcast(F32)
        if in_.dtype == F32R:
            in_ = in_.bitcast(F32)
        i = self.dnext % 96
        self.dnext += 1
        sem, key = self.dsem[i], f"dma{i}"
        if self.dcount[i]:
            q.wait((sem, self.dcount[i], key))
        q.wait(*tokens)
        self.dcount[i] += 16
        q.ops.append((lambda e: e.dma_start(out, in_), (sem, 16)))
        return (sem, self.dcount[i], key)

    def gather(self, out, in_, idx, *tokens):
        i = self.gnext % 16
        self.gnext += 1
        sem, key = self.gsem[i], f"gather{i}"
        if self.gcount[i]:
            self.G.wait((sem, self.gcount[i], key))
        self.G.wait(*tokens)
        self.gcount[i] += 16
        self.G.ops.append((lambda e: e.indirect_dma_start(out, None, in_, bass.IndirectOffsetOnAxis(ap=idx, axis=0)), (sem, 16)))
        return (sem, self.gcount[i], key)

    def everything(self):
        t = [q.here() for q in (self.PE, self.V, self.S, self.G)]
        return t + [(self.dsem[i], self.dcount[i], f"dma{i}") for i in range(96) if self.dcount[i]] + [
            (self.gsem[i], self.gcount[i], f"gather{i}") for i in range(16) if self.gcount[i]]

    def barrier(self):
        t = self.everything()
        for q in (self.PE, self.V, self.S, self.G, self.Y):
            q.wait(t)


def build(nc, A, out):
    with ExitStack() as ctx:
        P = Program(nc, ctx)
        PE, V, S, G, Y = P.PE, P.V, P.S, P.G, P.Y

        def sb(c, name, shape, dt=F32):
            return c.enter_context(nc.sbuf_tensor(name, shape, dt))

        PS = ctx.enter_context(nc.psum_tensor("PS", [128, 4096], F32))

        def bank(i, n=1):
            return PS[:, 512 * i:512 * (i + n)]

        free = [None] * 8

        def mm(o, l, r, st, sp, q=PE.raw):
            return q(lambda e: e.matmul(o, l, r, start=st, stop=sp, skip_group_check=True))

        def copy(q, o, i, *t):
            return q.do(lambda e: e.copy(o, i) if q is S else e.tensor_copy(o, i), *t)

        def act(o, i, f, *t, **kw):
            return S.do(lambda e: e.activation(o, i, f, **kw), *t)

        def two(q, o, a, b, op, *t):
            return q.do(lambda e: e.tensor_tensor(o, a, b, op), *t)

        def ts(q, o, a, s1, s2, op0, op1, *t):
            if op1 is None:
                return q.do(lambda e: e.tensor_scalar(o, a, s1, None, op0), *t)
            return q.do(lambda e: e.tensor_scalar(o, a, s1, s2, op0, op1), *t)

        def sst(q, o, a, s, b, op0, op1, *t):
            return q.do(lambda e: e.scalar_tensor_tensor(out=o, in0=a, scalar=s, in1=b, op0=op0, op1=op1), *t)

        def red(o, i, op, *t):
            return V.do(lambda e: e.tensor_reduce(o, i, AX, op), *t)

        def rmax(o, i, *t):
            return V.do(lambda e: e.reduce_max(o, i, AX, negate=True), *t)

        def rec(o, i, *t):
            return V.do(lambda e: e.reciprocal(o, i), *t)

        def fill(q, o, v, *t):
            return q.do(lambda e: e.memset(o, v), *t)

        X = sb(ctx, "X", [128, 16, 256])
        XT = sb(ctx, "XT", [128, 2, 2048])
        ident = sb(ctx, "ident", [128, 128])
        epsc = sb(ctx, "epsc", [128, 1])
        onesf = sb(ctx, "onesf", [128, 128])
        ZB = sb(ctx, "ZB", [128, 256])
        stt = sb(ctx, "stt", [128, 4, 16])

        t = G.do(lambda e: e.memset(ident[:, :], 0.0))
        t_id = G.do(lambda e: e.affine_select(out=ident[:, :], in_=ident[:, :], compare_op=ALU.not_equal, fill=1.0,
                                              base=0, pattern=[[-1, 128]], channel_multiplier=1), t)
        t_eps = fill(G, epsc[:, :], 1e-5)
        S.wait(t_eps)
        t_ones = G.do(lambda e: e.memset(onesf[:, :], 1.0))
        t_x = [P.dma(Y, X[:, 4 * i:4 * i + 4, :], A["x"].rearrange("b (t p) d -> p (b t) d", p=128)[:, 4 * i:4 * i + 4, :])
               for i in range(4)]

        def transpose(o, i, k=128):
            return PE.do(lambda e: e.transpose(o, i, ident[0:k, 0:k]))

        def to_xt(src, dst, tt, b, tok, scale=None, bias=None, slot=None, after=None):
            PE.wait(t_id, free[b], tok)
            k = tt if slot is None else slot
            transpose(bank(b)[:, 0:128], src[:, k, 0:128])
            t = transpose(bank(b)[:, 128:256], src[:, k, 128:256])
            S.wait(after)
            if scale is None:
                t = copy(S, dst[:, :, tt * 128:tt * 128 + 128], bank(b)[:, 0:256].rearrange("p (c n) -> p c n", c=2), t)
            else:
                for c in range(2):
                    t = act(dst[:, c, tt * 128:tt * 128 + 128], bank(b)[:, 128 * c:128 * c + 128], ACT.Identity, t,
                            bias=bias[:, c:c + 1], scale=scale[:, c:c + 1])
            free[b] = t
            return t

        LS = sb(ctx, "LS", [128, 4, 256])
        lsn = [0]

        def norm(tt, src, dst, tok, eps=1e-5):
            k = lsn[0] % 4
            lsn[0] += 1
            st = stt[:, k, :]
            t = V.do(lambda e: e.bn_stats(st[:, 0:6], src), tok)
            t = V.do(lambda e: e.bn_aggr(st[:, 6:8], st[:, 0:6]), t)
            t = act(st[:, 9:10], st[:, 7:8], ACT.Sqrt, t, bias=epsc[:, 0:1])
            t = rec(st[:, 8:9], st[:, 9:10], t)
            return V.do(lambda e: e.tensor_scalar(dst, src, st[:, 6:7], st[:, 8:9], ALU.subtract, ALU.mult), t)

        def add_norm(tt, ps, biasB, tok, fr=None):
            k = lsn[0] % 4
            tmp = LS[:, k, :]
            t = two(V, tmp, ps, X[:, tt, :], ALU.add, tok)
            if fr is not None:
                free[fr] = t
            if biasB is not None:
                t = two(V, tmp, tmp, biasB, ALU.add, t)
            return norm(tt, tmp, X[:, tt, :], t)

        t_xt = [to_xt(X, XT, i, 2 + i % 4, t_x[i // 4]) for i in range(16)]

        with ExitStack() as c:
            QS = [sb(c, f"a_QS{i}", [128, 4, 1024], F32R) for i in range(2)]
            KS = [sb(c, f"a_KS{i}", [128, 4, 1024], F32R) for i in range(2)]
            QH = sb(c, "a_QH", [128, 2, 1024], F32R)
            QL = sb(c, "a_QL", [128, 2, 1024], F32R)
            KH = sb(c, "a_KH", [128, 2, 1024], F32R)
            KL = sb(c, "a_KL", [128, 2, 1024], F32R)
            VA = sb(c, "a_VA", [128, 8, 16, 32])
            PB = [sb(c, f"a_P{i}", [128, 1024]) for i in range(4)]
            OT = sb(c, "a_OT", [128, 4, 1024])
            WQ = sb(c, "a_WQ", [128, 2, 256])
            WK = sb(c, "a_WK", [128, 2, 256])
            WV = sb(c, "a_WV", [128, 2, 256])
            WF = sb(c, "a_WF", [128, 4, 256])
            sel = sb(c, "a_sel", [128, 128])
            MX = sb(c, "a_MX", [128, 2, 16])
            MT = sb(c, "a_MT", [16, 2, 128], F32R)
            OU = sb(c, "a_OU", [128, 512])
            RC = sb(c, "a_RC", [128, 512])
            mdram = nc.dram_tensor("a_m", [2, 16, 128], F32R, kind="Internal").ap()

            t_w = {n: P.dma(Y, W[:, :, :], A[n].rearrange("(c p) n -> p c n", p=128))
                   for n, W in (("L0_attn_WqT", WQ), ("L0_attn_WkT", WK), ("L0_attn_WvT", WV))}
            t = V.do(lambda e: e.memset(WF[:, :, :], 0.0))
            t_wf = [P.dma(Y, WF[32 * j:32 * j + 16, :, :],
                          A["L0_attn_WffT"].rearrange("(g j d) n -> j d g n", j=4, d=16)[j], t) for j in range(4)]
            t_bf = P.dma(Y, ZB[:, :], A["L0_attn_bff"].rearrange("(o d) -> o d", o=1).broadcast_to([128, 256]))
            t = G.do(lambda e: e.memset(sel[:, :], 0.0))
            t_sel = G.do(lambda e: e.affine_select(out=sel[:, :].rearrange("p (a b) -> p a b", a=4),
                                                   in_=sel[:, :].rearrange("p (a b) -> p a b", a=4),
                                                   compare_op=ALU.not_equal, fill=1.0, base=-16,
                                                   pattern=[[-32, 4], [0, 32]], channel_multiplier=1), t)
            t_va1 = G.do(lambda e: e.memset(VA[:, :, :, :], 1.0))
            t_ks = []
            for i in range(2):
                G.do(lambda e, i=i: e.memset(KS[i][:, :, :].bitcast(F32), 0.0))
                t = G.do(lambda e, i=i: e.memset(QS[i][:, :, :].bitcast(F32), 0.0))
                t_ks.append(G.do(lambda e, i=i: e.memset(KS[i][64:65, :, :].bitcast(F32), 1.0), t))

            stack_free = [None, None]
            ot_free = None
            prep_free = None
            for b in range(2):
                nb = 0
                lastp = {}
                for half in range(2):
                    tok = slice(half * 512, half * 512 + 512)
                    src = slice(b * 1024 + half * 512, b * 1024 + half * 512 + 512)
                    for g in range(2):
                        for W, wn, H, L in ((WQ, "L0_attn_WqT", QH, QL), (WK, "L0_attn_WkT", KH, KL)):
                            bk = 2 + nb % 4
                            nb += 1
                            PE.wait(t_w[wn], free[bk], t_xt)
                            mm(bank(bk), W[:, 0, g * 128:g * 128 + 128], XT[:, 0, src], True, False)
                            t = mm(bank(bk), W[:, 1, g * 128:g * 128 + 128], XT[:, 1, src], False, True, PE.do)
                            t = copy(S, H[:, g, tok], bank(bk), t, prep_free)
                            t = two(V, L[:, g, tok], bank(bk), H[:, g, tok].bitcast(F32), ALU.subtract, t, prep_free)
                            free[bk] = t
                            lastp[(wn, g)] = t
                t_va = []
                for kt in range(8):
                    bk = 2 + nb % 4
                    nb += 1
                    src = slice(b * 1024 + kt * 128, b * 1024 + kt * 128 + 128)
                    PE.wait(t_w["L0_attn_WvT"], free[bk])
                    mm(bank(bk)[:, 0:256], XT[:, 0, src], WV[:, 0, :], True, False)
                    t = mm(bank(bk)[:, 0:256], XT[:, 1, src], WV[:, 1, :], False, True, PE.do)
                    t = copy(V, VA[:, kt, :, 0:16], bank(bk)[:, 0:256].rearrange("p (h d) -> p h d", d=16), t, t_va1)
                    free[bk] = t
                    t_va.append(t)

                t_stack = {}

                def build_stack(g4):
                    i = (b * 4 + g4) % 2
                    g = g4 // 2
                    tk = [lastp[("L0_attn_WqT", g)], lastp[("L0_attn_WkT", g)], stack_free[i], t_ks[i]]
                    ts = []
                    for j in range(4):
                        p0 = ((g4 % 2) * 4 + j) * 16
                        for r, (q, k) in enumerate(((QH, KH), (QL, KH), (QH, KL), (QL, KL))):
                            ts.append(P.dma(Y, QS[i][16 * r:16 * r + 16, j, :], q[p0:p0 + 16, g, :], tk))
                            ts.append(P.dma(Y, KS[i][16 * r:16 * r + 16, j, :], k[p0:p0 + 16, g, :], tk))
                    t_stack[g4] = ts

                units = [(g4, qh) for g4 in range(4) for qh in range(2)]
                tm, t_m, t_ex, ost = {}, {}, {}, {}

                def s_tile(n):
                    u, i = divmod(n, 16)
                    g4, qh = units[u]
                    j, qt = divmod(i, 4)
                    s = (b * 4 + g4) % 2
                    if i == 0 and qh == 0 and g4 not in t_stack:
                        build_stack(g4)
                    PE.wait(t_stack[g4], free[0])
                    q = QS[s][0:64, j, qh * 512 + qt * 128:qh * 512 + qt * 128 + 128]
                    mm(bank(0), q, KS[s][0:64, j, 0:512], True, True)
                    t = mm(bank(1), q, KS[s][0:64, j, 512:1024], True, True, PE.do)
                    if i == 0 and u >= 2:
                        V.wait(tm[u - 2])
                    t = rmax(MX[:, u % 2, i:i + 1], bank(0, 2), t)
                    free[0] = t
                    if i == 15:
                        tm[u] = t

                def m_row(u):
                    g4, qh = units[u]
                    s = (b * 4 + g4) % 2
                    PE.wait(tm[u], free[7], t_id)
                    t = transpose(bank(7)[0:16, 0:128], MX[:, u % 2, :])
                    tm[u] = t
                    t = copy(V, MT[:, u % 2, :], bank(7)[0:16, 0:128], t, t_m.get(u - 2))
                    free[7] = t
                    t = P.dma(Y, mdram[u % 2], MT[:, u % 2, :], t, t_m.get(u - 2))
                    t_m[u] = P.dma(Y, QS[s][64:65, :, qh * 512:qh * 512 + 512],
                                   mdram[u % 2].rearrange("(o j) q -> o j q", j=4 * 4)
                                   .rearrange("o (j t) q -> o j (t q)", j=4), t)

                def st(n):
                    u, i = divmod(n, 16)
                    g4, qh = units[u]
                    kt, hp = divmod(i, 2)
                    s = (b * 4 + g4) % 2
                    bk = 2 + 2 * (n % 2)
                    PE.wait(t_m[u], free[bk])
                    for jj in range(2):
                        j = 2 * hp + jj
                        t = mm(bank(bk + jj), KS[s][:, j, kt * 128:kt * 128 + 128], QS[s][:, j, qh * 512:qh * 512 + 512],
                               True, True, PE.do)
                    t_ex[n] = act(PB[n % 4][:, :], bank(bk, 2), ACT.Exp, t, ost.get(("pv", n - 4)), scale=1.0 / 16)
                    free[bk] = t_ex[n]
                    if i == 15 and qh == 1:
                        stack_free[s] = t

                def pv(n):
                    u, i = divmod(n, 16)
                    g4, qh = units[u]
                    kt = i // 2
                    PE.wait(t_ex[n], t_ex[n + 1], t_va[kt])
                    if kt == 0:
                        PE.wait(free[6])
                    for j in range(4):
                        t = mm(bank(6)[32 * j:32 * j + 32, :], VA[:, kt, 4 * g4 + j, :],
                               PB[(n + j // 2) % 4][:, 512 * (j % 2):512 * (j % 2) + 512], kt == 0, kt == 7,
                               PE.do if j == 3 else PE.raw)
                    ost[("pv", n)] = ost[("pv", n + 1)] = t
                    if kt == 7:
                        t = copy(V, OU[:, :], bank(6), t, ost.get("sel"), ost.get("ot"))
                        free[6] = t
                        ost["ou"] = t

                def finish(u):
                    g4, qh = units[u]
                    PE.wait(ost["ou"], free[7], t_sel)
                    t = ost["sel"] = mm(bank(7), sel[:, :], OU[:, :], True, True, PE.do)
                    t = rec(RC[:, :], bank(7), t, ost.get("ot"))
                    free[7] = t
                    ost["ot"] = two(V, OT[:, g4, qh * 512:qh * 512 + 512], OU[:, :], RC[:, :], ALU.mult, t, ot_free)
                    ost["ou_done"] = ost["ot"]

                N = 16 * len(units)
                LEAD = 24
                build_stack(0)
                build_stack(1)
                done = 0
                for n in range(-LEAD, N + 4):
                    if n + LEAD < N:
                        s_tile(n + LEAD)
                    k = n + LEAD - 1
                    if k >= 0 and k % 16 == 15 and k < N:
                        m_row(k // 16)
                    if 0 <= n < N:
                        st(n)
                    if n >= 3 and n % 2 == 1 and n - 3 < N:
                        pv(n - 3)
                    if n >= 19 and (n - 19) % 16 == 1:
                        finish((n - 20) // 16)
                finish(N // 16 - 1)
                prep_free = [t for v in t_stack.values() for t in v]
                for i in range(8):
                    tt = b * 8 + i
                    bk = 2 + i % 4
                    PE.wait(ost["ot"], t_wf, free[bk])
                    for g4 in range(4):
                        t = mm(bank(bk)[:, 0:256], OT[:, g4, i * 128:i * 128 + 128], WF[:, g4, :], g4 == 0, g4 == 3,
                               PE.do if g4 == 3 else PE.raw)
                    ot_free = t
                    t = add_norm(tt, bank(bk)[:, 0:256], ZB[:, :], [t, t_bf], bk)
                    t_xt[tt] = to_xt(X, XT, tt, bk, t)
        P.barrier()

        CT = sb(ctx, "CT", [128, 2, 154])

        def wload(c, name, W, q, *tok):
            return P.dma(q, W, A[name].rearrange("(c p) n -> p c n", p=128), *tok)

        def ctx_attention(c, pre, t_in, scale, bias, wnames, emit, bias_done=None):
            WQ = sb(c, pre + "WQ", [128, 2, 1024])
            WK = sb(c, pre + "WK", [128, 2, 1024])
            WV = sb(c, pre + "WV", [128, 2, 1024])
            WO = sb(c, pre + "WO", [128, 8, 256])
            KT = sb(c, pre + "KT", [128, 8, 154])
            VC = sb(c, pre + "VC", [77, 2, 1024])
            QB = [sb(c, pre + f"QB{i}", [128, 8, 512]) for i in range(1)]
            SS = [sb(c, pre + f"SS{i}", [128, 16, 77]) for i in range(2)]
            PT = sb(c, pre + "PT", [77, 16, 512])
            OT = sb(c, pre + "OT", [128, 8, 512])
            st = sb(c, pre + "st", [128, 2, 3, 16])
            t_wk = wload(c, wnames[1], WK[:, :, :], Y)
            t_wq = wload(c, wnames[0], WQ[:, :, :], Y)
            t_wv = wload(c, wnames[2], WV[:, :, :], Y)
            t_wo = wload(c, wnames[3], WO[:, :, :], Y)
            t_kt, t_vc = [], []
            for p in range(8):
                bk = 5 + p % 3
                PE.wait(t_wk, t_ct, free[bk])
                mm(bank(bk)[:, 0:154], WK[:, 0, p * 128:p * 128 + 128], CT[:, 0, :], True, False)
                t = mm(bank(bk)[:, 0:154], WK[:, 1, p * 128:p * 128 + 128], CT[:, 1, :], False, True, PE.do)
                free[bk] = t = copy(V, KT[:, p, :], bank(bk)[:, 0:154], t)
                t_kt.append(t)
            for b in range(2):
                for h in range(2):
                    bk = 5 + (2 * b + h) % 3
                    PE.wait(t_wv, free[bk])
                    mm(bank(bk)[0:77, :], CT[:, 0, 77 * b:77 * b + 77], WV[:, 0, 512 * h:512 * h + 512], True, False)
                    t = mm(bank(bk)[0:77, :], CT[:, 1, 77 * b:77 * b + 77], WV[:, 1, 512 * h:512 * h + 512], False, True, PE.do)
                    free[bk] = t = copy(S, VC[:, b, 512 * h:512 * h + 512], bank(bk)[0:77, :], t)
                    t_vc.append(t)
            heads = [list(range(0, 12, 2)), list(range(1, 12, 2)), [12, 14, 13, 15]]

            def part(a, bk):
                if bk == 2:
                    return a[:, 12:16]
                if len(a.shape) == 3:
                    return a[:, 0:12].rearrange("p (g k) n -> p g k n", k=2)[:, :, bk, :]
                return a[:, 0:12].rearrange("p (g k) -> p g k", k=2)[:, :, bk]
            tok = {"s": {}, "p": {}, "pt": {}, "pv": None, "q": None, "wo": None}

            def project_q(tb):
                for p in range(8):
                    bk = 5 + p % 3
                    PE.wait(t_wq, free[bk], [t_in[4 * tb + i] for i in range(4)])
                    mm(bank(bk), WQ[:, 0, p * 128:p * 128 + 128], XT[:, 0, tb * 512:tb * 512 + 512], True, False)
                    t = mm(bank(bk), WQ[:, 1, p * 128:p * 128 + 128], XT[:, 1, tb * 512:tb * 512 + 512], False, True, PE.do)
                    free[bk] = t = copy(S if p % 2 else V, QB[0][:, p, :], bank(bk), t, tok["s"].get(4 * tb - 1))
                    tok[("q", p)] = t
                tok["q"] = [tok[("q", p)] for p in range(8)]

            def scores(i):
                b, tq = i // 8, i % 4
                ss, k = SS[i % 2][:, :, :], i % 2
                PE.wait(tok["q"], t_kt)
                ts_ = []
                for bk in range(3):
                    PE.wait(free[bk])
                    for n, h in enumerate(heads[bk]):
                        r = 64 * (h % 2)
                        if h == 13:
                            PE.wait(t)
                        at = 77 * n if bk < 2 else 77 * (h - 12)
                        t = mm(bank(bk)[:, at:at + 77], QB[0][r:r + 64, h // 2, tq * 128:tq * 128 + 128],
                               KT[r:r + 64, h // 2, 77 * b:77 * b + 77], True, True,
                               PE.do if h == heads[bk][-1] or h == 14 else PE.raw)
                    ts_.append(t)
                tok["s"][i] = t
                m, s_, r_ = st[:, k, 0, :], st[:, k, 1, :], st[:, k, 2, :]
                ps = [bank(bk)[:, 0:77 * len(heads[bk])].rearrange("p (h n) -> p h n", n=77) for bk in range(3)]
                if bias is not None:
                    BM, t_b = bias(i)
                    t_s = []
                    for bk in range(3):
                        free[bk] = t = two(V, part(ss, bk), ps[bk], part(BM, bk), ALU.add, ts_[bk], t_b, tok["pt"].get(i - 2))
                    bias_done[i] = t
                    t = red(m, ss[:, :, :], ALU.max, t)
                    t = two(V, ss[:, :, :], ss[:, :, :], m.unsqueeze(2).broadcast_to([128, 16, 77]), ALU.subtract, t)
                else:
                    for bk in range(3):
                        t = red(part(m, bk), ps[bk], ALU.max, ts_[bk], tok["p"].get(i - 2))
                    for bk in range(3):
                        free[bk] = t = two(V, part(ss, bk), ps[bk], part(m, bk).unsqueeze(2).broadcast_to([128, len(heads[bk]), 77]),
                                           ALU.subtract, t, tok["pt"].get(i - 2))
                t = act(ss[:, :, :], ss[:, :, :], ACT.Exp, t, scale=scale)
                t = red(s_, ss[:, :, :], ALU.add, t)
                t = rec(r_, s_, t)
                tok["p"][i] = two(V, ss[:, :, :], ss[:, :, :], r_.unsqueeze(2).broadcast_to([128, 16, 77]), ALU.mult, t)

            def turn(i):
                tq = i % 4
                PE.wait(tok["p"][i])
                for g in range(4):
                    bk = 3 + g % 2
                    PE.wait(free[bk])
                    for j in range(4):
                        t = transpose(bank(bk)[0:77, 128 * j:128 * j + 128], SS[i % 2][:, 4 * g + j, :])
                    t2 = copy(S if g % 2 else V, PT[:, 4 * g:4 * g + 4, tq * 128:tq * 128 + 128],
                              bank(bk)[0:77, :].rearrange("p (h n) -> p h n", h=4), t, tok["pv"])
                    free[bk] = t2
                    tok[("turned", g)] = t2
                tok["pt"][i] = t
                tok[("pt", i)] = [tok[("turned", g)] for g in range(4)]

            def values(tb):
                b = tb // 2
                PE.wait([tok[("pt", 4 * tb + i)] for i in range(4)], t_vc)
                outs = []
                for p in range(8):
                    bk = 5 + p % 3
                    PE.wait(free[bk])
                    for h in range(2):
                        t = mm(bank(bk)[64 * h:64 * h + 64, :], VC[:, b, 128 * p + 64 * h:128 * p + 64 * h + 64], PT[:, 2 * p + h, :],
                               True, True, PE.do if h else PE.raw)
                    free[bk] = copy(S if p % 2 else V, OT[:, p, :], bank(bk), t, tok["wo"])
                    outs.append(free[bk])
                tok["pv"] = t
                PE.wait(outs, t_wo)
                for i in range(4):
                    bk = 5 + (i + 2) % 3
                    PE.wait(free[bk])
                    for p in range(8):
                        t = mm(bank(bk)[:, 0:256], OT[:, p, 128 * i:128 * i + 128], WO[:, p, :], p == 0, p == 7,
                               PE.do if p == 7 else PE.raw)
                    tok["wo"] = t
                    emit(4 * tb + i, bank(bk)[:, 0:256], bk, t)

            for i in range(17):
                if i < 16:
                    if i % 4 == 0:
                        project_q(i // 4)
                    scores(i)
                if i:
                    turn(i - 1)
                    if i % 4 == 0:
                        values(i // 4 - 1)

        CX = sb(ctx, "CX", [77, 2, 256])
        t = P.dma(Y, CX[:, :, :], A["ctx_1024"].rearrange("b s d -> s b d"))
        for b in range(2):
            PE.wait(t, t_id, free[7])
            for k in range(2):
                t2 = PE.do(lambda e, b=b, k=k: e.transpose(bank(7)[:, k * 77:k * 77 + 77], CX[:, b, 128 * k:128 * k + 128],
                                                           ident[0:77, 0:77]))
            free[7] = t_ct = copy(V, CT[:, :, 77 * b:77 * b + 77], bank(7)[:, 0:154].rearrange("p (c n) -> p c n", c=2), t2)

        with ExitStack() as c:
            YY = sb(c, "b_YY", [128, 16, 256])
            t_bo = P.dma(Y, ZB[:, :], A["L0_xattn_bo"].rearrange("(o d) -> o d", o=1).broadcast_to([128, 256]))

            def emit_b(tt, ps, bk, tok):
                t = two(V, YY[:, tt, :], ps, X[:, tt, :], ALU.add, tok)
                free[bk] = t
                t = two(V, YY[:, tt, :], YY[:, tt, :], ZB[:, :], ALU.add, t, t_bo)
                t_xt[tt] = to_xt(YY, XT, tt, 3 + tt % 2, t)

            ctx_attention(c, "b_", list(t_xt), 0.125, None, ("L0_xattn_Wq", "L0_xattn_Wk", "L0_xattn_Wv", "L0_xattn_Wo"), emit_b)
        P.barrier()

        with ExitStack() as c:
            QA = [sb(c, f"c_QA{i}", [128, 2, 512], F32R) for i in range(3)]
            QM = [sb(c, f"c_QM{i}", [128, 2, 512], F32R) for i in range(3)]
            KA = [sb(c, f"c_KA{i}", [128, 2, 1024], F32R) for i in range(2)]
            KM = [sb(c, f"c_KM{i}", [128, 2, 1024], F32R) for i in range(2)]
            VV = sb(c, "c_VV", [128, 8, 1024])
            OT = sb(c, "c_OT", [128, 8, 1024])
            PB = [sb(c, f"c_P{i}", [128, 512]) for i in range(6)]
            WQ = sb(c, "c_WQ", [128, 2, 1024])
            WK = sb(c, "c_WK", [128, 2, 1024])
            WVO = sb(c, "c_WVO", [128, 2048])
            MX = sb(c, "c_MX", [128, 2, 8])
            MT = sb(c, "c_MT", [8, 2, 128], F32R)
            RC = sb(c, "c_RC", [128, 512])
            mdram = nc.dram_tensor("c_m", [2, 8, 128], F32R, kind="Internal").ap()
            WV = WVO[:, :].rearrange("p (c n) -> p c n", c=2)
            WO = WVO[:, :].rearrange("p (c n) -> p c n", c=8)
            t_wv = wload(c, "L0_xattn_Wv", WV, Y)
            t_wq = wload(c, "L0_xattn_Wq", WQ[:, :, :], Y)
            t_wk = wload(c, "L0_xattn_Wk", WK[:, :, :], Y)
            t_one = []
            for i in range(2):
                fill(G, KM[i][:, :, :].bitcast(F32), 0.0)
                t_one.append(fill(G, KM[i][64:65, :, :].bitcast(F32), 1.0))
            t_qz = [fill(G, QM[i][:, :, :].bitcast(F32), 0.0) for i in range(3)]
            kfree = [None, None]
            qfree = [None] * 3
            pfree = [None] * 6
            tok = {"ot": None, "wo": None}
            mxfree = [None, None]
            mtfree = [None, None]
            vfree = None
            for b in range(2):
                t_v = []
                for kt in range(8):
                    tt_ = 8 * b + kt
                    bk = 2 + kt % 2
                    xk = LS[:, kt % 4, :].rearrange("p (c n) -> p c n", c=2)
                    PE.wait(free[bk])
                    transpose(bank(bk)[:, 0:128], X[:, tt_, 0:128])
                    t = transpose(bank(bk)[:, 128:256], X[:, tt_, 128:256])
                    free[bk] = t = copy(S, xk, bank(bk)[:, 0:256].rearrange("p (c n) -> p c n", c=2), t,
                                        tok.get(("xv", kt % 4)))
                    for h in range(2):
                        bk = 4 + h
                        PE.wait(t, t_wv, free[bk])
                        mm(bank(bk), xk[:, 0, :], WV[:, 0, 512 * h:512 * h + 512], True, False)
                        t3 = mm(bank(bk), xk[:, 1, :], WV[:, 1, 512 * h:512 * h + 512], False, True, PE.do)
                        free[bk] = copy(V, VV[:, kt, 512 * h:512 * h + 512], bank(bk), t3, vfree)
                        t_v.append(free[bk])
                    tok[("xv", kt % 4)] = t3
                t_wo = P.dma(Y, WO, A["L0_xattn_Wo"].rearrange("(c p) n -> p c n", p=128), t3)
                t_k, t_q, t_qm, t_mx, t_m, t_ex = {}, {}, {}, {}, {}, {}

                def prep_k(p, half):
                    i = p % 2
                    cols = slice(half * 512, half * 512 + 512)
                    src = slice(b * 1024 + half * 512, b * 1024 + half * 512 + 512)
                    PE.wait(free[7], t_wk, t_xt)
                    mm(bank(7), WK[:, 0, p * 128:p * 128 + 128], XT[:, 0, src], True, False)
                    t = mm(bank(7), WK[:, 1, p * 128:p * 128 + 128], XT[:, 1, src], False, True, PE.do)
                    for h in range(2):
                        ps = bank(7)[64 * h:64 * h + 64, :]
                        copy(S, KA[i][0:64, h, cols], ps, t, kfree[i])
                        t1 = copy(S, KA[i][64:128, h, cols], ps, t)
                    ends = [t1]
                    for h in range(2):
                        ps = bank(7)[64 * h:64 * h + 64, :]
                        ends.append(two(V, KM[i][0:64, h, cols], ps, KA[i][0:64, h, cols].bitcast(F32), ALU.subtract, t1, kfree[i],
                                        t_one[i]))
                    free[7] = ends
                    t_k[(p, half)] = ends

                def prep_q(u):
                    p, qh = divmod(u, 2)
                    i = (b * 16 + u) % 3
                    src = slice(b * 1024 + qh * 512, b * 1024 + qh * 512 + 512)
                    PE.wait(free[7], t_wq, t_xt)
                    mm(bank(7), WQ[:, 0, p * 128:p * 128 + 128], XT[:, 0, src], True, False)
                    t = mm(bank(7), WQ[:, 1, p * 128:p * 128 + 128], XT[:, 1, src], False, True, PE.do)
                    ends, qm = [], []
                    for h in range(2):
                        t1 = copy(S, QA[i][0:64, h, :], bank(7)[64 * h:64 * h + 64, :], t, qfree[i])
                    for h in range(2):
                        ps = bank(7)[64 * h:64 * h + 64, :]
                        ends.append(two(V, QA[i][64:128, h, :], ps, QA[i][0:64, h, :].bitcast(F32), ALU.subtract, t1))
                        qm.append(copy(G, QM[i][0:64, h, :], QA[i][0:64, h, :].bitcast(F32), t1, qfree[i], t_qz[i]))
                    free[7] = ends
                    t_q[u] = ends
                    t_qm[u] = qm

                def s_tile(u, i):
                    p, qh = divmod(u, 2)
                    h, qt = divmod(i, 4)
                    q, k = QA[(b * 16 + u) % 3], KA[p % 2]
                    PE.wait(t_q[u], t_k[(p, 0)], t_k[(p, 1)], free[0])
                    mm(bank(0), q[:, h, qt * 128:qt * 128 + 128], k[:, h, 0:512], True, True)
                    t = mm(bank(1), q[:, h, qt * 128:qt * 128 + 128], k[:, h, 512:1024], True, True, PE.do)
                    if i == 0:
                        V.wait(mxfree[u % 2])
                    t = rmax(MX[:, u % 2, i:i + 1], bank(0, 2), t)
                    free[0] = t
                    if i == 7:
                        t_mx[u] = t

                def m_row(u):
                    PE.wait(t_mx[u], free[7])
                    t = transpose(bank(7)[0:8, 0:128], MX[:, u % 2, :])
                    mxfree[u % 2] = t
                    free[7] = t = copy(V, MT[:, u % 2, :], bank(7)[0:8, 0:128], t, mtfree[u % 2])
                    mtfree[u % 2] = t = P.dma(Y, mdram[u % 2], MT[:, u % 2, :], t, t_m.get(u - 2))
                    t_m[u] = P.dma(Y, QM[(b * 16 + u) % 3][64:65, :, :],
                                   mdram[u % 2].rearrange("(o j) q -> o j q", o=1).rearrange("o (j t) q -> o j (t q)", j=2), t,
                                   t_qm[u])

                def st(u, n):
                    p, qh = divmod(u, 2)
                    kt, h = divmod(n, 2)
                    g = 16 * u + n
                    q, qm = QA[(b * 16 + u) % 3], QM[(b * 16 + u) % 3]
                    bk = 2 + g % 3
                    PE.wait(t_m[u], t_qm[u], free[bk])
                    mm(bank(bk), KA[p % 2][:, h, kt * 128:kt * 128 + 128], q[:, h, :], True, False)
                    t = mm(bank(bk), KM[p % 2][:, h, kt * 128:kt * 128 + 128], qm[:, h, :], False, True, PE.do)
                    t_ex[g] = free[bk] = act(PB[g % 6][:, :], bank(bk), ACT.Exp, t, pfree[g % 6], scale=0.125)
                    if n == 15:
                        qfree[(b * 16 + u) % 3] = t
                        if qh == 1:
                            kfree[p % 2] = t

                def pv(u, kt):
                    p, qh = divmod(u, 2)
                    g = 16 * u + 2 * kt
                    PE.wait(t_ex[g], t_ex[g + 1], t_v)
                    if kt == 0:
                        PE.wait(free[6], free[5])
                    for h in range(2):
                        mm(bank(6)[64 * h:64 * h + 64, :], VV[:, kt, 128 * p + 64 * h:128 * p + 64 * h + 64], PB[(g + h) % 6][:, :],
                           kt == 0, kt == 7)
                    for h in range(2):
                        t = mm(bank(5)[64 * h:64 * h + 64, :], onesf[:, 0:64], PB[(g + h) % 6][:, :], kt == 0, kt == 7,
                               PE.do if h else PE.raw)
                    pfree[g % 6] = pfree[(g + 1) % 6] = t
                    if kt == 7:
                        free[5] = t = rec(RC[:, :], bank(5), t, tok["ot"])
                        free[6] = tok["ot"] = two(V, OT[:, p, qh * 512:qh * 512 + 512], bank(6), RC[:, :], ALU.mult, t, tok["wo"])

                prep_k(0, 0)
                prep_k(0, 1)
                prep_q(0)
                prep_q(1)
                for i in range(8):
                    s_tile(0, i)
                m_row(0)
                when = {0: 0, 1: 1, 3: 2, 4: 3, 6: 4, 7: 5, 9: 6, 10: 7}
                for u in range(16):
                    p, qh = divmod(u, 2)
                    for n in range(16):
                        if n in when and u + 1 < 16:
                            s_tile(u + 1, when[n])
                        if n == 11 and u + 1 < 16:
                            m_row(u + 1)
                        if n in (2, 6) and qh == 0 and p + 1 < 8:
                            prep_k(p + 1, n // 4)
                        if n == 13 and u + 2 < 16:
                            prep_q(u + 2)
                        st(u, n)
                        if n % 2 == 1:
                            g = 8 * u + n // 2 - 1
                            if g >= 0:
                                pv(g // 8, g % 8)
                pv(15, 7)
                vfree = tok["pv"] = PE.here()
                for i in range(8):
                    tt_ = b * 8 + i
                    bk = 2 + i % 3
                    PE.wait(tok["ot"], t_wo, free[bk])
                    for p in range(8):
                        t = mm(bank(bk)[:, 0:256], OT[:, p, i * 128:i * 128 + 128], WO[:, p, :], p == 0, p == 7,
                               PE.do if p == 7 else PE.raw)
                    tok["wo"] = t
                    t = add_norm(tt_, bank(bk)[:, 0:256], ZB[:, :], [t, t_bo, tok.get(("xv", 3))], bk)
                    t_late = to_xt(X, XT, tt_, bk, t)
                    tok[("late", tt_)] = t_late
                if b == 0:
                    t_wv = wload(c, "L0_xattn_Wv", WV, Y, tok["wo"])
            for i in range(16):
                t_xt[i] = tok[("late", i)]
        P.barrier()

        def row(name, n=256):
            return A[name].rearrange("(o d) -> o d", o=1).broadcast_to([128, n])

        with ExitStack() as c:
            GT = sb(c, "f_GT", [128, 2, 2048])
            AW = sb(c, "f_AW", [128, 2, 256])
            NW = sb(c, "f_NW", [128, 2, 256])
            AB = sb(c, "f_AB", [128, 256])
            NBB = sb(c, "f_NB", [128, 256])
            W1 = [sb(c, f"f_W1{i}", [128, 2, 1024]) for i in range(2)]
            W2 = [sb(c, f"f_W2{i}", [128, 8, 256]) for i in range(2)]
            HT = [sb(c, f"f_HT{i}", [128, 8, 256]) for i in range(2)]
            YT = [sb(c, f"f_YT{i}", [128, 2, 256]) for i in range(2)]
            TM = sb(c, "f_TM", [128, 4, 256])
            CR = sb(c, "f_CR", [84, 128])
            CC = sb(c, "f_CC", [128, 84])
            t_aw = wload(c, "L0_ffn_attn_w", AW[:, :, :], Y)
            t_cr = [P.dma(Y, CR[0:64, :], A["L0_ffn_b1"].rearrange("e (f p) -> (e f) p", p=128)),
                    P.dma(Y, CR[64:80, :], A["L0_ffn_b2"].rearrange("e (f p) -> (e f) p", p=128)),
                    P.dma(Y, CR[80:82, :], A["L0_ffn_ln_g"].rearrange("(f p) -> f p", p=128)),
                    P.dma(Y, CR[82:84, :], A["L0_ffn_ln_b"].rearrange("(f p) -> f p", p=128)),
                    P.dma(Y, AB[:, :], row("L0_ffn_attn_b")), P.dma(Y, NBB[:, :], row("L0_ffn_next_b"))]
            t_w1, t_w2 = {}, {}

            def load_expert(e, *tok):
                t_w1[e] = P.dma(Y, W1[e % 2][:, :, :], A["L0_ffn_w1"][e].rearrange("(c p) n -> p c n", p=128), *tok)
                t_w2[e] = P.dma(Y, W2[e % 2][:, :, :], A["L0_ffn_w2"][e].rearrange("(c p) n -> p c n", p=128), *tok)

            load_expert(0)
            load_expert(1)
            t_nw = wload(c, "L0_ffn_next_w", NW[:, :, :], Y)
            PE.wait(t_cr, free[7])
            t = transpose(bank(7)[:, 0:84], CR[:, :], 84)
            free[7] = t_cc = copy(V, CC[:, :], bank(7)[:, 0:84], t)
            S.wait(t_cc)
            t_g = [None] * 16
            tmfree = [None] * 4
            for i in range(16):
                tm_ = TM[:, i % 4, :]
                t = norm(i, X[:, i, :], tm_, tmfree[i % 4])
                t = to_xt(TM, XT, i, 2 + i % 2, t, scale=CC[:, 80:82], bias=CC[:, 82:84], slot=i % 4)
                bk = 4 + i % 2
                PE.wait(t, t_aw, free[bk])
                for k in range(2):
                    t = mm(bank(bk)[:, 0:256], XT[:, k, 128 * i:128 * i + 128], AW[:, k, :], k == 0, k == 1,
                           PE.do if k else PE.raw)
                free[bk] = t = two(V, tm_, bank(bk)[:, 0:256], X[:, i, :], ALU.add, t)
                t = two(V, tm_, tm_, AB[:, :], ALU.add, t)
                t_g[i] = to_xt(TM, GT, i, 6 + i % 2, t, slot=i % 4)
                tmfree[i % 4] = PE.here()
            gt_pair = [GT[:, k, :].rearrange("p (m t) -> p m t", m=2) for k in range(2)]
            fr, fin = {}, []
            for e in range(8):
                w1, w2, ht, yt = W1[e % 2], W2[e % 2], HT[e % 2], YT[e % 2]
                th = []
                for f in range(8):
                    bk = f % 3
                    o = bank(bk)[:, 0:256]
                    PE.wait(t_w1[e], t_g[e], t_g[e + 8], free[bk])
                    for k in range(2):
                        t = mm(o.rearrange("p (m t) -> p m t", m=2), w1[:, k, 128 * f:128 * f + 128],
                               gt_pair[k][:, :, 128 * e:128 * e + 128], k == 0, k == 1, PE.do if k else PE.raw)
                    free[bk] = t = act(ht[:, f, :], o, ACT.Gelu, t, fr.get(("ht", e - 2)), bias=CC[:, 8 * e + f:8 * e + f + 1])
                    th.append(t)
                ty = []
                for d in range(2):
                    bk = 3 + d
                    PE.wait(t_w2[e], free[bk])
                    for f in range(8):
                        PE.wait(th[f])
                        t = mm(bank(bk)[:, 0:256], w2[:, f, 128 * d:128 * d + 128], ht[:, f, :], f == 0, f == 7,
                               PE.do if f == 7 else PE.raw)
                    free[bk] = t2 = ts(V, yt[:, d, :], bank(bk)[:, 0:256], CC[:, 64 + 2 * e + d:65 + 2 * e + d], None, ALU.add, None,
                                       t, fr.get(("yt", e - 2)))
                    ty.append(t2)
                fr[("ht", e)] = t
                if e + 2 < 8:
                    load_expert(e + 2, t)
                for m in range(2):
                    i = e + 8 * m
                    bk = 5 + m
                    PE.wait(ty, t_nw, free[bk])
                    for k in range(2):
                        t = mm(bank(bk)[:, 0:256], yt[:, k, 128 * m:128 * m + 128], NW[:, k, :], k == 0, k == 1,
                               PE.do if k else PE.raw)
                    fr[("yt", e)] = t
                    tm_ = TM[:, i % 4, :]
                    free[bk] = t = two(V, tm_, bank(bk)[:, 0:256], NBB[:, :], ALU.add, t, tmfree[i % 4])
                    t = act(tm_, tm_, ACT.Gelu, t)
                    t = tmfree[i % 4] = two(V, X[:, i, :], X[:, i, :], tm_, ALU.add, t)
                    fin.append((i, t))
            for i, t in fin:
                t = norm(i, X[:, i, :], X[:, i, :], t)
                t_xt[i] = to_xt(X, XT, i, 2 + i % 4, t)
        P.barrier()

        with ExitStack() as c:
            QT = sb(c, "d_QT", [128, 4, 1024])
            KT = sb(c, "d_KT", [128, 4, 1024])
            VV = sb(c, "d_VV", [128, 8, 512])
            EN = sb(c, "d_EN", [128, 16, 256])
            VB = sb(c, "d_VB", [128, 16, 256])
            al = sb(c, "d_al", [128, 8])
            VBB = sb(c, "d_VBB", [128, 256])
            OBB = sb(c, "d_OBB", [128, 256])
            ER = sb(c, "d_ER", [128, 256], I32)
            EC = sb(c, "d_EC", [128, 256], I32)
            EV = sb(c, "d_EV", [128, 256])
            IX = sb(c, "d_IX", [128, 256], I32)
            IH = sb(c, "d_IH", [128, 256], I32)
            EH = sb(c, "d_EH", [128, 256])
            EL = sb(c, "d_EL", [128, 256])
            EG = sb(c, "d_EG", [128, 256])
            io = sb(c, "d_io", [128, 32])
            ddram = nc.dram_tensor("d_data", [1024 * 1024, 1], F32, kind="Internal").ap()
            adram = nc.dram_tensor("d_alpha", [32, 32], F32, kind="Internal").ap()
            t_e = [P.dma(Y, ER[:, :], A["L1_attn_adj_rows"].rearrange("(p j) -> p j", p=128)),
                   P.dma(Y, EC[:, :], A["L1_attn_adj_cols"].rearrange("(p j) -> p j", p=128)),
                   P.dma(Y, EV[:, :], A["L1_attn_adj_vals"].rearrange("(p j) -> p j", p=128)),
                   P.dma(Y, VBB[:, :], row("L1_attn_wv_b")), P.dma(Y, OBB[:, :], row("L1_attn_out_b"))]
            t_io = G.do(lambda e: e.iota(io[:, :], [[1, 32]], base=0, channel_multiplier=0, allow_small_or_imprecise_dtypes=True))

            t = copy(V, EH[:, :], ER[:, :], t_e)
            t = ts(V, EL[:, :], EH[:, :], 0.0, None, ALU.is_ge, None, t)
            t = two(V, EV[:, :], EV[:, :], EL[:, :], ALU.mult, t)
            t = ts(V, EL[:, :], EH[:, :], 1024.0, None, ALU.is_lt, None, t)
            t = two(V, EV[:, :], EV[:, :], EL[:, :], ALU.mult, t)
            t = ts(V, EH[:, :], EH[:, :], 0.0, 1023.0, ALU.max, ALU.min, t)
            t_r = copy(V, IH[:, :], EH[:, :], t)
            t = copy(V, EL[:, :], EC[:, :], t)
            t = ts(V, EG[:, :], EL[:, :], 0.0, 1024.0, ALU.is_lt, ALU.mult, t)
            t = two(V, EL[:, :], EL[:, :], EG[:, :], ALU.add, t)
            t = ts(V, EL[:, :], EL[:, :], 0.0, 1023.0, ALU.max, ALU.min, t)
            t = sst(V, EL[:, :], EH[:, :], 1024.0, EL[:, :], ALU.mult, ALU.add, t)
            t_ix = copy(V, IX[:, :], EL[:, :], t)
            t = ts(V, EC[:, :], IH[:, :], 5, None, ALU.arith_shift_right, None, t_ix, t_r)
            t = copy(V, EH[:, :], EC[:, :], t)
            t = ts(V, EC[:, :], IH[:, :], 31, None, ALU.bitwise_and, None, t)
            t_hl = copy(V, EL[:, :], EC[:, :], t)

            with ExitStack() as c2:
                WA = sb(c2, "d_WA", [128, 2, 1536])
                WOUT = sb(c2, "d_WOUT", [128, 4, 256])
                WVW = sb(c2, "d_WVW", [128, 2, 256])
                WQE = sb(c2, "d_WQE", [128, 2, 64])
                WKE = sb(c2, "d_WKE", [128, 2, 64])
                TT = sb(c2, "d_TT", [128, 8, 160])
                XL = sb(c2, "d_XL", [128, 2, 128])
                QL = sb(c2, "d_QL", [128, 4, 128])
                KL = sb(c2, "d_KL", [128, 4, 128])
                t_wa = wload(c2, "L1_attn_qkv_w", WA[:, :, :], Y)
                t_wv = wload(c2, "L1_attn_wv_w", WVW[:, :, :], Y)
                t_tt = P.dma(Y, TT[:, :, :], A["conv_toeplitz"])
                t_wo = wload(c2, "L1_attn_out_w", WOUT[:, :, :], Y)
                t_we = [wload(c2, "L1_attn_wq", WQE[:, :, :], Y), wload(c2, "L1_attn_wk", WKE[:, :, :], Y)]
                t_xl = V.do(lambda e: e.tensor_reduce(XL[:, :, :], XT[:, :, :].rearrange("p c (m l) -> p c m l", l=16), AX, ALU.add),
                            t_xt)
                tl = []
                for W0, L, bk, sc in ((0, QL, 0, 1.0 / 128), (512, KL, 1, 1.0 / 16)):
                    PE.wait(t_wa, t_xl, free[bk])
                    for p in range(4):
                        for k in range(2):
                            t = mm(bank(bk)[:, 128 * p:128 * p + 128], WA[:, k, W0 + 128 * p:W0 + 128 * p + 128], XL[:, k, :],
                                   k == 0, k == 1, PE.do if k and p == 3 else PE.raw)
                    free[bk] = t = act(L[:, :, :], bank(bk).rearrange("p (a n) -> p a n", a=4), ACT.Copy, t, scale=sc)
                    tl.append(t)
                A2 = sb(c2, "d_A2", [128, 8, 64])
                sm = sb(c2, "d_sm", [128, 3, 8])
                PE.wait(tl, free[2])
                for h in range(2):
                    if h:
                        PE.wait(t)
                    for bp in range(8):
                        b, p = divmod(bp, 4)
                        t = mm(bank(2)[64 * h:64 * h + 64, 64 * bp:64 * bp + 64], QL[64 * h:64 * h + 64, p, 64 * b:64 * b + 64],
                               KL[64 * h:64 * h + 64, p, 64 * b:64 * b + 64], True, True, PE.do if bp == 7 else PE.raw)

                def softmax(dst, ps, n, w, m, tok, *after):
                    for d, s_, mo in zip(dst, ps, m):
                        tok = red(mo, s_, ALU.max, tok)
                    for d, s_, mo in zip(dst, ps, m):
                        tok = two(V, d, s_, mo.unsqueeze(2).broadcast_to([128, mo.shape[1], w]), ALU.subtract, tok, *after)
                    return tok

                a2 = A2[:, :, :]
                t = softmax([a2], [bank(2).rearrange("p (a n) -> p a n", n=64)], 8, 64, [sm[:, 0, :]], t)
                free[2] = t
                t = act(a2, a2, ACT.Exp, t)
                t = red(sm[:, 1, :], a2, ALU.add, t)
                t = rec(sm[:, 2, :], sm[:, 1, :], t)
                t_a2 = two(V, a2, a2, sm[:, 2, :].unsqueeze(2).broadcast_to([128, 8, 64]), ALU.mult, t)
                RM = sb(c2, "d_RM", [128, 4])
                R1 = sb(c2, "d_R1", [1, 4])
                t = red(sm[:, 1, :], a2, ALU.add, t_a2)
                t_rm = red(RM[:, 0:1], sm[:, 1, :], ALU.max, t)
                PE.wait(t_a2, free[3], t_ones)
                for h in range(2):
                    if h:
                        PE.wait(t)
                    t = mm(bank(3)[64 * h:64 * h + 64, :], onesf[64 * h:64 * h + 64, 0:64], A2[64 * h:64 * h + 64, :, :], True, True,
                           PE.do)
                free[3] = t = red(RM[:, 1:2], bank(3), ALU.max, t)
                PE.wait(t, t_rm, free[7])
                transpose(bank(7)[0:1, 0:128], RM[:, 0:1])
                t = transpose(bank(7)[0:1, 128:256], RM[:, 1:2])
                t = red(R1[:, 0:2], bank(7)[0:1, 0:256].rearrange("p (a n) -> p a n", a=2), ALU.max, t)
                t = two(V, R1[:, 2:3], R1[:, 0:1], R1[:, 1:2], ALU.mult, t)
                t = rec(R1[:, 3:4], R1[:, 2:3], t)
                PE.wait(t)
                t = mm(bank(7)[:, 256:257], onesf[0:1, :], R1[:, 3:4], True, True, PE.do)
                free[7] = t_sc = copy(V, RM[:, 2:3], bank(7)[:, 256:257], t)
                I4 = sb(c2, "d_I4", [128, 4, 128])
                M = {n: sb(c2, "d_M" + n, [128, 4, 128]) for n in ("A", "AT", "z", "zT", "xz", "xzT", "t")}
                for p in range(4):
                    t = copy(G, I4[:, p, :], ident[:, :])
                t_i4 = t
                t = fill(G, M["A"][:, :, :], 0.0)
                copy(V, M["A"][0:64, :, 0:64], A2[0:64, 0:4, :], t, t_a2)
                t_A = copy(V, M["A"][64:128, :, 64:128], A2[64:128, 0:4, :])
                PE.wait(t_A, free[0])
                for p in range(4):
                    t = transpose(bank(0)[:, 128 * p:128 * p + 128], M["A"][:, p, :])
                bv = [bank(i).rearrange("p (a n) -> p a n", a=4) for i in range(8)]
                free[0] = t_AT = copy(V, M["AT"][:, :, :], bv[0], t)
                t_z = ts(V, M["z"][:, :, :], M["AT"][:, :, :], RM[:, 2:3], None, ALU.mult, None, t_AT, t_sc)
                t_zT = ts(V, M["zT"][:, :, :], M["A"][:, :, :], RM[:, 2:3], None, ALU.mult, None, t_A, t_sc)

                def product(bk, l, r, *tok):
                    PE.wait(free[bk], *tok)
                    for p in range(4):
                        t = mm(bank(bk)[:, 128 * p:128 * p + 128], M[l][:, p, :], M[r][:, p, :], True, True,
                               PE.do if p == 3 else PE.raw)
                    return t

                def minus(k, bk, tok):
                    free[bk] = t = sst(V, M["t"][:, :, :], I4[:, :, :], k, bv[bk], ALU.mult, ALU.subtract, tok, t_i4)
                    return t

                def full(n):
                    return M[n][:, :, :]

                background = []

                def breathe():
                    if background:
                        background.pop(0)()

                t_qt, t_kt, t_vv, t_vb = {}, {}, {}, {}
                nb = [0]

                def bg_bank():
                    nb[0] += 1
                    return 4 + nb[0] % 4

                def proj(p, half, W0, D, sc, toks):
                    def go():
                        bk = bg_bank()
                        PE.wait(t_wa, free[bk], t_xt)
                        for k in range(2):
                            t = mm(bank(bk), WA[:, k, W0 + 128 * p:W0 + 128 * p + 128], XT[:, k, 512 * half:512 * half + 512],
                                   k == 0, k == 1, PE.do if k else PE.raw)
                        free[bk] = toks[(p, half)] = act(D[:, p, 512 * half:512 * half + 512], bank(bk), ACT.Copy, t, scale=sc)
                    return go

                def vproj(i):
                    def go():
                        bk = bg_bank()
                        PE.wait(t_wa, free[bk], t_xt)
                        for k in range(2):
                            t = mm(bank(bk), XT[:, k, 128 * i:128 * i + 128], WA[:, k, 1024:1536], k == 0, k == 1,
                                   PE.do if k else PE.raw)
                        free[bk] = t_vv[i] = copy(S, VV[:, i, :], bank(bk), t)
                    return go

                def valproj(i):
                    def go():
                        bk = bg_bank()
                        PE.wait(t_wv, free[bk], t_xt)
                        for k in range(2):
                            t = mm(bank(bk)[:, 0:256], XT[:, k, 128 * i:128 * i + 128], WVW[:, k, :], k == 0, k == 1,
                                   PE.do if k else PE.raw)
                        free[bk] = t_vb[i] = two(V, VB[:, i, :], bank(bk)[:, 0:256], VBB[:, :], ALU.add, t)
                    return go

                for p in range(4):
                    for half in range(2):
                        background.append(proj(p, half, 512, KT, 1.0, t_kt))
                background += [vproj(i) for i in range(8)]
                for p in range(4):
                    for half in range(2):
                        background.append(proj(p, half, 0, QT, 0.125, t_qt))
                background += [valproj(i) for i in range(16)]
                for it in range(6):
                    t1 = product(0, "AT", "z", t_AT, t_z)
                    t2 = product(1, "z", "AT")
                    free[0] = t3 = copy(S, full("xz"), bv[0], t1)
                    t4 = sst(V, full("t"), I4[:, :, :], 7.0, bv[0], ALU.mult, ALU.subtract, t1, t_i4, t3)
                    free[0] = t4
                    free[1] = t5 = copy(S, full("xzT"), bv[1], t2)
                    breathe()
                    breathe()
                    t = product(2, "xzT", "t", t4, t5)
                    t = minus(15.0, 2, t)
                    breathe()
                    breathe()
                    t = product(3, "xzT", "t", t)
                    t = minus(13.0, 3, t)
                    breathe()
                    breathe()
                    if it < 5:
                        t1 = product(0, "zT", "t", t, t_zT)
                    t2 = product(1, "t", "zT", t, t_zT)
                    if it < 5:
                        free[0] = t_z = ts(V, full("z"), bv[0], 0.25, None, ALU.mult, None, t1, t2)
                    free[1] = t_zT = act(full("zT"), bv[1], ACT.Copy, t2, scale=0.25)
                while background:
                    breathe()
                P3 = sb(c2, "d_P3", [128, 2, 1024])
                P3T = sb(c2, "d_P3T", [128, 2, 8, 128])
                s3 = sb(c2, "d_s3", [128, 4, 3])
                W3 = sb(c2, "d_W3", [128, 4, 64])
                W2 = sb(c2, "d_W2", [128, 4, 64])
                SS = sb(c2, "d_SS", [128, 2, 8, 64])
                A1T = EN[:, :, :].rearrange("p (a b) n -> p a (b n)", a=4)
                s1 = sb(c2, "d_s1", [128, 2, 3, 8])
                OT = QT
                last = {}
                t_w3 = []
                for p in range(4):
                    PE.wait(t_kt[(p, 0)], t_kt[(p, 1)], free[0], free[1], tl)
                    for h in range(2):
                        if h:
                            PE.wait(t)
                        for half in range(2):
                            t = mm(bank(half)[64 * h:64 * h + 64, :], QL[64 * h:64 * h + 64, p, 0:64],
                                   KT[64 * h:64 * h + 64, p, 512 * half:512 * half + 512], True, True, PE.do)
                    t = rmax(s3[:, p, 0:1], bank(0, 2), t)
                    t = act(P3[:, p % 2, :], bank(0, 2), ACT.Exp, t, last.get(("p3", p - 2)), bias=s3[:, p, 0:1],
                            accum_out=s3[:, p, 1:2])
                    free[0] = free[1] = t
                    t_rs = rec(s3[:, p, 2:3], s3[:, p, 1:2], t)
                    tt3 = []
                    for g in range(2):
                        PE.wait(t, free[2 + g])
                        for j in range(4):
                            t6 = transpose(bank(2 + g)[:, 128 * j:128 * j + 128], P3[:, p % 2, 128 * (4 * g + j):128 * (4 * g + j) + 128])
                        free[2 + g] = t7 = copy(S if g else V, P3T[:, p % 2, 4 * g:4 * g + 4, :], bv[2 + g], t6, last.get(("w3", p - 2)))
                        tt3.append(t7)
                    last[("p3", p)] = t6
                    PE.wait(tt3, free[4], [t_vv[i] for i in range(8)])
                    for kt in range(8):
                        for h in range(2):
                            t = mm(bank(4)[64 * h:64 * h + 64, 0:64], P3T[:, p % 2, kt, 64 * h:64 * h + 64],
                                   VV[:, kt, 128 * p + 64 * h:128 * p + 64 * h + 64], kt == 0, kt == 7,
                                   PE.do if kt == 7 and h else PE.raw)
                    last[("w3", p)] = t
                    free[4] = t = ts(V, W3[:, p, :], bank(4)[:, 0:64], s3[:, p, 2:3], None, ALU.mult, None, t, t_rs)
                    t_w3.append(t)
                t_a1 = []
                for i in range(8):
                    k = i % 2
                    PE.wait([t_qt[(p, i // 4)] for p in range(4)], tl, free[0], free[1])
                    for h in range(8):
                        r = 64 * (h % 2)
                        t = mm(bank(h % 2)[:, 64 * (h // 2):64 * (h // 2) + 64], QT[r:r + 64, h // 2, 128 * i:128 * i + 128],
                               KL[r:r + 64, h // 2, 0:64], True, True, PE.do)
                    ss = SS[:, k, :, :]
                    sv = ss.rearrange("p (g k) n -> p g k n", k=2)
                    mv = s1[:, k, 0, :].rearrange("p (g k) -> p g k", k=2)
                    t = softmax([sv[:, :, 0, :], sv[:, :, 1, :]],
                                [bank(q)[:, 0:256].rearrange("p (a n) -> p a n", n=64) for q in range(2)], 4, 64,
                                [mv[:, :, 0], mv[:, :, 1]], t, last.get(("a1", i - 2)))
                    free[0] = free[1] = t
                    t = act(ss, ss, ACT.Exp, t)
                    t = red(s1[:, k, 1, :], ss, ALU.add, t)
                    t = rec(s1[:, k, 2, :], s1[:, k, 1, :], t)
                    t = two(V, ss, ss, s1[:, k, 2, :].unsqueeze(2).broadcast_to([128, 8, 64]), ALU.mult, t)
                    bk = 2 + i % 2
                    PE.wait(t, free[bk])
                    for p in range(4):
                        t = transpose(bank(bk)[:, 128 * p:128 * p + 128], SS[:, k, 2 * p:2 * p + 2, :])
                    last[("a1", i)] = t
                    free[bk] = t = copy(S, A1T[:, :, 128 * i:128 * i + 128], bv[bk], t)
                    t_a1.append(t)
                PE.wait(t_zT, t_w3, free[4])
                for p in range(4):
                    t = mm(bank(4)[:, 64 * p:64 * p + 64], M["zT"][:, p, :], W3[:, p, :], True, True, PE.do)
                free[4] = t_w2 = copy(V, W2[:, :, :], bank(4)[:, 0:256].rearrange("p (a n) -> p a n", a=4), t)
                t_ot = {}
                for p in range(4):
                    for half in range(2):
                        bk = 5 + (2 * p + half) % 3
                        PE.wait(t_w2, t_a1, t_tt, free[bk])
                        for h in range(2):
                            if h:
                                PE.wait(t)
                            t = mm(bank(bk)[64 * h:64 * h + 64, :], W2[64 * h:64 * h + 64, p, :],
                                   A1T[64 * h:64 * h + 64, p, 512 * half:512 * half + 512], True, False, PE.do)
                        for kb in range(8):
                            lo, hi = max(128 * kb - 16, 512 * half), min(128 * kb + 144, 512 * half + 512)
                            if lo >= hi:
                                continue
                            c0 = lo - 128 * kb + 16
                            for h in range(2):
                                t = mm(bank(bk)[64 * h:64 * h + 64, lo - 512 * half:hi - 512 * half],
                                       VV[:, kb, 128 * p + 64 * h:128 * p + 64 * h + 64], TT[:, 2 * p + h, c0:c0 + hi - lo],
                                       False, False, PE.do)
                        free[bk] = t_ot[(p, half)] = copy(V if half else S, OT[:, p, 512 * half:512 * half + 512], bank(bk), t,
                                                          last[("a1", 7)])
                t_en = [None] * 16
                ET = KT[:, 0:2, :]
                t_et = []
                for i in range(8):
                    bk = 2 + i % 2
                    PE.wait([t_ot[(p, i // 4)] for p in range(4)], t_wo, free[bk])
                    for p in range(4):
                        t = mm(bank(bk)[:, 0:256], OT[:, p, 128 * i:128 * i + 128], WOUT[:, p, :], p == 0, p == 3, PE.do)
                    t = two(V, LS[:, i % 4, :], bank(bk)[:, 0:256], OBB[:, :], ALU.add, t, t_en[8 + i - 4] if i >= 4 else None)
                    free[bk] = t
                    t_en[i] = two(V, EN[:, i, :], LS[:, i % 4, :], X[:, i, :], ALU.add, t)
                    t_en[8 + i] = two(G, EN[:, 8 + i, :], LS[:, i % 4, :], X[:, 8 + i, :], ALU.add, t)
                    t_et.append(to_xt(EN, ET, i, 5 + i % 2, t_en[i], after=[last[("w3", 3)]]))
                QE = VV[0:64, 0:2, :].rearrange("p a n -> p (a n)")
                KE = VV[0:64, 2:4, :].rearrange("p a n -> p (a n)")
                t_qe = []
                for half in range(2):
                    for W, D, sc, bk in ((WQE, QE, 0.125, 2 * half), (WKE, KE, 1.0, 2 * half + 1)):
                        PE.wait(t_et, t_we, free[bk])
                        for k in range(2):
                            t = mm(bank(bk)[0:64, :], W[:, k, :], ET[:, k, 512 * half:512 * half + 512], k == 0, k == 1, PE.do)
                        free[bk] = t = act(D[:, 512 * half:512 * half + 512], bank(bk)[0:64, :], ACT.Copy, t, scale=sc)
                        t_qe.append(t)
                t_dd = []
                for i in range(8):
                    bk = 4 + 2 * (i % 2)
                    PE.wait(t_qe, free[bk], free[bk + 1])
                    for half in range(2):
                        t = mm(bank(bk + half), QE[:, 128 * i:128 * i + 128], KE[:, 512 * half:512 * half + 512], True, True, PE.do)
                    t = copy(S if i % 2 else V, P3[:, i % 2, :], bank(bk, 2), t, t_dd[i - 2] if i > 1 else None)
                    free[bk] = free[bk + 1] = t
                    t_dd.append(P.dma(Y, ddram.rearrange("(t p n) o -> t p (n o)", p=128, n=1024)[i], P3[:, i % 2, :], t))
            P.barrier()
            with ExitStack() as c2:
                OHH = sb(c2, "d_OHH", [128, 256, 32])
                OHL = sb(c2, "d_OHL", [128, 256, 32])
                i32 = io[:, :].unsqueeze(1).broadcast_to([128, 256, 32])
                t_hh = two(V, OHH[:, :, :], EH[:, :].unsqueeze(2).broadcast_to([128, 256, 32]), i32, ALU.is_equal, t_hl, t_io)
                t = two(V, OHL[:, :, :], EL[:, :].unsqueeze(2).broadcast_to([128, 256, 32]), i32, ALU.is_equal, t_hl)
                t_g = []
                for j in range(256):
                    t_g.append(P.gather(EG[:, j:j + 1], ddram, IX[:, j:j + 1], t_ix, t_dd))
                t_g = t_g[-96:]
                t = two(V, EG[:, :], EG[:, :], EV[:, :], ALU.mult, t_g)
                t = two(V, OHL[:, :, :], OHL[:, :, :], EG[:, :].unsqueeze(2).broadcast_to([128, 256, 32]), ALU.mult, t)
                PE.wait(t, t_hh, free[0])
                for j in range(256):
                    t = mm(bank(0)[0:32, 0:32], OHH[:, j, :], OHL[:, j, :], j == 0, j == 255, PE.do if j == 255 else PE.raw)
                AR = sb(c2, "d_AR", [32, 32])
                r_ = sb(c2, "d_r", [32, 8])
                t = red(r_[:, 0:1], bank(0)[0:32, 0:32], ALU.max, t)
                PE.wait(t, free[1])
                t = transpose(bank(1)[0:1, 0:32], r_[:, 0:1], 32)
                t = red(r_[0:1, 1:2], bank(1)[0:1, 0:32], ALU.max, t)
                t = ts(V, r_[0:1, 1:2], r_[0:1, 1:2], -1.0, None, ALU.mult, None, t)
                PE.wait(t)
                t = mm(bank(1)[0:32, 64:65], onesf[0:1, 0:32], r_[0:1, 1:2], True, True, PE.do)
                t = copy(V, r_[:, 2:3], bank(1)[0:32, 64:65], t)
                t = act(AR[:, :], bank(0)[0:32, 0:32], ACT.Exp, t, bias=r_[:, 2:3], accum_out=r_[:, 3:4])
                free[0] = t
                PE.wait(t)
                t = mm(bank(1)[0:32, 128:129], onesf[0:32, 0:32], r_[:, 3:4], True, True, PE.do)
                free[1] = t = rec(r_[:, 4:5], bank(1)[0:32, 128:129], t)
                t = ts(V, AR[:, :], AR[:, :], r_[:, 4:5], None, ALU.mult, None, t)
                t = P.dma(Y, adram, AR[:, :], t)
                A8 = sb(c2, "d_A8", [8, 128])
                t = P.dma(Y, A8[:, :], adram.rearrange("a b -> (a b)").rearrange("(t p) -> t p", p=128), t)
                PE.wait(t, free[2])
                t = transpose(bank(2)[:, 0:8], A8[:, :], 8)
                free[2] = t_al = copy(V, al[:, :], bank(2)[:, 0:8], t)
                SG = sb(c2, "d_SG", [128, 4, 256])
                XLm = sb(c2, "d_XLm", [128, 4, 256])
                last = {}
                fin = []
                for i in range(16):
                    k = i % 4
                    xl, sg = XLm[:, k, :], SG[:, k, :]
                    t1 = ts(V, xl, VB[:, i, :], al[:, i % 8:i % 8 + 1], None, ALU.mult, None, t_al, last.get(("xl", k)))
                    t = act(sg, xl, ACT.Sigmoid, t1, last.get(("sg", k)), scale=-1.0)
                    t2 = act(sg, sg, ACT.Square, t)
                    t3 = two(G, xl, xl, EN[:, i, :], ALU.subtract, t)
                    t = two(V, sg, sg, xl, ALU.mult, t2, t3)
                    last[("xl", k)] = t
                    t = two(V, sg, sg, EN[:, i, :], ALU.add, t)
                    t = sst(V, X[:, i, :], sg, 2.0, X[:, i, :], ALU.mult, ALU.add, t)
                    last[("sg", k)] = t
                    fin.append(t)
                for i, t in enumerate(fin):
                    t = norm(i, X[:, i, :], X[:, i, :], t)
                    t_xt[i] = to_xt(X, XT, i, 2 + i % 4, t)
        P.barrier()

        with ExitStack() as c:
            FB = [sb(c, f"g_FB{i}", [128, 16, 77]) for i in range(2)]
            BM = [sb(c, f"g_BM{i}", [128, 16, 77]) for i in range(2)]
            MB = sb(c, "g_MB", [128, 2, 77])
            t_mb = P.dma(Y, MB[:, :, :], A["mask_Bx1x1xS2_ff0"].rearrange("b o u s -> (o u) b s").broadcast_to([128, 2, 77]))
            fb_t, bm_t, bm_free = {}, {}, {}

            def load_bias(i):
                fb_t[i] = P.dma(Y, FB[i % 2][:, :, :],
                                A["fside_1x16xSxS2_0"][0, :, 128 * (i % 8):128 * (i % 8) + 128, :].rearrange("h q s -> q h s"),
                                bm_t.get(i - 2))

            def bias_of(i):
                if i == 0:
                    load_bias(0)
                    load_bias(1)
                bm_t[i] = two(G, BM[i % 2][:, :, :], FB[i % 2][:, :, :],
                              MB[:, i // 8, :].unsqueeze(1).broadcast_to([128, 16, 77]), ALU.add, fb_t[i], t_mb,
                              bm_free.get(i - 2))
                if i + 2 < 16:
                    load_bias(i + 2)
                return BM[i % 2][:, :, :], bm_t[i]

            def emit_g(i, ps, bk, tok):
                t = add_norm(i, ps, None, tok, bk)
                t_xt[i] = to_xt(X, XT, i, 3 + i % 2, t)

            ctx_attention(c, "g_", list(t_xt), 1.0, bias_of, ("L1_xattn_Wq", "L1_xattn_Wk", "L1_xattn_Wv", "L1_xattn_Wo"), emit_g,
                          bm_free)
        P.barrier()

        with ExitStack() as c:
            WG = [sb(c, f"h_WG{i}", [128, 2, 256]) for i in range(2)]
            WU = [sb(c, f"h_WU{i}", [128, 2, 256]) for i in range(2)]
            WD = [sb(c, f"h_WD{i}", [128, 2, 256]) for i in range(2)]
            WR = sb(c, "h_WR", [128, 2, 8])
            TE = sb(c, "h_TE", [128, 2])
            R = {n: sb(c, "h_" + n, [128, 16, 8]) for n in ("inh", "dist", "w", "fb", "z", "rank")}
            R8 = [sb(c, f"h_R8{i}", [128, 16, 8, 8]) for i in range(2)]
            LT = sb(c, "h_LT", [128, 8, 8])
            rs = sb(c, "h_rs", [128, 2, 16])
            SL = sb(c, "h_SL", [128, 2, 512])
            HT = [sb(c, f"h_HT{i}", [128, 2, 512]) for i in range(2)]
            gc = sb(c, "h_gc", [128, 1])
            t_wr = wload(c, "L1_ffn_Wr", WR[:, :, :], Y)
            t_te = P.dma(Y, TE[:, 0:1], A["L1_ffn_temperature"].rearrange("(o d) -> o d", o=1).broadcast_to([128, 1]))
            t_w = {}

            def load_moe(e, *tok):
                t_w[e] = [P.dma(Y, W[e % 2][:, :, :], A[n][e].rearrange("(c p) n -> p c n", p=128), *tok)
                          for n, W in (("L1_ffn_Wg", WG), ("L1_ffn_Wu", WU), ("L1_ffn_Wd", WD))]

            load_moe(0)
            load_moe(1)
            CENTER, LOWER, UPPER = float(np.exp(-1.0)), float(0.5 - np.log(4.0 / 3.0)), 0.5
            t = fill(G, LT[:, :, :], 0.0)
            t_lt = G.do(lambda e: e.affine_select(out=LT[:, :, :], in_=LT[:, :, :], compare_op=ALU.is_ge, fill=1.0,
                                                  base=0, pattern=[[-1, 8], [1, 8]], channel_multiplier=0), t)
            PE.wait(t_wr, t_xt, free[7])
            for i in range(16):
                for k in range(2):
                    t = mm(bank(7)[:, 8 * i:8 * i + 8], XT[:, k, 128 * i:128 * i + 128], WR[:, k, :], k == 0, k == 1, PE.do)
            def r3(n):
                return R[n][:, :, :]

            t_r = rec(TE[:, 1:2], TE[:, 0:1], t_te)
            free[7] = t = ts(V, r3("z"), bank(7)[:, 0:128].rearrange("p (a n) -> p a n", n=8), TE[:, 1:2], None, ALU.mult, None, t, t_r)
            t_inh = act(r3("inh"), r3("z"), ACT.Sigmoid, t)
            t = ts(V, r3("dist"), r3("inh"), CENTER, None, ALU.subtract, None, t_inh)
            t = act(r3("dist"), r3("dist"), ACT.Abs, t)
            t1 = act(r3("w"), r3("dist"), ACT.Exp, t, scale=-1.0 / 0.1)
            t2 = act(r3("fb"), r3("dist"), ACT.Exp, t, scale=-1.0 / 0.3)
            t = sst(V, r3("w"), r3("inh"), LOWER, r3("w"), ALU.is_ge, ALU.mult, t1)
            t = sst(V, r3("w"), r3("inh"), UPPER, r3("w"), ALU.is_le, ALU.mult, t)
            t_w8 = red(rs[:, 0, :], r3("w"), ALU.add, t)
            a = R["fb"][:, :, :].unsqueeze(2).broadcast_to([128, 16, 8, 8])
            b_ = R["fb"][:, :, :].unsqueeze(3).broadcast_to([128, 16, 8, 8])
            t = two(V, R8[0][:, :, :, :], a, b_, ALU.is_gt, t2)
            t = two(V, R8[1][:, :, :, :], a, b_, ALU.is_equal, t)
            t = two(V, R8[1][:, :, :, :], R8[1][:, :, :, :], LT[:, :, :].unsqueeze(1).broadcast_to([128, 16, 8, 8]), ALU.mult, t, t_lt)
            t = two(V, R8[0][:, :, :, :], R8[0][:, :, :, :], R8[1][:, :, :, :], ALU.add, t)
            t = red(r3("rank"), R8[0][:, :, :, :], ALU.add, t)
            t = sst(V, r3("fb"), r3("rank"), 2.0, r3("fb"), ALU.is_lt, ALU.mult, t)

            def share(n, k, tok):
                tok = red(rs[:, k, :], r3(n), ALU.add, tok)
                tok = ts(V, rs[:, k, :], rs[:, k, :], 1e-8, None, ALU.max, None, tok)
                tok = rec(rs[:, k, :], rs[:, k, :], tok)
                return two(V, r3(n), r3(n), rs[:, k, :].unsqueeze(2).broadcast_to([128, 16, 8]), ALU.mult, tok)

            t = share("fb", 1, t)
            t = ts(V, rs[:, 0, :], rs[:, 0, :], 1e-8, None, ALU.is_lt, None, t, t_w8)
            pick = rs[:, 0, :].unsqueeze(2).broadcast_to([128, 16, 8])
            t = two(V, r3("fb"), r3("fb"), pick, ALU.mult, t)
            t = two(V, r3("z"), r3("w"), pick, ALU.mult, t)
            t = two(V, r3("w"), r3("w"), r3("z"), ALU.subtract, t)
            t = two(V, r3("w"), r3("w"), r3("fb"), ALU.add, t)
            t_rw = share("w", 0, t)
            fr = {}
            t_acc = [None] * 16
            n = 0
            jobs = [(e, tb) for e in range(8) for tb in range(4)]
            t_h = {}

            def up(n):
                e, tb = jobs[n]
                ends = []
                for i in range(2):
                    for W, bk in ((WG, 0), (WU, 1)):
                        bk = bk + 2 * i
                        PE.wait(t_w[e], free[bk])
                        for k in range(2):
                            t = mm(bank(bk), W[e % 2][:, k, 128 * i:128 * i + 128], XT[:, k, 512 * tb:512 * tb + 512],
                                   k == 0, k == 1, PE.do)
                        if W is WG:
                            free[bk] = t1 = act(SL[:, i, :], bank(bk), ACT.Silu, t, fr.get(("sl", i)))
                    free[bk] = fr[("sl", i)] = t = two(V, HT[n % 2][:, i, :], bank(bk), SL[:, i, :], ALU.mult, t, t1,
                                                       fr.get(("ht", n - 2)))
                    ends.append(t)
                t_h[n] = ends

            def down(n):
                e, tb = jobs[n]
                for i in range(4):
                    tt_ = 4 * tb + i
                    bk = 4 + i
                    PE.wait(t_h[n], free[bk])
                    for k in range(2):
                        t = mm(bank(bk)[:, 0:256], HT[n % 2][:, k, 128 * i:128 * i + 128], WD[e % 2][:, k, :], k == 0, k == 1, PE.do)
                    free[bk] = t_acc[tt_] = sst(V, X[:, tt_, :], bank(bk)[:, 0:256], R["w"][:, tt_, e:e + 1], X[:, tt_, :],
                                                ALU.mult, ALU.add, t, t_rw, t_acc[tt_])
                fr[("ht", n)] = t
                if tb == 3 and e + 2 < 8:
                    load_moe(e + 2, t)

            for n in range(33):
                if n < 32:
                    up(n)
                if n:
                    down(n - 1)
            t_fin = [norm(i, X[:, i, :], X[:, i, :], t_acc[i]) for i in range(16)]

        Y.wait([P.dma(Y, out.rearrange("b (t p) d -> p (b t) d", p=128)[:, 4 * i:4 * i + 4, :], X[:, 4 * i:4 * i + 4, :],
                      t_fin[4 * i:4 * i + 4]) for i in range(4)])

        block = ctx.enter_context(nc.Block())

        @block.sync
        def _(e):
            Y.run(e)

        @block.tensor
        def _(e):
            PE.run(e)

        @block.vector
        def _(e):
            V.run(e)

        @block.scalar
        def _(e):
            S.run(e)

        @block.gpsimd
        def _(e):
            G.run(e)


_T = {"L0_attn_Wq": "L0_attn_WqT", "L0_attn_Wk": "L0_attn_WkT", "L0_attn_Wv": "L0_attn_WvT", "L0_attn_Wff": "L0_attn_WffT"}
_UNUSED = ("L0_ffn_gate_w",)


def kernel(**inputs):
    import concourse.bacc as _bacc
    from concourse.bass_utils import run_bass_kernel_spmd as _run

    nc = _bacc.Bacc("TRN2", target_bir_lowering=False, num_devices=1)
    arrays, A = {}, {}
    for name in inputs:
        if name in _UNUSED:
            continue
        if name == "L1_attn_conv_w":
            w = np.asarray(inputs[name])[:, 0, :, 0]
            a = np.zeros((128, 8, 160), w.dtype)
            for p in range(128):
                for j in range(33):
                    a[p, :, p + 32 - j] = w[:, j]
            arrays["in_conv"] = a
            A["conv_toeplitz"] = nc.dram_tensor("in_conv", a.shape, F32, kind="ExternalInput").ap()
            continue
        a = np.asarray(inputs[name])
        key = name
        if name in _T:
            a, key = a.T, _T[name]
        a = np.ascontiguousarray(a)
        arrays[f"in_{key}"] = a
        A[key] = nc.dram_tensor(f"in_{key}", a.shape, mybir.dt.from_np(a.dtype), kind="ExternalInput").ap()
    out = nc.dram_tensor("out_0", (2, 1024, 256), F32, kind="ExternalOutput").ap()
    build(nc, A, out)
    r = _run(nc, [arrays], core_ids=[0])
    return r.results[0]["out_0"]
```

```python
from contextlib import ExitStack

import numpy as np

import concourse.bass as bass
from concourse import mybir

F32 = mybir.dt.float32
F32R = mybir.dt.float32r
BF16 = mybir.dt.bfloat16
I32 = mybir.dt.int32
ALU = mybir.AluOpType
ACT = mybir.ActivationFunctionType
AX = mybir.AxisListType.X


class Queue:

    def __init__(self, sem, serial=False):
        self.sem, self.n, self.ops, self.passed, self.serial = sem, 0, [], {}, serial

    def wait(self, *tokens):
        for t in tokens:
            if isinstance(t, list):
                self.wait(*t)
            elif t is not None and self.passed.get(t[2], 0) < t[1]:
                self.passed[t[2]] = t[1]
                self.ops.append((lambda e, t=t: e.wait_ge(t[0], t[1]), None))

    def raw(self, fn):
        self.ops.append((fn, None))

    def do(self, fn, *tokens):
        self.wait(*tokens)
        if self.serial:
            self.wait(self.here())
        self.n += 1
        self.ops.append((fn, (self.sem, 1)))
        return (self.sem, self.n, id(self))

    def here(self):
        return (self.sem, self.n, id(self)) if self.n else None

    def run(self, e):
        for fn, inc in self.ops:
            ins = fn(e)
            if inc:
                ins.then_inc(*inc)


class Program:
    def __init__(self, nc, ctx):
        self.nc, self.ctx = nc, ctx
        self.PE, self.V, self.S, self.G, self.Y = [Queue(ctx.enter_context(nc.semaphore(n)), n == "pool") for n in
                                                   ("pe", "dve", "act", "pool", "sp")]
        self.dsem = [ctx.enter_context(nc.semaphore(f"dma{i}")) for i in range(96)]
        self.dcount = [0] * 96
        self.dnext = 0
        self.gsem = [ctx.enter_context(nc.semaphore(f"gather{i}")) for i in range(16)]
        self.gcount = [0] * 16
        self.gnext = 0

    def dma(self, q, out, in_, *tokens):
        if out.dtype == F32R:
            out = out.bitcast(F32)
        if in_.dtype == F32R:
            in_ = in_.bitcast(F32)
        i = self.dnext % 96
        self.dnext += 1
        sem, key = self.dsem[i], f"dma{i}"
        if self.dcount[i]:
            q.wait((sem, self.dcount[i], key))
        q.wait(*tokens)
        self.dcount[i] += 16
        q.ops.append((lambda e: e.dma_start(out, in_), (sem, 16)))
        return (sem, self.dcount[i], key)

    def scatter_add(self, out, in_, idx, *tokens):
        i = self.gnext % 16
        self.gnext += 1
        sem, key = self.gsem[i], f"gather{i}"
        if self.gcount[i]:
            self.G.wait((sem, self.gcount[i], key))
        self.G.wait(*tokens)
        self.gcount[i] += 16
        self.G.ops.append((lambda e: e.indirect_dma_start(out, bass.IndirectOffsetOnAxis(ap=idx, axis=0), in_, None,
                                                          compute_op=ALU.add), (sem, 16)))
        return (sem, self.gcount[i], key)

    def everything(self):
        t = [q.here() for q in (self.PE, self.V, self.S, self.G)]
        return t + [(self.dsem[i], self.dcount[i], f"dma{i}") for i in range(96) if self.dcount[i]] + [
            (self.gsem[i], self.gcount[i], f"gather{i}") for i in range(16) if self.gcount[i]]

    def barrier(self):
        t = self.everything()
        for q in (self.PE, self.V, self.S, self.G, self.Y):
            q.wait(t)


def build(nc, A, out):
    with ExitStack() as ctx:
        P = Program(nc, ctx)
        PE, V, S, G, Y = P.PE, P.V, P.S, P.G, P.Y

        def sb(c, name, shape, dt=F32):
            return c.enter_context(nc.sbuf_tensor(name, shape, dt))

        PS = ctx.enter_context(nc.psum_tensor("PS", [128, 4096], F32))

        def bank(i, n=1):
            return PS[:, 512 * i:512 * (i + n)]

        free = [None] * 8

        def mm(o, l, r, st, sp, q=PE.raw):
            return q(lambda e: e.matmul(o, l, r, start=st, stop=sp, skip_group_check=True))

        def copy(q, o, i, *t):
            return q.do(lambda e: e.copy(o, i) if q is S else e.tensor_copy(o, i), *t)

        def act(o, i, f, *t, **kw):
            return S.do(lambda e: e.activation(o, i, f, **kw), *t)

        def two(q, o, a, b, op, *t):
            return q.do(lambda e: e.tensor_tensor(o, a, b, op), *t)

        def ts(q, o, a, s1, s2, op0, op1, *t):
            if op1 is None:
                return q.do(lambda e: e.tensor_scalar(o, a, s1, None, op0), *t)
            return q.do(lambda e: e.tensor_scalar(o, a, s1, s2, op0, op1), *t)

        def sst(q, o, a, s, b, op0, op1, *t):
            return q.do(lambda e: e.scalar_tensor_tensor(out=o, in0=a, scalar=s, in1=b, op0=op0, op1=op1), *t)

        def red(o, i, op, *t):
            return V.do(lambda e: e.tensor_reduce(o, i, AX, op), *t)

        def rmax(o, i, *t):
            return V.do(lambda e: e.reduce_max(o, i, AX, negate=True), *t)

        def ttr(o, a, b, s, *t):
            return V.do(lambda e: e.tensor_tensor_reduce(o, a, b, 1.0, 0.0, ALU.mult, ALU.add, s), *t)

        def rec(o, i, *t):
            return V.do(lambda e: e.reciprocal(o, i), *t)

        def fill(q, o, v, *t):
            return q.do(lambda e: e.memset(o, v), *t)

        X = sb(ctx, "X", [128, 16, 256])
        XT = sb(ctx, "XT", [128, 2, 2048])
        ident = sb(ctx, "ident", [128, 128])
        epsc = sb(ctx, "epsc", [128, 1])
        onesf = sb(ctx, "onesf", [128, 128])
        ZB = sb(ctx, "ZB", [128, 256])
        stt = sb(ctx, "stt", [128, 4, 16])

        t = G.do(lambda e: e.memset(ident[:, :], 0.0))
        t_id = G.do(lambda e: e.affine_select(out=ident[:, :], in_=ident[:, :], compare_op=ALU.not_equal, fill=1.0,
                                              base=0, pattern=[[-1, 128]], channel_multiplier=1), t)
        t_eps = fill(G, epsc[:, :], 1e-5)
        S.wait(t_eps)
        t_ones = G.do(lambda e: e.memset(onesf[:, :], 1.0))
        t_x = [P.dma(Y, X[:, 4 * i:4 * i + 4, :], A["x"].rearrange("b (t p) d -> p (b t) d", p=128)[:, 4 * i:4 * i + 4, :])
               for i in range(4)]

        def transpose(o, i, k=128):
            return PE.do(lambda e: e.transpose(o, i, ident[0:k, 0:k]))

        def to_xt(src, dst, tt, b, tok, scale=None, bias=None, slot=None, after=None):
            PE.wait(t_id, free[b], tok)
            k = tt if slot is None else slot
            transpose(bank(b)[:, 0:128], src[:, k, 0:128])
            t = transpose(bank(b)[:, 128:256], src[:, k, 128:256])
            S.wait(after)
            if scale is None:
                t = copy(S, dst[:, :, tt * 128:tt * 128 + 128], bank(b)[:, 0:256].rearrange("p (c n) -> p c n", c=2), t)
            else:
                for c in range(2):
                    t = act(dst[:, c, tt * 128:tt * 128 + 128], bank(b)[:, 128 * c:128 * c + 128], ACT.Identity, t,
                            bias=bias[:, c:c + 1], scale=scale[:, c:c + 1])
            free[b] = t
            return t

        LS = sb(ctx, "LS", [128, 4, 256])
        lsn = [0]

        def norm(tt, src, dst, tok, eps=1e-5):
            k = lsn[0] % 4
            lsn[0] += 1
            st = stt[:, k, :]
            t = V.do(lambda e: e.bn_stats(st[:, 0:6], src), tok)
            t = V.do(lambda e: e.bn_aggr(st[:, 6:8], st[:, 0:6]), t)
            t = act(st[:, 9:10], st[:, 7:8], ACT.Sqrt, t, bias=epsc[:, 0:1])
            t = rec(st[:, 8:9], st[:, 9:10], t)
            return V.do(lambda e: e.tensor_scalar(dst, src, st[:, 6:7], st[:, 8:9], ALU.subtract, ALU.mult), t)

        SA = sb(ctx, "SA", [128, 16, 10])

        def stats(toks):
            for i in range(16):
                V.do(lambda e, i=i: e.bn_stats(SA[:, i, 0:6], X[:, i, :]), toks[i])
            for i in range(16):
                t = V.do(lambda e, i=i: e.bn_aggr(SA[:, i, 6:8], SA[:, i, 0:6]), V.here() if i == 0 else None)
            t = act(SA[:, :, 9], SA[:, :, 7], ACT.Sqrt, t, bias=epsc[:, 0:1])
            return rec(SA[:, :, 8], SA[:, :, 9], t)

        def standard(i, dst, *tok):
            return V.do(lambda e: e.tensor_scalar(dst, X[:, i, :], SA[:, i, 6:7], SA[:, i, 8:9], ALU.subtract, ALU.mult), *tok)

        def norm_all(toks):
            t = stats(toks)
            return [standard(i, X[:, i, :], t) for i in range(16)]

        def add_norm(tt, ps, biasB, tok, fr=None):
            k = lsn[0] % 4
            tmp = LS[:, k, :]
            t = two(V, tmp, ps, X[:, tt, :], ALU.add, tok)
            if fr is not None:
                free[fr] = t
            if biasB is not None:
                t = two(V, tmp, tmp, biasB, ALU.add, t)
            return norm(tt, tmp, X[:, tt, :], t)

        t_xt = [to_xt(X, XT, i, 2 + i % 4, t_x[i // 4]) for i in range(16)]

        adj = nc.dram_tensor("adj", [1024 * 1024 + 128, 1], F32, kind="Internal").ap()
        kdram = nc.dram_tensor("adj_key", [256, 128], F32, kind="Internal").ap()
        vdram = nc.dram_tensor("adj_val", [256, 128], F32, kind="Internal").ap()
        CT = sb(ctx, "CT", [128, 2, 154])
        EE = sb(ctx, "e_EE", [128, 256])
        IXE = sb(ctx, "e_IX", [128, 256], I32)
        ectx = ctx.enter_context(ExitStack())
        NB = 4
        LOTS = 256 // NB
        KC = sb(ectx, "e_KC", [128, 256])
        VP = sb(ectx, "e_VP", [128, 256, 3], BF16)
        KR = sb(ectx, "e_KR", [128, 2, NB, 128])
        LTE = sb(ectx, "e_LT", [128, 128], BF16)
        one_b = sb(ectx, "e_one", [128, 1], BF16)
        EQ = sb(ectx, "e_EQ", [128, 2, NB, 128], BF16)
        EM = sb(ectx, "e_EM", [128, NB, 128], BF16)
        EP = sb(ectx, "e_EP", [128, 256, 4])
        EF = sb(ectx, "e_EF", [128, 64])
        EA = sb(ectx, "e_EA", [128, 64])
        own = sb(ectx, "e_own", [128, 1])
        zt = sb(ectx, "e_zt", [128, 256])
        with ExitStack() as c:
            ER = sb(c, "e_ER", [128, 2, 128], I32)
            EC = sb(c, "e_EC", [128, 2, 128], I32)
            EV = sb(c, "e_EV", [128, 2, 128])
            EH = sb(c, "e_EH", [128, 2, 128])
            EL = sb(c, "e_EL", [128, 2, 128])
            EG = sb(c, "e_EG", [128, 2, 128])
        edge = {"n": 0, "load": {}, "equal": {}, "mult": {}, "sum": {}, "ready": {}, "sent": 0, "last": None}

        def edge_setup():
            er, ec, ev, eh, el, eg = [a[:, :, :].rearrange("p a b -> p (a b)") for a in (ER, EC, EV, EH, EL, EG)]
            t_e = [P.dma(Y, d[:, :, :], A[n].rearrange("(a p e) -> p a e", p=128, e=128))
                   for d, n in ((ER, "L1_attn_adj_rows"), (EC, "L1_attn_adj_cols"), (EV, "L1_attn_adj_vals"))]
            t = copy(V, eh, er, t_e)
            t = ts(V, el, eh, 0.0, None, ALU.is_ge, None, t)
            t = two(V, ev, ev, el, ALU.mult, t)
            t = ts(V, el, eh, 1024.0, None, ALU.is_lt, None, t)
            t_v = two(V, ev, ev, el, ALU.mult, t)
            t = ts(V, eh, eh, 0.0, 1023.0, ALU.max, ALU.min, t_v)
            t = copy(V, el, ec, t)
            t = ts(V, eg, el, 0.0, 1024.0, ALU.is_lt, ALU.mult, t)
            t = two(V, el, el, eg, ALU.add, t)
            t = ts(V, el, el, 0.0, 1023.0, ALU.max, ALU.min, t)
            t = sst(V, el, eh, 1024.0, el, ALU.mult, ALU.add, t)
            t_ek = P.dma(Y, kdram.rearrange("(a p) e -> p a e", p=128), EL[:, :, :], t)
            PE.wait(t, t_id, free[7])
            for i in range(2):
                transpose(bank(7)[:, 128 * i:128 * i + 128], EL[:, i, :])
            for i in range(2):
                t2 = transpose(bank(7)[:, 256 + 128 * i:384 + 128 * i], EV[:, i, :])
            t_kc = copy(V, KC[:, :], bank(7)[:, 0:256], t2)
            t = copy(V, VP[:, :, 0], bank(7)[:, 256:512], t2)
            free[7] = t = two(V, eh, bank(7)[:, 256:512], VP[:, :, 0], ALU.subtract, t)
            t = copy(V, VP[:, :, 1], eh, t)
            t_vp = two(V, VP[:, :, 2], eh, VP[:, :, 1], ALU.subtract, t)
            t = fill(G, LTE[:, :], 1.0)
            t_lte = G.do(lambda e: e.affine_select(out=LTE[:, :], in_=LTE[:, :], compare_op=ALU.is_gt, fill=0.0,
                                                   base=0, pattern=[[1, 128]], channel_multiplier=-1), t)
            t_own = G.do(lambda e: e.iota(own[:, :], [[0, 1]], base=1024 * 1024, channel_multiplier=1,
                                          allow_small_or_imprecise_dtypes=True))
            t_one = fill(G, one_b[:, :], 1.0)
            edge.update(key=t_ek, kc=t_kc, vp=t_vp, lte=t_lte, own=t_own, one=t_one)
            edge_load(0)
            edge_load(1)
            return [t_vp, t_kc, t_ek]

        def edge_zero(i):
            t_zt = edge.setdefault("zt", fill(G, zt[:, :], 0.0)) if i == 0 else edge["zt"]
            edge.setdefault("zero", []).append(
                P.dma(Y, adj[0:1024 * 1024, :].rearrange("(a p k n) o -> a p k (n o)", p=128, k=8, n=256)[i],
                      zt[:, :].unsqueeze(1).broadcast_to([128, 8, 256]), t_zt))
            if i == 3:
                edge["zero"].append(P.dma(Y, adj[1024 * 1024:1024 * 1024 + 128, :], zt[:, 0:1], t_zt))

        def edge_load(i):
            src = kdram[NB * i:NB * i + NB, :].rearrange("a e -> (a e)").rearrange("(o n) -> o n", o=1)
            edge["load"][i] = P.dma(Y, KR[:, i % 2, :, :].rearrange("p a e -> p (a e)"), src.broadcast_to([128, NB * 128]),
                                    edge["equal"].get(i - 2), edge["key"])

        def edge_step():
            i = edge["n"]
            edge["n"] += 1
            if i < LOTS:
                kc = KC[:, NB * i:NB * i + NB].unsqueeze(2).broadcast_to([128, NB, 128])
                eq = EQ[:, i % 2, :, :]
                t = edge["equal"][i] = two(V, eq, KR[:, i % 2, :, :], kc, ALU.is_equal, edge["load"][i], edge["kc"],
                                           edge["sum"].get(i - 2))
                edge["mult"][i] = two(G, EM[:, :, :], eq, LTE[:, :].unsqueeze(1).broadcast_to([128, NB, 128]), ALU.mult, t,
                                      edge["lte"], edge["sum"].get(i - 1)) if i == 0 else None
                if i + 2 < LOTS:
                    edge_load(i + 2)
            if 1 <= i <= LOTS:
                k = i - 1
                PE.wait(edge["mult"][k], edge["vp"], edge["one"], free[7])
                for j in range(NB):
                    mm(bank(7)[:, 4 * j:4 * j + 3], EQ[:, k % 2, j, :], VP[:, NB * k + j, :], True, True)
                    t = mm(bank(7)[:, 4 * j + 3:4 * j + 4], EM[:, j, :], one_b[:, :], True, True, PE.do if j == NB - 1 else PE.raw)
                edge["sum"][k] = t
                free[7] = tp = copy(V, EP[:, NB * k:NB * k + NB, :], bank(7)[:, 0:4 * NB].rearrange("p (a b) -> p a b", b=4), t)
                if i < LOTS:
                    edge["mult"][i] = two(G, EM[:, :, :], EQ[:, i % 2, :, :], LTE[:, :].unsqueeze(1).broadcast_to([128, NB, 128]),
                                          ALU.mult, edge["equal"][i], t)
                if k % 16 == 15:
                    lot = slice(64 * (k // 16), 64 * (k // 16) + 64)
                    red(EE[:, lot], EP[:, lot, 0:3], ALU.add, tp)
                    t = ts(V, EF[:, :], EP[:, lot, 3], 0.5, None, ALU.is_gt, None, tp)
                    t2 = ts(V, EA[:, :], KC[:, lot], -1.0, own[:, 0:1], ALU.mult, ALU.add, edge["own"], tp)
                    t2 = two(V, EA[:, :], EA[:, :], EF[:, :], ALU.mult, t2, t)
                    t2 = two(V, EA[:, :], EA[:, :], KC[:, lot], ALU.add, t2)
                    edge["ready"][k // 16] = copy(V, IXE[:, lot], EA[:, :], t2)

        def edge_send(n=1):
            for _ in range(n):
                k = edge["sent"]
                if k < 256 and k // 64 in edge["ready"]:
                    edge["sent"] += 1
                    edge["last"] = P.scatter_add(adj, EE[:, k:k + 1], IXE[:, k:k + 1], edge["ready"][k // 64], edge["last"],
                                                 edge["zero"])

        with ExitStack() as c:
            PB = [sb(c, f"a_P{i}", [128, 1024]) for i in range(4)]
            OU = sb(c, "a_OU", [128, 512])
            RC = sb(c, "a_RC", [128, 512])
            QS = [sb(c, f"a_QS{i}", [128, 4, 1024], F32R) for i in range(2)]
            KS = [sb(c, f"a_KS{i}", [128, 4, 1024], F32R) for i in range(2)]
            HL = [sb(c, f"a_{n}", [128, 1024], F32R) for n in ("QH", "QL", "KH", "KL")]
            VA = sb(c, "a_VA", [128, 8, 16, 32])
            OT = sb(c, "a_OT", [128, 4, 1024])
            WQ = sb(c, "a_WQ", [128, 2, 256])
            WK = sb(c, "a_WK", [128, 2, 256])
            WV = sb(c, "a_WV", [128, 2, 256])
            WF = sb(c, "a_WF", [128, 4, 256])
            sel = sb(c, "a_sel", [128, 128])
            MX = sb(c, "a_MX", [128, 2, 16, 2])
            MM = sb(c, "a_MM", [128, 16])
            MT = sb(c, "a_MT", [16, 2, 128], F32R)
            mdram = nc.dram_tensor("a_m", [2, 16, 128], F32, kind="Internal").ap()
            zdram = nc.dram_tensor("a_z", [1, 4096], F32, kind="Internal").ap()

            t_w = {n: P.dma(Y, W[:, :, :], A[n].rearrange("(c p) n -> p c n", p=128))
                   for n, W in (("L0_attn_WqT", WQ), ("L0_attn_WkT", WK), ("L0_attn_WvT", WV))}
            t = fill(G, sel[:, :], 0.0)
            t_sel = G.do(lambda e: e.affine_select(out=sel[:, :].rearrange("p (a b) -> p a b", a=4),
                                                   in_=sel[:, :].rearrange("p (a b) -> p a b", a=4),
                                                   compare_op=ALU.not_equal, fill=1.0, base=-16,
                                                   pattern=[[-32, 4], [0, 32]], channel_multiplier=1), t)
            t_ks = []
            for i in range(2):
                fill(G if i else V, KS[i][:, :, :].bitcast(F32), 0.0)
                t = fill(G if i else V, QS[i][:, :, :].bitcast(F32), 0.0)
                t_ks.append(fill(G if i else V, KS[i][64:65, :, :].bitcast(F32), 1.0, t))
            t_zd = P.dma(Y, zdram, QS[0][64:65, :, :].rearrange("p a n -> p (a n)"), t_ks[0])
            t_va1 = fill(G, VA[:, :, :, :], 1.0)

            stack_free = [None, None]
            t_prep, t_stack = {}, {}
            hl_free = [None]
            ost = {}
            U = [(b, g4, qh) for b in range(2) for g4 in range(4) for qh in range(2)]

            def prep(b, g, half, which, bk):
                W, wn = (WQ, "L0_attn_WqT") if which == 0 else (WK, "L0_attn_WkT")
                H, L = HL[2 * which], HL[2 * which + 1]
                src = slice(b * 1024 + half * 512, b * 1024 + half * 512 + 512)
                cols = slice(half * 512, half * 512 + 512)
                PE.wait(t_w[wn], free[bk], t_xt0)
                mm(bank(bk), W[:, 0, g * 128:g * 128 + 128], XT[:, 0, src], True, False)
                t = mm(bank(bk), W[:, 1, g * 128:g * 128 + 128], XT[:, 1, src], False, True, PE.do)
                t = copy(S, H[:, cols], bank(bk), t, hl_free[0])
                t = two(V, L[:, cols], bank(bk), H[:, cols].bitcast(F32), ALU.subtract, t, hl_free[0])
                free[bk] = t
                t_prep[(b, g, half, which)] = t

            def prep_v(b, kt, bk):
                src = slice(b * 1024 + kt * 128, b * 1024 + kt * 128 + 128)
                PE.wait(t_w["L0_attn_WvT"], free[bk], t_xt0)
                mm(bank(bk)[:, 0:256], XT[:, 0, src], WV[:, 0, :], True, False)
                t = mm(bank(bk)[:, 0:256], XT[:, 1, src], WV[:, 1, :], False, True, PE.do)
                free[bk] = t_va[(b, kt)] = copy(S, VA[:, kt, :, 0:16], bank(bk)[:, 0:256].rearrange("p (h d) -> p h d", d=16),
                                                t, t_va1, ost.get("va_free"))

            t_va = {}
            t_xt0 = list(t_xt)

            def build_stack(b, g4):
                i, g = g4 % 2, g4 // 2
                tk = [t_prep[(b, g, half, w)] for half in range(2) for w in range(2)] + [stack_free[i], t_ks[i]]
                ts_ = [P.dma(Y, QS[i][64:65, :, :].rearrange("p a n -> p (a n)"), zdram, tk, t_zd)]
                rows = slice(64 * (g4 % 2), 64 * (g4 % 2) + 64)
                for r, (q, k) in enumerate(((0, 2), (1, 2), (0, 3), (1, 3))):
                    ts_.append(P.dma(Y, QS[i][16 * r:16 * r + 16, :, :], HL[q][rows, :], tk))
                    ts_.append(P.dma(Y, KS[i][16 * r:16 * r + 16, :, :], HL[k][rows, :], tk))
                t_stack[(b, g4)] = ts_
                if g4 % 2:
                    hl_free[0] = ts_ + t_stack[(b, g4 - 1)]

            tm, t_m, t_ex = {}, {}, {}

            def s_half(n):
                u, i = divmod(n, 32)
                b, g4, qh = U[u]
                i, kh = divmod(i, 2)
                j, qt = divmod(i, 4)
                s = g4 % 2
                bk = n % 3
                PE.wait(t_stack[(b, g4)], free[bk])
                t = mm(bank(bk), QS[s][:, j, qh * 512 + qt * 128:qh * 512 + qt * 128 + 128],
                       KS[s][:, j, 512 * kh:512 * kh + 512], True, True, PE.do)
                free[bk] = t = rmax(MX[:, u % 2, i, kh:kh + 1], bank(bk), t)
                if n % 32 == 31:
                    tm[u] = t

            def m_row(u):
                b, g4, qh = U[u]
                t = red(MM[:, :], MX[:, u % 2, :, :], ALU.min, tm[u], tm.get(("pe", u - 1)))
                PE.wait(t, free[7], t_id)
                t = tm[("pe", u)] = transpose(bank(7)[0:16, 0:128], MM[:, :])
                free[7] = t = copy(V, MT[:, u % 2, :], bank(7)[0:16, 0:128], t, t_m.get(u - 2))
                t = P.dma(Y, mdram[u % 2], MT[:, u % 2, :], t, t_m.get(u - 2))
                t_m[u] = P.dma(Y, QS[g4 % 2][64:65, :, qh * 512:qh * 512 + 512],
                               mdram[u % 2].rearrange("(o j) q -> o j q", o=1).rearrange("o (j t) q -> o j (t q)", j=4), t)

            def st(n):
                u, i = divmod(n, 16)
                b, g4, qh = U[u]
                kt, hp = divmod(i, 2)
                s = g4 % 2
                for jj in range(2):
                    j = 2 * hp + jj
                    bk = 3 + (2 * n + jj) % 3
                    PE.wait(t_m[u], free[bk])
                    t = mm(bank(bk), KS[s][:, j, kt * 128:kt * 128 + 128], QS[s][:, j, qh * 512:qh * 512 + 512],
                           True, True, PE.do)
                    t_ex[n] = free[bk] = act(PB[n % 4][:, 512 * jj:512 * jj + 512], bank(bk), ACT.Exp, t,
                                             ost.get(("pv", n - 4)), scale=1.0 / 16)
                if i == 15 and qh == 1:
                    stack_free[s] = t

            def pv(n):
                u, i = divmod(n, 16)
                b, g4, qh = U[u]
                kt = i // 2
                PE.wait(t_ex[n], t_ex[n + 1], t_va[(b, kt)])
                if kt == 0:
                    PE.wait(free[6])
                for j in range(4):
                    t = mm(bank(6)[32 * j:32 * j + 32, :], VA[:, kt, 4 * g4 + j, :],
                           PB[(n + j // 2) % 4][:, 512 * (j % 2):512 * (j % 2) + 512], kt == 0, kt == 7,
                           PE.do if j == 3 else PE.raw)
                ost[("pv", n)] = ost[("pv", n + 1)] = t
                if kt == 7:
                    ost["va_free"] = t
                    ost["ou"] = free[6] = copy(S, OU[:, :], bank(6), t, ost.get("sel"), ost.get("ot"))

            def finish(u):
                b, g4, qh = U[u]
                PE.wait(ost["ou"], free[7], t_sel)
                t = ost["sel"] = mm(bank(7), sel[:, :], OU[:, :], True, True, PE.do)
                free[7] = t = rec(RC[:, :], bank(7), t, ost.get("ot"))
                ost["ot"] = two(G, OT[:, g4, qh * 512:qh * 512 + 512], OU[:, :], RC[:, :], ALU.mult, t, ost.get("ot_free"))

            def project_out(b, i, bk):
                PE.wait(ost["ot"], t_wf, free[bk])
                for g4 in range(4):
                    t = mm(bank(bk)[:, 0:256], OT[:, g4, i * 128:i * 128 + 128], WF[:, g4, :], g4 == 0, g4 == 3,
                           PE.do if g4 == 3 else PE.raw)
                ost["ot_free"] = t
                return add_norm(b * 8 + i, bank(bk)[:, 0:256], ZB[:, :], [t, t_bf], bk)

            for half in range(2):
                for which in range(2):
                    prep(0, 0, half, which, 2 + 2 * half + which)
            build_stack(0, 0)
            t_early = edge_setup()
            for kt in range(8):
                prep_v(0, kt, 6 + kt % 2)
            build_stack(0, 1)
            t = fill(G, WF[:, :, :], 0.0)
            t_wf = [P.dma(Y, WF[32 * j:32 * j + 16, :, :],
                          A["L0_attn_WffT"].rearrange("(g j d) n -> j d g n", j=4, d=16)[j], t) for j in range(4)]
            t_bf = P.dma(Y, ZB[:, :], A["L0_attn_bff"].rearrange("(o d) -> o d", o=1).broadcast_to([128, 256]))
            S.wait(t_early)
            V.wait(t_early)
            LEAD = 24
            jobs = {}

            def at(n, f):
                jobs.setdefault(n, []).append(f)

            for k, (b, g) in enumerate(((0, 1), (1, 0), (1, 1))):
                base = 64 * k + 14
                for q in range(4):
                    at(base + 4 * q, lambda b=b, g=g, q=q: prep(b, g, q // 2, q % 2, 7))
                for g4 in (2 * g, 2 * g + 1):
                    at(64 * (k + 1) + 32 * (g4 % 2) - 32 + 1, lambda b=b, g4=g4: build_stack(b, g4))
            for kt in range(8):
                at(16 * 8 + 2 + 2 * kt, lambda kt=kt: prep_v(1, kt, 7))
            for i in range(4):
                at(-9 + 4 * i, lambda i=i: edge_zero(i))
            t_out = {}
            for i in range(8):
                at(16 * 8 + 5 + 2 * i if i < 7 else 16 * 8 + 18, lambda i=i: t_out.update({i: project_out(0, i, 7)}))
            N = 16 * 16
            for n in range(-LEAD, N + 5):
                if 0 <= n < N:
                    st(n)
                for f in jobs.get(n, ()):
                    f()
                k = 2 * (n + LEAD)
                if k < 2 * N:
                    s_half(k)
                if n >= 3 and n % 2 == 1 and n - 3 < N:
                    pv(n - 3)
                if k < 2 * N:
                    s_half(k + 1)
                if k > 32 and k % 32 == 2 and k // 32 <= 16:
                    m_row(k // 32 - 1)
                if n >= -8 and n % 4 == 0:
                    edge_step()
                if n % 2 == 1:
                    edge_send()
                if n >= 20 and n % 16 == 4:
                    finish((n - 20) // 16)
            for i in range(8):
                t_out[8 + i] = project_out(1, i, 2 + i % 4)
            for i in range(16):
                t_xt[i] = to_xt(X, XT, i, 2 + i % 4, t_out[i], after=t_out[i])
        P.barrier()
        ectx.close()
        CX = LS[0:77, 0:2, :]

        def wload(c, name, W, q, *tok):
            return P.dma(q, W, A[name].rearrange("(c p) n -> p c n", p=128), *tok)

        def ctx_attention(c, pre, t_in, scale, bias, wnames, emit, bias_done=None):
            WQ = sb(c, pre + "WQ", [128, 2, 1024])
            WK = sb(c, pre + "WK", [128, 2, 1024])
            WV = sb(c, pre + "WV", [128, 2, 1024])
            WO = sb(c, pre + "WO", [128, 8, 256])
            KT = sb(c, pre + "KT", [128, 2, 8, 154])
            VC = sb(c, pre + "VC", [77, 2, 1024])
            QB = [sb(c, pre + f"QB{i}", [128, 8, 256]) for i in range(2)]
            SS = [sb(c, pre + f"SS{i}", [128, 16, 77]) for i in range(3)]
            PT = [sb(c, pre + f"PT{i}", [77, 16, 256]) for i in range(2)]
            OT = [sb(c, pre + f"OT{i}", [128, 8, 256]) for i in range(2)]
            st = sb(c, pre + "st", [128, 3, 3, 16])
            t_kz = fill(G, KT[:, :, :, :], 0.0)
            t_wk = wload(c, wnames[1], WK[:, :, :], Y)
            t_wq = wload(c, wnames[0], WQ[:, :, :], Y)
            t_wv = wload(c, wnames[2], WV[:, :, :], Y)
            t_wo = wload(c, wnames[3], WO[:, :, :], Y)
            t_kt, t_vc = [], []
            for p in range(8):
                bk = 5 + p % 3
                PE.wait(t_wk, t_ct, free[bk])
                mm(bank(bk)[:, 0:154], WK[:, 0, p * 128:p * 128 + 128], CT[:, 0, :], True, False)
                t = mm(bank(bk)[:, 0:154], WK[:, 1, p * 128:p * 128 + 128], CT[:, 1, :], False, True, PE.do)
                for h in range(2):
                    t1 = copy(V, KT[64 * h:64 * h + 64, :, p, 77 * h:77 * h + 77],
                              bank(bk)[64 * h:64 * h + 64, 0:154].rearrange("p (b n) -> p b n", b=2), t, t_kz)
                free[bk] = t1
                t_kt.append(t1)
            for b in range(2):
                for h in range(2):
                    bk = 5 + (2 * b + h) % 3
                    PE.wait(t_wv, free[bk])
                    mm(bank(bk)[0:77, :], CT[:, 0, 77 * b:77 * b + 77], WV[:, 0, 512 * h:512 * h + 512], True, False)
                    t = mm(bank(bk)[0:77, :], CT[:, 1, 77 * b:77 * b + 77], WV[:, 1, 512 * h:512 * h + 512], False, True, PE.do)
                    free[bk] = t = copy(S, VC[:, b, 512 * h:512 * h + 512], bank(bk)[0:77, :], t)
                    t_vc.append(t)
            groups = [slice(0, 6), slice(6, 12), slice(12, 16)]
            tok = {"s": {}, "p": {}, "pt": {}}
            nb = [0]

            def next_bank():
                nb[0] += 1
                return 5 + nb[0] % 3

            def project_q(j, ps):
                for p in ps:
                    bk = next_bank()
                    o = bank(bk)[:, 0:256]
                    PE.wait(t_wq, free[bk], t_in[2 * j], t_in[2 * j + 1])
                    mm(o, WQ[:, 0, p * 128:p * 128 + 128], XT[:, 0, j * 256:j * 256 + 256], True, False)
                    t = mm(o, WQ[:, 1, p * 128:p * 128 + 128], XT[:, 1, j * 256:j * 256 + 256], False, True, PE.do)
                    free[bk] = t = copy(S, QB[j % 2][:, p, :], o, t, tok["s"].get(2 * j - 3))
                    tok[("q", j, p)] = t

            def scores(i):
                b, tq, j = i // 8, i % 2, i // 2
                ss, k = SS[i % 3][:, :, :], i % 3
                PE.wait([tok[("q", j, p)] for p in range(8)], t_kt)
                ts_ = []
                for p in range(8):
                    bk = p // 3
                    if p % 3 == 0:
                        PE.wait(free[bk])
                    t = mm(bank(bk)[:, 154 * (p % 3):154 * (p % 3) + 154], QB[j % 2][:, p, tq * 128:tq * 128 + 128],
                           KT[:, b, p, :], True, True, PE.do if p in (2, 5, 7) else PE.raw)
                    if p in (2, 5, 7):
                        ts_.append(t)
                tok["s"][i] = t
                m, s_, r_ = st[:, k, 0, :], st[:, k, 1, :], st[:, k, 2, :]
                ps = [bank(bk)[:, 0:77 * (g.stop - g.start)].rearrange("p (h n) -> p h n", n=77) for bk, g in enumerate(groups)]
                if bias is not None:
                    BM, t_b = bias(i)
                    for bk, g in enumerate(groups):
                        free[bk] = t = two(V, ss[:, g, :], ps[bk], BM[:, g, :], ALU.add, ts_[bk], t_b, tok["pt"].get(i - 3))
                    bias_done[i] = t
                    t = red(m, ss[:, :, :], ALU.max, t)
                    t = two(V, ss[:, :, :], ss[:, :, :], m.unsqueeze(2).broadcast_to([128, 16, 77]), ALU.subtract, t)
                else:
                    for bk, g in enumerate(groups):
                        t = red(m[:, g], ps[bk], ALU.max, ts_[bk], tok["p"].get(i - 3))
                    for bk, g in enumerate(groups):
                        free[bk] = t = two(V, ss[:, g, :], ps[bk], m[:, g].unsqueeze(2).broadcast_to([128, g.stop - g.start, 77]),
                                           ALU.subtract, t, tok["pt"].get(i - 3))
                t = act(ss[:, :, :], ss[:, :, :], ACT.Exp, t, scale=scale)
                t = red(s_, ss[:, :, :], ALU.add, t)
                t = rec(r_, s_, t)
                tok["p"][i] = two(V, ss[:, :, :], ss[:, :, :], r_.unsqueeze(2).broadcast_to([128, 16, 77]), ALU.mult, t)

            def turn(i):
                tq, k = i % 2, i // 2
                PE.wait(tok["p"][i])
                for g in range(4):
                    bk = 3 + g % 2
                    PE.wait(free[bk])
                    for j in range(4):
                        t = transpose(bank(bk)[0:77, 128 * j:128 * j + 128], SS[i % 3][:, 4 * g + j, :])
                    free[bk] = t2 = copy(V if g == 3 else S, PT[k % 2][:, 4 * g:4 * g + 4, tq * 128:tq * 128 + 128],
                                         bank(bk)[0:77, :].rearrange("p (h n) -> p h n", h=4), t, tok.get(("pv", k - 2)))
                    tok[("turned", i, g)] = t2
                tok["pt"][i] = t

            def values(j, ps):
                b = j // 4
                PE.wait([tok[("turned", 2 * j + i, g)] for i in range(2) for g in range(4)], t_vc)
                for p in ps:
                    bk = next_bank()
                    PE.wait(free[bk])
                    for h in range(2):
                        t = mm(bank(bk)[64 * h:64 * h + 64, 0:256], VC[:, b, 128 * p + 64 * h:128 * p + 64 * h + 64],
                               PT[j % 2][:, 2 * p + h, :], True, True, PE.do if h else PE.raw)
                    free[bk] = tok[("o", j, p)] = copy(S, OT[j % 2][:, p, :], bank(bk)[:, 0:256], t, tok.get(("wo", j - 2)))
                tok[("pv", j)] = t

            def project_out(i):
                j = i // 2
                bk = next_bank()
                PE.wait([tok[("o", j, p)] for p in range(8)], t_wo, free[bk])
                for p in range(8):
                    t = mm(bank(bk)[:, 0:256], OT[j % 2][:, p, 128 * (i % 2):128 * (i % 2) + 128], WO[:, p, :], p == 0, p == 7,
                           PE.do if p == 7 else PE.raw)
                tok[("wo", j)] = t
                late.append(emit(i, bank(bk)[:, 0:256], bk, t))

            late = []
            project_q(0, range(8))
            for i in range(22):
                j, half = i // 2, range(4 * (i % 2), 4 * (i % 2) + 4)
                if i < 16:
                    scores(i)
                if j + 1 < 8:
                    project_q(j + 1, half)
                if 2 <= i < 18:
                    turn(i - 2)
                if 0 <= j - 2 < 8:
                    values(j - 2, half)
                if late:
                    late.pop()()
                if i >= 6:
                    project_out(i - 6)
            late.pop()()

        t = P.dma(Y, CX[:, :, :], A["ctx_1024"].rearrange("b s d -> s b d"))
        for b in range(2):
            PE.wait(t, t_id, free[7])
            for k in range(2):
                t2 = PE.do(lambda e, b=b, k=k: e.transpose(bank(7)[:, k * 77:k * 77 + 77], CX[:, b, 128 * k:128 * k + 128],
                                                           ident[0:77, 0:77]))
            free[7] = t_ct = copy(V, CT[:, :, 77 * b:77 * b + 77], bank(7)[:, 0:154].rearrange("p (c n) -> p c n", c=2), t2)

        with ExitStack() as c:
            YY = sb(c, "b_YY", [128, 4, 256])
            t_bo = P.dma(Y, ZB[:, :], A["L0_xattn_bo"].rearrange("(o d) -> o d", o=1).broadcast_to([128, 256]))

            def emit_b(tt, ps, bk, tok):
                y = YY[:, tt % 4, :]
                t = two(V, y, ps, X[:, tt, :], ALU.add, tok, t_xt[tt - 4] if tt > 3 else None)
                free[bk] = t
                t = two(V, y, y, ZB[:, :], ALU.add, t, t_bo)
                edge_send(6)

                def turn_b():
                    t_xt[tt] = to_xt(YY, XT, tt, 3 + tt % 2, t, slot=tt % 4)
                return turn_b

            ctx_attention(c, "b_", list(t_xt), 0.125, None, ("L0_xattn_Wq", "L0_xattn_Wk", "L0_xattn_Wv", "L0_xattn_Wo"), emit_b)
        P.barrier()

        with ExitStack() as c:
            QA = [sb(c, f"c_QA{i}", [128, 2, 512], F32R) for i in range(3)]
            QM = [sb(c, f"c_QM{i}", [128, 2, 512], F32R) for i in range(3)]
            KA = [sb(c, f"c_KA{i}", [128, 2, 1024], F32R) for i in range(2)]
            KM = [sb(c, f"c_KM{i}", [128, 2, 1024], F32R) for i in range(2)]
            VV = sb(c, "c_VV", [128, 8, 1024])
            OT = sb(c, "c_OT", [128, 8, 1024])
            PB = [sb(c, f"c_P{i}", [128, 2, 512]) for i in range(3)]
            AC = sb(c, "c_AC", [128, 2, 512])
            WQ = sb(c, "c_WQ", [128, 2, 1024])
            WK = sb(c, "c_WK", [128, 2, 1024])
            WVO = sb(c, "c_WVO", [128, 2048])
            MX = sb(c, "c_MX", [128, 2, 8, 2])
            MM = sb(c, "c_MM", [128, 8])
            MT = sb(c, "c_MT", [8, 2, 128], F32R)
            mdram = nc.dram_tensor("c_m", [2, 8, 128], F32R, kind="Internal").ap()
            WV = WVO[:, :].rearrange("p (c n) -> p c n", c=2)
            WO = WVO[:, :].rearrange("p (c n) -> p c n", c=8)
            t_wv = wload(c, "L0_xattn_Wv", WV, Y)
            t_wq = wload(c, "L0_xattn_Wq", WQ[:, :, :], Y)
            t_wk = wload(c, "L0_xattn_Wk", WK[:, :, :], Y)
            t_one = []
            for i in range(2):
                fill(G, KM[i][:, :, :].bitcast(F32), 0.0)
                t_one.append(fill(G, KM[i][64:65, :, :].bitcast(F32), 1.0))
            t_qz = [fill(G, QM[i][:, :, :].bitcast(F32), 0.0) for i in range(3)]
            kfree = [None, None]
            qfree = [None] * 3
            pfree = [None] * 3
            tok = {"ot": None, "wo": None}
            mtfree = [None, None]
            vfree = None
            for b in range(2):
                t_v, t_xv = [], {}

                def turn_x(kt):
                    tt_ = 8 * b + kt
                    bk = 2 + kt % 2
                    xk = LS[:, kt % 4, :].rearrange("p (c n) -> p c n", c=2)
                    PE.wait(free[bk])
                    transpose(bank(bk)[:, 0:128], X[:, tt_, 0:128])
                    t = transpose(bank(bk)[:, 128:256], X[:, tt_, 128:256])
                    free[bk] = t_xv[kt] = copy(S, xk, bank(bk)[:, 0:256].rearrange("p (c n) -> p c n", c=2), t,
                                               tok.get(("xv", kt % 4)), tok.get("ls"))

                def project_v(kt):
                    xk = LS[:, kt % 4, :].rearrange("p (c n) -> p c n", c=2)
                    for h in range(2):
                        bk = 4 + h
                        PE.wait(t_xv[kt], t_wv, free[bk])
                        mm(bank(bk), xk[:, 0, :], WV[:, 0, 512 * h:512 * h + 512], True, False)
                        t3 = mm(bank(bk), xk[:, 1, :], WV[:, 1, 512 * h:512 * h + 512], False, True, PE.do)
                        free[bk] = copy(V if h else S, VV[:, kt, 512 * h:512 * h + 512], bank(bk), t3, vfree)
                        t_v.append(free[bk])
                    tok[("xv", kt % 4)] = t3
                    return t3

                t_k, t_q, t_qm, t_mx, t_m, t_ex = {}, {}, {}, {}, {}, {}

                def prep_k(p, half):
                    i = p % 2
                    cols = slice(half * 512, half * 512 + 512)
                    src = slice(b * 1024 + half * 512, b * 1024 + half * 512 + 512)
                    PE.wait(free[7], t_wk, t_xt)
                    mm(bank(7), WK[:, 0, p * 128:p * 128 + 128], XT[:, 0, src], True, False)
                    t = mm(bank(7), WK[:, 1, p * 128:p * 128 + 128], XT[:, 1, src], False, True, PE.do)
                    for h in range(2):
                        ps = bank(7)[64 * h:64 * h + 64, :]
                        copy(S, KA[i][0:64, h, cols], ps, t, kfree[i])
                        t1 = copy(S, KA[i][64:128, h, cols], ps, t)
                    ends = [t1]
                    for h in range(2):
                        ps = bank(7)[64 * h:64 * h + 64, :]
                        ends.append(two(V, KM[i][0:64, h, cols], ps, KA[i][0:64, h, cols].bitcast(F32), ALU.subtract, t1, kfree[i],
                                        t_one[i]))
                    free[7] = ends
                    t_k[(p, half)] = ends

                def prep_q(u):
                    p, qh = divmod(u, 2)
                    i = (b * 16 + u) % 3
                    src = slice(b * 1024 + qh * 512, b * 1024 + qh * 512 + 512)
                    PE.wait(free[7], t_wq, t_xt)
                    mm(bank(7), WQ[:, 0, p * 128:p * 128 + 128], XT[:, 0, src], True, False)
                    t = mm(bank(7), WQ[:, 1, p * 128:p * 128 + 128], XT[:, 1, src], False, True, PE.do)
                    ends, qm = [], []
                    for h in range(2):
                        t1 = copy(S, QA[i][0:64, h, :], bank(7)[64 * h:64 * h + 64, :], t, qfree[i])
                    for h in range(2):
                        ps = bank(7)[64 * h:64 * h + 64, :]
                        ends.append(two(V, QA[i][64:128, h, :], ps, QA[i][0:64, h, :].bitcast(F32), ALU.subtract, t1))
                        qm.append(copy(G, QM[i][0:64, h, :], QA[i][0:64, h, :].bitcast(F32), t1, qfree[i], t_qz[i]))
                    free[7] = ends
                    t_q[u] = ends
                    t_qm[u] = qm

                def s_half(u, n):
                    p, qh = divmod(u, 2)
                    i, kh = divmod(n, 2)
                    h, qt = divmod(i, 4)
                    PE.wait(t_q[u], t_k[(p, 0)], t_k[(p, 1)], free[kh])
                    t = mm(bank(kh), QA[(b * 16 + u) % 3][:, h, qt * 128:qt * 128 + 128],
                           KA[p % 2][:, h, 512 * kh:512 * kh + 512], True, True, PE.do)
                    free[kh] = t_mx[u] = rmax(MX[:, u % 2, i, kh:kh + 1], bank(kh), t)

                def m_row(u):
                    t = red(MM[:, :], MX[:, u % 2, :, :], ALU.min, t_mx[u], mtfree[0])
                    PE.wait(t, free[7])
                    t = transpose(bank(7)[0:8, 0:128], MM[:, :])
                    mtfree[0] = t
                    free[7] = t = copy(V, MT[:, u % 2, :], bank(7)[0:8, 0:128], t, t_m.get(u - 2))
                    t = P.dma(Y, mdram[u % 2], MT[:, u % 2, :], t, t_m.get(u - 2))
                    t_m[u] = P.dma(Y, QM[(b * 16 + u) % 3][64:65, :, :],
                                   mdram[u % 2].rearrange("(o j) q -> o j q", o=1).rearrange("o (j t) q -> o j (t q)", j=2), t,
                                   t_qm[u])

                def st(u, n):
                    p, qh = divmod(u, 2)
                    kt, h = divmod(n, 2)
                    g = 16 * u + n
                    q, qm = QA[(b * 16 + u) % 3], QM[(b * 16 + u) % 3]
                    bk = 2 + g % 3
                    PE.wait(t_m[u], t_qm[u], free[bk])
                    mm(bank(bk), KA[p % 2][:, h, kt * 128:kt * 128 + 128], q[:, h, :], True, False)
                    t = mm(bank(bk), KM[p % 2][:, h, kt * 128:kt * 128 + 128], qm[:, h, :], False, True, PE.do)
                    k = g // 2 % 3
                    t_ex[g] = free[bk] = act(PB[k][:, h, :], bank(bk), ACT.Exp, t, pfree[k], scale=0.125)
                    if n == 15:
                        qfree[(b * 16 + u) % 3] = t
                        if qh == 1:
                            kfree[p % 2] = t

                def pv(u, kt):
                    p, qh = divmod(u, 2)
                    g = 16 * u + 2 * kt
                    k = g // 2 % 3
                    bk = 5 + u % 2
                    PE.wait(t_ex[g], t_ex[g + 1], t_v)
                    if kt == 0:
                        PE.wait(free[bk])
                    for h in range(2):
                        t = mm(bank(bk)[64 * h:64 * h + 64, :], VV[:, kt, 128 * p + 64 * h:128 * p + 64 * h + 64], PB[k][:, h, :],
                               kt == 0, kt == 7, PE.do if h else PE.raw)
                    if kt == 1:
                        k0 = (k + 2) % 3
                        tok["ac"] = ta = [two(V if h == 0 else G, AC[:, h, :], PB[k0][:, h, :], PB[k][:, h, :], ALU.add,
                                              t_ex[g - 2 + h], t_ex[g + h], tok.get("sum")) for h in range(2)]
                        pfree[k0] = [pfree[k0], ta]
                    elif kt > 1:
                        tok["ac"] = ta = [two(V if h == 0 else G, AC[:, h, :], AC[:, h, :], PB[k][:, h, :], ALU.add,
                                              t_ex[g + h], tok["ac"][h]) for h in range(2)]
                    pfree[k] = [t, ta] if kt else t
                    tok["pv", u] = t

                def finish(u):
                    p, qh = divmod(u, 2)
                    bk = 5 + u % 2
                    PE.wait(tok["ac"], free[7])
                    for h in range(2):
                        t = mm(bank(7)[64 * h:64 * h + 64, :], onesf[:, 0:64], AC[:, h, :], True, True, PE.do if h else PE.raw)
                    ot = OT[:, p, qh * 512:qh * 512 + 512]
                    free[bk] = t2 = copy(S, ot, bank(bk), tok["pv", u], tok["wo"])
                    free[7] = t = rec(AC[:, 0, :], bank(7), t)
                    tok["sum"] = tok["ot"] = two(G, ot, ot, AC[:, 0, :], ALU.mult, t, t2)

                prep_k(0, 0)
                prep_k(0, 1)
                prep_q(0)
                prep_q(1)
                if b:
                    for i in range(8):
                        project_out(0, i)
                        s_half(0, 2 * i)
                        s_half(0, 2 * i + 1)
                    project_out(0, 8)
                    t_wv = wload(c, "L0_xattn_Wv", WV, Y, tok["wo"])
                    m_row(0)
                turn_x(0)
                for kt in range(8):
                    if kt < 7:
                        turn_x(kt + 1)
                    t3 = project_v(kt)
                    for n in (3 * kt, 3 * kt + 1, 3 * kt + 2):
                        if b == 0 and n < 22:
                            s_half(n // 16, n % 16)
                        elif b and n < 6:
                            s_half(1, n)
                    if b == 0 and kt == 5:
                        m_row(0)
                t_wo = P.dma(Y, WO, A["L0_xattn_Wo"].rearrange("(c p) n -> p c n", p=128), t3)
                for u in range(16):
                    p, qh = divmod(u, 2)
                    for n in range(16):
                        if n < 10 and u + 1 < 16:
                            s_half(u + 1, n + 6)
                        if n >= 10 and u + 2 < 16:
                            s_half(u + 2, n - 10)
                        if n == 11 and u + 1 < 16:
                            m_row(u + 1)
                        if n in (1, 4) and qh == 0 and p + 1 < 8:
                            prep_k(p + 1, n // 4)
                        if n == 7 and u + 2 < 16:
                            prep_q(u + 2)
                        st(u, n)
                        if n % 4 == 3:
                            edge_send()
                        if n % 2 == 1:
                            g = 8 * u + n // 2 - 1
                            if u and n == 3:
                                finish(u - 1)
                            if g >= 0:
                                pv(g // 8, g % 8)
                pv(15, 7)
                finish(15)
                vfree = PE.here()

                def project_out(b, i):
                    tt_ = b * 8 + i
                    bk = 2 + i % 3
                    if i < 8:
                        PE.wait(tok["ot"], t_wo, free[bk])
                        for p in range(8):
                            t = mm(bank(bk)[:, 0:256], OT[:, p, i * 128:i * 128 + 128], WO[:, p, :], p == 0, p == 7,
                                   PE.do if p == 7 else PE.raw)
                        tok["wo"] = t
                        tok["ls"] = tok["norm", i] = add_norm(tt_, bank(bk)[:, 0:256], ZB[:, :], [t, t_bo, tok.get(("xv", 3))], bk)
                    if i:
                        tok[("late", tt_ - 1)] = to_xt(X, XT, tt_ - 1, 2 + (i - 1) % 3, tok["norm", i - 1])

            for i in range(9):
                project_out(1, i)
            for i in range(16):
                t_xt[i] = tok[("late", i)]
        P.barrier()

        def row(name, n=256):
            return A[name].rearrange("(o d) -> o d", o=1).broadcast_to([128, n])

        with ExitStack() as c:
            GT = sb(c, "f_GT", [128, 2, 2048])
            AW = sb(c, "f_AW", [128, 2, 256])
            NW = sb(c, "f_NW", [128, 2, 256])
            AB = sb(c, "f_AB", [128, 256])
            NBB = sb(c, "f_NB", [128, 256])
            W1 = [sb(c, f"f_W1{i}", [128, 2, 1024]) for i in range(2)]
            W2 = [sb(c, f"f_W2{i}", [128, 8, 256]) for i in range(2)]
            HT = [sb(c, f"f_HT{i}", [128, 8, 256]) for i in range(2)]
            YT = [sb(c, f"f_YT{i}", [128, 2, 256]) for i in range(2)]
            TM = sb(c, "f_TM", [128, 4, 256])
            CR = sb(c, "f_CR", [84, 128])
            CC = sb(c, "f_CC", [128, 84])
            t_aw = wload(c, "L0_ffn_attn_w", AW[:, :, :], Y)
            t_cr = [P.dma(Y, CR[0:64, :], A["L0_ffn_b1"].rearrange("e (f p) -> (e f) p", p=128)),
                    P.dma(Y, CR[64:80, :], A["L0_ffn_b2"].rearrange("e (f p) -> (e f) p", p=128)),
                    P.dma(Y, CR[80:82, :], A["L0_ffn_ln_g"].rearrange("(f p) -> f p", p=128)),
                    P.dma(Y, CR[82:84, :], A["L0_ffn_ln_b"].rearrange("(f p) -> f p", p=128)),
                    P.dma(Y, AB[:, :], row("L0_ffn_attn_b")), P.dma(Y, NBB[:, :], row("L0_ffn_next_b"))]
            t_w1, t_w2 = {}, {}

            def load_expert(e, *tok):
                t_w1[e] = P.dma(Y, W1[e % 2][:, :, :], A["L0_ffn_w1"][e].rearrange("(c p) n -> p c n", p=128), *tok)
                t_w2[e] = P.dma(Y, W2[e % 2][:, :, :], A["L0_ffn_w2"][e].rearrange("(c p) n -> p c n", p=128), *tok)

            load_expert(0)
            load_expert(1)
            t_nw = wload(c, "L0_ffn_next_w", NW[:, :, :], Y)
            PE.wait(t_cr, free[7])
            t = transpose(bank(7)[:, 0:84], CR[:, :], 84)
            free[7] = t_cc = copy(V, CC[:, :], bank(7)[:, 0:84], t)
            S.wait(t_cc)
            t_g = [None] * 16
            tmfree = [None] * 4
            t_n, t_at = {}, {}
            t_stats = stats([None] * 16)

            def normed(i):
                t = standard(i, TM[:, i % 4, :], t_stats, tmfree[i % 4])
                t_n[i] = to_xt(TM, XT, i, 2 + i % 2, t, scale=CC[:, 80:82], bias=CC[:, 82:84], slot=i % 4)

            def attended(i):
                tm_ = TM[:, i % 4, :]
                bk = 4 + i % 2
                PE.wait(t_n[i], t_aw, free[bk])
                for k in range(2):
                    t = mm(bank(bk)[:, 0:256], XT[:, k, 128 * i:128 * i + 128], AW[:, k, :], k == 0, k == 1,
                           PE.do if k else PE.raw)
                free[bk] = t = two(V, tm_, bank(bk)[:, 0:256], X[:, i, :], ALU.add, t)
                t_at[i] = two(V, tm_, tm_, AB[:, :], ALU.add, t)

            for i in range(19):
                if i < 16:
                    normed(i)
                if 1 <= i < 17:
                    attended(i - 1)
                if i >= 3:
                    t_g[i - 3] = to_xt(TM, GT, i - 3, 6 + i % 2, t_at[i - 3], slot=(i - 3) % 4)
                    tmfree[(i - 3) % 4] = PE.here()
            gt_pair = [GT[:, k, :].rearrange("p (m t) -> p m t", m=2) for k in range(2)]
            fr, fin = {}, []
            for e in range(8):
                w1, w2, ht, yt = W1[e % 2], W2[e % 2], HT[e % 2], YT[e % 2]
                th = []
                for f in range(8):
                    bk = f % 3
                    o = bank(bk)[:, 0:256]
                    PE.wait(t_w1[e], t_g[e], t_g[e + 8], free[bk])
                    for k in range(2):
                        t = mm(o.rearrange("p (m t) -> p m t", m=2), w1[:, k, 128 * f:128 * f + 128],
                               gt_pair[k][:, :, 128 * e:128 * e + 128], k == 0, k == 1, PE.do if k else PE.raw)
                    free[bk] = t = act(ht[:, f, :], o, ACT.Gelu, t, fr.get(("ht", e - 2)), bias=CC[:, 8 * e + f:8 * e + f + 1])
                    th.append(t)
                ty = []
                for d in range(2):
                    bk = 3 + d
                    PE.wait(t_w2[e], free[bk])
                    for f in range(8):
                        PE.wait(th[f])
                        t = mm(bank(bk)[:, 0:256], w2[:, f, 128 * d:128 * d + 128], ht[:, f, :], f == 0, f == 7,
                               PE.do if f == 7 else PE.raw)
                    free[bk] = t2 = ts(V, yt[:, d, :], bank(bk)[:, 0:256], CC[:, 64 + 2 * e + d:65 + 2 * e + d], None, ALU.add, None,
                                       t, fr.get(("yt", e - 2)))
                    ty.append(t2)
                fr[("ht", e)] = t
                if e + 2 < 8:
                    load_expert(e + 2, t)
                for m in range(2):
                    i = e + 8 * m
                    bk = 5 + m
                    PE.wait(ty, t_nw, free[bk])
                    for k in range(2):
                        t = mm(bank(bk)[:, 0:256], yt[:, k, 128 * m:128 * m + 128], NW[:, k, :], k == 0, k == 1,
                               PE.do if k else PE.raw)
                    fr[("yt", e)] = t
                    tm_ = TM[:, i % 4, :]
                    free[bk] = t = two(V, tm_, bank(bk)[:, 0:256], NBB[:, :], ALU.add, t, tmfree[i % 4])
                    t = act(tm_, tm_, ACT.Gelu, t)
                    t = tmfree[i % 4] = two(V, X[:, i, :], X[:, i, :], tm_, ALU.add, t)
                    fin.append((i, t))
            fin = dict(fin)
            for i, t in enumerate(norm_all([fin[i] for i in range(16)])):
                t_xt[i] = to_xt(X, XT, i, 2 + i % 4, t)
        P.barrier()

        with ExitStack() as c:
            QT = sb(c, "d_QT", [128, 4, 1024])
            KT = sb(c, "d_KT", [128, 4, 1024])
            VV = sb(c, "d_VV", [128, 8, 512])
            EN = sb(c, "d_EN", [128, 16, 256])
            VB = sb(c, "d_VB", [128, 16, 256])
            al = sb(c, "d_al", [128, 8])
            VBB = sb(c, "d_VBB", [128, 256])
            OBB = sb(c, "d_OBB", [128, 256])
            t_e = [P.dma(Y, VBB[:, :], row("L1_attn_wv_b")), P.dma(Y, OBB[:, :], row("L1_attn_out_b"))]

            with ExitStack() as c2:
                WA = sb(c2, "d_WA", [128, 2, 1536])
                WOUT = sb(c2, "d_WOUT", [128, 4, 256])
                WVW = sb(c2, "d_WVW", [128, 2, 256])
                WQE = sb(c2, "d_WQE", [128, 2, 64])
                WKE = sb(c2, "d_WKE", [128, 2, 64])
                TT = sb(c2, "d_TT", [128, 8, 160])
                AJ = sb(c2, "d_AJ", [128, 3, 1024])

                def load_adj(i, *tok):
                    return P.dma(Y, AJ[:, i % 3, :], adj[0:1024 * 1024, :].rearrange("(t p n) o -> t p (n o)", p=128, n=1024)[i], *tok)

                XL = sb(c2, "d_XL", [128, 2, 128])
                QL = sb(c2, "d_QL", [128, 4, 128])
                KL = sb(c2, "d_KL", [128, 4, 128])
                t_wa = wload(c2, "L1_attn_qkv_w", WA[:, :, :], Y)
                t_wv = wload(c2, "L1_attn_wv_w", WVW[:, :, :], Y)
                t_tt = P.dma(Y, TT[:, :, :], A["conv_toeplitz"])
                t_wo = wload(c2, "L1_attn_out_w", WOUT[:, :, :], Y)
                t_we = [wload(c2, "L1_attn_wq", WQE[:, :, :], Y), wload(c2, "L1_attn_wk", WKE[:, :, :], Y)]
                t_xl = V.do(lambda e: e.tensor_reduce(XL[:, :, :], XT[:, :, :].rearrange("p c (m l) -> p c m l", l=16), AX, ALU.add),
                            t_xt)
                t_aj = {i: load_adj(i) for i in range(3)}
                tl = []
                for W0, L, bk, sc in ((0, QL, 0, 1.0 / 128), (512, KL, 1, 1.0 / 16)):
                    PE.wait(t_wa, t_xl, free[bk])
                    for p in range(4):
                        for k in range(2):
                            t = mm(bank(bk)[:, 128 * p:128 * p + 128], WA[:, k, W0 + 128 * p:W0 + 128 * p + 128], XL[:, k, :],
                                   k == 0, k == 1, PE.do if k and p == 3 else PE.raw)
                    free[bk] = t = act(L[:, :, :], bank(bk).rearrange("p (a n) -> p a n", a=4), ACT.Copy, t, scale=sc)
                    tl.append(t)
                A2 = sb(c2, "d_A2", [128, 8, 64])
                sm = sb(c2, "d_sm", [128, 3, 8])
                PE.wait(tl, free[2])
                for h in range(2):
                    if h:
                        PE.wait(t)
                    for bp in range(8):
                        b, p = divmod(bp, 4)
                        t = mm(bank(2)[64 * h:64 * h + 64, 64 * bp:64 * bp + 64], QL[64 * h:64 * h + 64, p, 64 * b:64 * b + 64],
                               KL[64 * h:64 * h + 64, p, 64 * b:64 * b + 64], True, True, PE.do if bp == 7 else PE.raw)

                def softmax(dst, ps, n, w, m, tok, *after):
                    for d, s_, mo in zip(dst, ps, m):
                        tok = red(mo, s_, ALU.max, tok)
                    for d, s_, mo in zip(dst, ps, m):
                        tok = two(V, d, s_, mo.unsqueeze(2).broadcast_to([128, mo.shape[1], w]), ALU.subtract, tok, *after)
                    return tok

                a2 = A2[:, :, :]
                t = softmax([a2], [bank(2).rearrange("p (a n) -> p a n", n=64)], 8, 64, [sm[:, 0, :]], t)
                free[2] = t
                t = act(a2, a2, ACT.Exp, t)
                t = red(sm[:, 1, :], a2, ALU.add, t)
                t = rec(sm[:, 2, :], sm[:, 1, :], t)
                t_a2 = two(V, a2, a2, sm[:, 2, :].unsqueeze(2).broadcast_to([128, 8, 64]), ALU.mult, t)
                RM = sb(c2, "d_RM", [128, 4])
                R1 = sb(c2, "d_R1", [1, 4])
                t = red(sm[:, 1, :], a2, ALU.add, t_a2)
                t_rm = red(RM[:, 0:1], sm[:, 1, :], ALU.max, t)
                PE.wait(t_a2, free[3], t_ones)
                for h in range(2):
                    if h:
                        PE.wait(t)
                    t = mm(bank(3)[64 * h:64 * h + 64, :], onesf[64 * h:64 * h + 64, 0:64], A2[64 * h:64 * h + 64, :, :], True, True,
                           PE.do)
                free[3] = t = red(RM[:, 1:2], bank(3), ALU.max, t)
                PE.wait(t, t_rm, free[7])
                transpose(bank(7)[0:1, 0:128], RM[:, 0:1])
                t = transpose(bank(7)[0:1, 128:256], RM[:, 1:2])
                t = red(R1[:, 0:2], bank(7)[0:1, 0:256].rearrange("p (a n) -> p a n", a=2), ALU.max, t)
                t = two(V, R1[:, 2:3], R1[:, 0:1], R1[:, 1:2], ALU.mult, t)
                t = rec(R1[:, 3:4], R1[:, 2:3], t)
                PE.wait(t)
                t = mm(bank(7)[:, 256:257], onesf[0:1, :], R1[:, 3:4], True, True, PE.do)
                free[7] = t_sc = copy(V, RM[:, 2:3], bank(7)[:, 256:257], t)
                I4 = sb(c2, "d_I4", [128, 4, 128])
                M = {n: sb(c2, "d_M" + n, [128, 4, 128]) for n in ("A", "AT", "z", "zT", "xz", "xzT", "t")}
                for p in range(4):
                    t = copy(G, I4[:, p, :], ident[:, :])
                t_i4 = t
                t = fill(G, M["A"][:, :, :], 0.0)
                copy(V, M["A"][0:64, :, 0:64], A2[0:64, 0:4, :], t, t_a2)
                t_A = copy(V, M["A"][64:128, :, 64:128], A2[64:128, 0:4, :])
                PE.wait(t_A, free[0])
                for p in range(4):
                    t = transpose(bank(0)[:, 128 * p:128 * p + 128], M["A"][:, p, :])
                bv = [bank(i).rearrange("p (a n) -> p a n", a=4) for i in range(8)]
                free[0] = t_AT = copy(V, M["AT"][:, :, :], bv[0], t)
                t_z = ts(V, M["z"][:, :, :], M["AT"][:, :, :], RM[:, 2:3], None, ALU.mult, None, t_AT, t_sc)
                t_zT = ts(V, M["zT"][:, :, :], M["A"][:, :, :], RM[:, 2:3], None, ALU.mult, None, t_A, t_sc)

                def product(bk, l, r, *tok):
                    PE.wait(free[bk], *tok)
                    for p in range(4):
                        t = mm(bank(bk)[:, 128 * p:128 * p + 128], M[l][:, p, :], M[r][:, p, :], True, True,
                               PE.do if p == 3 else PE.raw)
                    return t

                def minus(k, bk, tok):
                    free[bk] = t = sst(V, M["t"][:, :, :], I4[:, :, :], k, bv[bk], ALU.mult, ALU.subtract, tok, t_i4)
                    return t

                def full(n):
                    return M[n][:, :, :]

                background = []

                def breathe():
                    if background:
                        background.pop(0)()

                t_qt, t_kt, t_vv, t_vb = {}, {}, {}, {}
                nb = [0]

                def bg_bank():
                    nb[0] += 1
                    return 4 + nb[0] % 4

                def proj(p, half, W0, D, sc, toks):
                    def go():
                        bk = bg_bank()
                        PE.wait(t_wa, free[bk], t_xt)
                        for k in range(2):
                            t = mm(bank(bk), WA[:, k, W0 + 128 * p:W0 + 128 * p + 128], XT[:, k, 512 * half:512 * half + 512],
                                   k == 0, k == 1, PE.do if k else PE.raw)
                        free[bk] = toks[(p, half)] = act(D[:, p, 512 * half:512 * half + 512], bank(bk), ACT.Copy, t, scale=sc)
                    return go

                def vproj(i):
                    def go():
                        bk = bg_bank()
                        PE.wait(t_wa, free[bk], t_xt)
                        for k in range(2):
                            t = mm(bank(bk), XT[:, k, 128 * i:128 * i + 128], WA[:, k, 1024:1536], k == 0, k == 1,
                                   PE.do if k else PE.raw)
                        free[bk] = t_vv[i] = copy(S, VV[:, i, :], bank(bk), t)
                    return go

                def valproj(i):
                    def go():
                        bk = bg_bank()
                        PE.wait(t_wv, free[bk], t_xt)
                        for k in range(2):
                            t = mm(bank(bk)[:, 0:256], XT[:, k, 128 * i:128 * i + 128], WVW[:, k, :], k == 0, k == 1,
                                   PE.do if k else PE.raw)
                        free[bk] = t_vb[i] = two(V, VB[:, i, :], bank(bk)[:, 0:256], VBB[:, :], ALU.add, t, t_e)
                    return go

                for p in range(4):
                    for half in range(2):
                        background.append(proj(p, half, 512, KT, 1.0, t_kt))
                background += [vproj(i) for i in range(8)]
                for p in range(4):
                    for half in range(2):
                        background.append(proj(p, half, 0, QT, 0.125, t_qt))
                background += [valproj(i) for i in range(16)]
                for it in range(6):
                    t1 = product(0, "AT", "z", t_AT, t_z)
                    t2 = product(1, "z", "AT")
                    free[0] = t3 = copy(S, full("xz"), bv[0], t1)
                    t4 = sst(V, full("t"), I4[:, :, :], 7.0, bv[0], ALU.mult, ALU.subtract, t1, t_i4, t3)
                    free[0] = t4
                    free[1] = t5 = copy(S, full("xzT"), bv[1], t2)
                    breathe()
                    breathe()
                    t = product(2, "xzT", "t", t4, t5)
                    t = minus(15.0, 2, t)
                    breathe()
                    breathe()
                    t = product(3, "xzT", "t", t)
                    t = minus(13.0, 3, t)
                    breathe()
                    breathe()
                    if it < 5:
                        t1 = product(0, "zT", "t", t, t_zT)
                    t2 = product(1, "t", "zT", t, t_zT)
                    if it < 5:
                        free[0] = t_z = ts(V, full("z"), bv[0], 0.25, None, ALU.mult, None, t1, t2)
                    free[1] = t_zT = act(full("zT"), bv[1], ACT.Copy, t2, scale=0.25)
                while background:
                    breathe()
                P3 = sb(c2, "d_P3", [128, 2, 1024])
                P3T = sb(c2, "d_P3T", [128, 2, 8, 128])
                s3 = sb(c2, "d_s3", [128, 4, 3])
                W3 = sb(c2, "d_W3", [128, 4, 64])
                W2 = sb(c2, "d_W2", [128, 4, 64])
                SS = sb(c2, "d_SS", [128, 2, 8, 64])
                A1T = EN[:, :, :].rearrange("p (a b) n -> p a (b n)", a=4)
                s1 = sb(c2, "d_s1", [128, 2, 3, 8])
                OT = QT
                last = {}
                t_w3 = []
                t_e3, t_r3 = {}, {}

                def rows3(p):
                    b0 = (0, 5)[p % 2]
                    PE.wait(t_kt[(p, 0)], t_kt[(p, 1)], free[b0], free[b0 + 1], tl)
                    for h in range(2):
                        if h:
                            PE.wait(t)
                        for half in range(2):
                            t = mm(bank(b0 + half)[64 * h:64 * h + 64, :], QL[64 * h:64 * h + 64, p, 0:64],
                                   KT[64 * h:64 * h + 64, p, 512 * half:512 * half + 512], True, True, PE.do)
                    t = rmax(s3[:, p, 0:1], bank(b0, 2), t)
                    t = act(P3[:, p % 2, :], bank(b0, 2), ACT.Exp, t, last.get(("p3", p - 2)), bias=s3[:, p, 0:1],
                            accum_out=s3[:, p, 1:2])
                    free[b0] = free[b0 + 1] = t_e3[p] = t
                    t_r3[p] = rec(s3[:, p, 2:3], s3[:, p, 1:2], t)

                def values3(p):
                    tt3 = []
                    for g in range(2):
                        PE.wait(t_e3[p], free[2 + g])
                        for j in range(4):
                            t6 = transpose(bank(2 + g)[:, 128 * j:128 * j + 128], P3[:, p % 2, 128 * (4 * g + j):128 * (4 * g + j) + 128])
                        free[2 + g] = t7 = copy(S if g else V, P3T[:, p % 2, 4 * g:4 * g + 4, :], bv[2 + g], t6, last.get(("w3", p - 2)))
                        tt3.append(t7)
                    last[("p3", p)] = t6
                    PE.wait(tt3, free[4], [t_vv[i] for i in range(8)])
                    for kt in range(8):
                        for h in range(2):
                            t = mm(bank(4)[64 * h:64 * h + 64, 0:64], P3T[:, p % 2, kt, 64 * h:64 * h + 64],
                                   VV[:, kt, 128 * p + 64 * h:128 * p + 64 * h + 64], kt == 0, kt == 7,
                                   PE.do if kt == 7 and h else PE.raw)
                    last[("w3", p)] = t
                    free[4] = t = ts(V, W3[:, p, :], bank(4)[:, 0:64], s3[:, p, 2:3], None, ALU.mult, None, t, t_r3[p])
                    t_w3.append(t)

                for p in range(5):
                    if p < 4:
                        rows3(p)
                    if p:
                        values3(p - 1)
                t_a1, t_s1 = [], {}

                def rows1(i):
                    k, b0 = i % 2, (0, 5)[i % 2]
                    PE.wait([t_qt[(p, i // 4)] for p in range(4)], tl, free[b0], free[b0 + 1])
                    for h in range(8):
                        r = 64 * (h % 2)
                        t = mm(bank(b0 + h % 2)[:, 64 * (h // 2):64 * (h // 2) + 64], QT[r:r + 64, h // 2, 128 * i:128 * i + 128],
                               KL[r:r + 64, h // 2, 0:64], True, True, PE.do)
                    ss = SS[:, k, :, :]
                    sv = ss.rearrange("p (g k) n -> p g k n", k=2)
                    mv = s1[:, k, 0, :].rearrange("p (g k) -> p g k", k=2)
                    t = softmax([sv[:, :, 0, :], sv[:, :, 1, :]],
                                [bank(b0 + q)[:, 0:256].rearrange("p (a n) -> p a n", n=64) for q in range(2)], 4, 64,
                                [mv[:, :, 0], mv[:, :, 1]], t, last.get(("a1", i - 2)))
                    free[b0] = free[b0 + 1] = t
                    t = act(ss, ss, ACT.Exp, t)
                    t = red(s1[:, k, 1, :], ss, ALU.add, t)
                    t = rec(s1[:, k, 2, :], s1[:, k, 1, :], t)
                    t_s1[i] = two(V, ss, ss, s1[:, k, 2, :].unsqueeze(2).broadcast_to([128, 8, 64]), ALU.mult, t)

                def turn1(i):
                    bk, k = 2 + i % 2, i % 2
                    PE.wait(t_s1[i], free[bk])
                    for p in range(4):
                        t = transpose(bank(bk)[:, 128 * p:128 * p + 128], SS[:, k, 2 * p:2 * p + 2, :])
                    last[("a1", i)] = t
                    free[bk] = t = copy(S, A1T[:, :, 128 * i:128 * i + 128], bv[bk], t)
                    t_a1.append(t)

                for i in range(9):
                    if i < 8:
                        rows1(i)
                    if i:
                        turn1(i - 1)
                PE.wait(t_zT, t_w3, free[4])
                for p in range(4):
                    t = mm(bank(4)[:, 64 * p:64 * p + 64], M["zT"][:, p, :], W3[:, p, :], True, True, PE.do)
                free[4] = t_w2 = copy(V, W2[:, :, :], bank(4)[:, 0:256].rearrange("p (a n) -> p a n", a=4), t)
                t_ot = {}
                for p in range(4):
                    for half in range(2):
                        bk = 5 + (2 * p + half) % 3
                        PE.wait(t_w2, t_a1, t_tt, free[bk])
                        for h in range(2):
                            if h:
                                PE.wait(t)
                            t = mm(bank(bk)[64 * h:64 * h + 64, :], W2[64 * h:64 * h + 64, p, :],
                                   A1T[64 * h:64 * h + 64, p, 512 * half:512 * half + 512], True, False, PE.do)
                        for kb in range(8):
                            lo, hi = max(128 * kb - 16, 512 * half), min(128 * kb + 144, 512 * half + 512)
                            if lo >= hi:
                                continue
                            c0 = lo - 128 * kb + 16
                            for h in range(2):
                                t = mm(bank(bk)[64 * h:64 * h + 64, lo - 512 * half:hi - 512 * half],
                                       VV[:, kb, 128 * p + 64 * h:128 * p + 64 * h + 64], TT[:, 2 * p + h, c0:c0 + hi - lo],
                                       False, False, PE.do)
                        free[bk] = t_ot[(p, half)] = copy(V if half else S, OT[:, p, 512 * half:512 * half + 512], bank(bk), t,
                                                          last[("a1", 7)])
                t_en = [None] * 16
                ET = KT[:, 0:2, :]
                t_et = []
                for i in range(9):
                    if i < 8:
                        bk = 2 + i % 2
                        PE.wait([t_ot[(p, i // 4)] for p in range(4)], t_wo, free[bk])
                        for p in range(4):
                            t = mm(bank(bk)[:, 0:256], OT[:, p, 128 * i:128 * i + 128], WOUT[:, p, :], p == 0, p == 3, PE.do)
                        t = two(V, LS[:, i % 4, :], bank(bk)[:, 0:256], OBB[:, :], ALU.add, t, t_en[8 + i - 4] if i >= 4 else None)
                        free[bk] = t
                        t_en[i] = two(V, EN[:, i, :], LS[:, i % 4, :], X[:, i, :], ALU.add, t)
                        t_en[8 + i] = two(G, EN[:, 8 + i, :], LS[:, i % 4, :], X[:, 8 + i, :], ALU.add, t)
                    if i:
                        t_et.append(to_xt(EN, ET, i - 1, 5 + i % 2, t_en[i - 1], after=[last[("w3", 3)]]))
                for j in range(16):
                    sst(V, X[:, j, :], EN[:, j, :], 2.0, X[:, j, :], ALU.mult, ALU.add, t_en[j])
                QE = VV[0:64, 0:2, :].rearrange("p a n -> p (a n)")
                KE = VV[0:64, 2:4, :].rearrange("p a n -> p (a n)")
                t_qe = []
                for half in range(2):
                    for W, D, sc, bk in ((WQE, QE, 0.125, 2 * half), (WKE, KE, 1.0, 2 * half + 1)):
                        PE.wait(t_et, t_we, free[bk])
                        for k in range(2):
                            t = mm(bank(bk)[0:64, :], W[:, k, :], ET[:, k, 512 * half:512 * half + 512], k == 0, k == 1, PE.do)
                        free[bk] = t = act(D[:, 512 * half:512 * half + 512], bank(bk)[0:64, :], ACT.Copy, t, scale=sc)
                        t_qe.append(t)
                AR = sb(c2, "d_AR", [128, 8])
                r_ = sb(c2, "d_r", [128, 8])
                t_ar = []
                for i in range(8):
                    bk = 4 + 2 * (i % 2)
                    PE.wait(t_qe, free[bk], free[bk + 1])
                    for half in range(2):
                        t = mm(bank(bk + half), QE[:, 128 * i:128 * i + 128], KE[:, 512 * half:512 * half + 512], True, True, PE.do)
                    free[bk] = free[bk + 1] = t = ttr(P3[:, i % 2, :], bank(bk, 2), AJ[:, i % 3, :], AR[:, i:i + 1], t, t_aj[i])
                    t_ar.append(t)
                    if i + 3 < 8:
                        t_aj[i + 3] = load_adj(i + 3, t)
                t = red(r_[:, 0:1], AR[:, :], ALU.max, t_ar)
                PE.wait(t, free[1], free[0])
                t = transpose(bank(1)[0:1, 0:128], r_[:, 0:1])
                t = red(r_[0:1, 1:2], bank(1)[0:1, 0:128], ALU.max, t)
                t = ts(V, r_[0:1, 1:2], r_[0:1, 1:2], -1.0, None, ALU.mult, None, t)
                PE.wait(t)
                t = mm(bank(1)[:, 256:257], onesf[0:1, :], r_[0:1, 1:2], True, True, PE.do)
                t = copy(V, r_[:, 2:3], bank(1)[:, 256:257], t)
                t = act(AR[:, :], AR[:, :], ACT.Exp, t, bias=r_[:, 2:3], accum_out=r_[:, 3:4])
                PE.wait(t)
                t = mm(bank(0)[:, 0:1], onesf[:, :], r_[:, 3:4], True, True, PE.do)
                free[0] = free[1] = t = rec(r_[:, 4:5], bank(0)[:, 0:1], t)
                t_al = ts(V, al[:, :], AR[:, :], r_[:, 4:5], None, ALU.mult, None, t)
            P.barrier()
            with ExitStack() as c2:
                SG = sb(c2, "d_SG", [128, 4, 256])
                XLm = sb(c2, "d_XLm", [128, 4, 256])
                last = {}
                fin = []
                gate, diff = {}, {}

                def gated(i):
                    k = i % 4
                    xl, sg = XLm[:, k, :], SG[:, k, :]
                    t1 = ts(V, xl, VB[:, i, :], al[:, i % 8:i % 8 + 1], None, ALU.mult, None, t_al, last.get(("xl", k)))
                    t = act(sg, xl, ACT.Sigmoid, t1, last.get(("sg", k)), scale=-1.0)
                    gate[i] = act(sg, sg, ACT.Square, t)
                    diff[i] = two(G, xl, xl, EN[:, i, :], ALU.subtract, t)

                def mixed(i):
                    k = i % 4
                    xl, sg = XLm[:, k, :], SG[:, k, :]
                    t = last[("xl", k)] = two(V, sg, sg, xl, ALU.mult, gate[i], diff[i])
                    t = last[("sg", k)] = sst(V, X[:, i, :], sg, 2.0, X[:, i, :], ALU.mult, ALU.add, t)
                    fin.append(t)

                for i in range(18):
                    if i < 16:
                        gated(i)
                    if i > 1:
                        mixed(i - 2)
                for i, t in enumerate(norm_all(fin)):
                    t_xt[i] = to_xt(X, XT, i, 2 + i % 4, t)
        P.barrier()

        with ExitStack() as c:
            FB = [sb(c, f"g_FB{i}", [128, 16, 77]) for i in range(2)]
            BM = [sb(c, f"g_BM{i}", [128, 16, 77]) for i in range(2)]
            MB = sb(c, "g_MB", [128, 2, 77])
            t_mb = P.dma(Y, MB[:, :, :], A["mask_Bx1x1xS2_ff0"].rearrange("b o u s -> (o u) b s").broadcast_to([128, 2, 77]))
            fb_t, bm_t, bm_free = {}, {}, {}

            def load_bias(i):
                fb_t[i] = P.dma(Y, FB[i % 2][:, :, :],
                                A["fside_1x16xSxS2_0"][0, :, 128 * (i % 8):128 * (i % 8) + 128, :].rearrange("h q s -> q h s"),
                                bm_t.get(i - 2))

            def bias_of(i):
                if i == 0:
                    load_bias(0)
                    load_bias(1)
                bm_t[i] = two(G, BM[i % 2][:, :, :], FB[i % 2][:, :, :],
                              MB[:, i // 8, :].unsqueeze(1).broadcast_to([128, 16, 77]), ALU.add, fb_t[i], t_mb,
                              bm_free.get(i - 2))
                if i + 2 < 16:
                    load_bias(i + 2)
                return BM[i % 2][:, :, :], bm_t[i]

            def emit_g(i, ps, bk, tok):
                t = add_norm(i, ps, None, tok, bk)

                def turn_g():
                    t_xt[i] = to_xt(X, XT, i, 3 + i % 2, t)
                return turn_g

            ctx_attention(c, "g_", list(t_xt), 1.0, bias_of, ("L1_xattn_Wq", "L1_xattn_Wk", "L1_xattn_Wv", "L1_xattn_Wo"), emit_g,
                          bm_free)
        P.barrier()

        with ExitStack() as c:
            WG = [sb(c, f"h_WG{i}", [128, 2, 256]) for i in range(2)]
            WU = [sb(c, f"h_WU{i}", [128, 2, 256]) for i in range(2)]
            WD = [sb(c, f"h_WD{i}", [128, 2, 256]) for i in range(2)]
            XH = sb(c, "h_XH", [128, 2, 2048], F32R)
            XLo = sb(c, "h_XL", [128, 2, 2048], F32R)
            WH = [sb(c, f"h_WH{i}", [128, 2, 2, 256], F32R) for i in range(2)]
            WL = [sb(c, f"h_WL{i}", [128, 2, 2, 256], F32R) for i in range(2)]
            WR = sb(c, "h_WR", [128, 2, 8])
            TE = sb(c, "h_TE", [128, 2])
            R = {n: sb(c, "h_" + n, [128, 16, 8]) for n in ("inh", "dist", "w", "fb", "z", "rank")}
            R8 = [sb(c, f"h_R8{i}", [128, 16, 8, 8]) for i in range(2)]
            LT = sb(c, "h_LT", [128, 8, 8])
            rs = sb(c, "h_rs", [128, 2, 16])
            SL = sb(c, "h_SL", [128, 2, 512])
            HT = [sb(c, f"h_HT{i}", [128, 2, 512]) for i in range(2)]
            gc = sb(c, "h_gc", [128, 1])
            t_wr = wload(c, "L1_ffn_Wr", WR[:, :, :], Y)
            t_te = P.dma(Y, TE[:, 0:1], A["L1_ffn_temperature"].rearrange("(o d) -> o d", o=1).broadcast_to([128, 1]))
            t_w = {}

            def load_moe(e, *tok):
                t_w[e] = [P.dma(Y, W[e % 2][:, :, :], A[n][e].rearrange("(c p) n -> p c n", p=128), *tok)
                          for n, W in (("L1_ffn_Wg", WG), ("L1_ffn_Wu", WU), ("L1_ffn_Wd", WD))]

            t_ws = {}

            def split_moe(e, *tok):
                t_ws[e] = []
                for i, W in ((0, WG), (1, WU)):
                    t = copy(S, WH[e % 2][:, i, :, :], W[e % 2][:, :, :], t_w[e], *tok)
                    t_ws[e].append(two(V, WL[e % 2][:, i, :, :], W[e % 2][:, :, :], WH[e % 2][:, i, :, :].bitcast(F32),
                                       ALU.subtract, t, *tok))

            load_moe(0)
            load_moe(1)
            split_moe(0)
            t_xs = []
            for tb in range(4):
                cols = slice(512 * tb, 512 * tb + 512)
                t = copy(S, XH[:, :, cols], XT[:, :, cols], t_xt)
                t_xs.append(two(V, XLo[:, :, cols], XT[:, :, cols], XH[:, :, cols].bitcast(F32), ALU.subtract, t))
            CENTER, LOWER, UPPER = float(np.exp(-1.0)), float(0.5 - np.log(4.0 / 3.0)), 0.5
            t = fill(G, LT[:, :, :], 0.0)
            t_lt = G.do(lambda e: e.affine_select(out=LT[:, :, :], in_=LT[:, :, :], compare_op=ALU.is_ge, fill=1.0,
                                                  base=0, pattern=[[-1, 8], [1, 8]], channel_multiplier=0), t)
            PE.wait(t_wr, t_xt, free[7])
            for i in range(16):
                for k in range(2):
                    t = mm(bank(7)[:, 8 * i:8 * i + 8], XT[:, k, 128 * i:128 * i + 128], WR[:, k, :], k == 0, k == 1, PE.do)
            def r3(n):
                return R[n][:, :, :]

            t_r = rec(TE[:, 1:2], TE[:, 0:1], t_te)
            free[7] = t = ts(V, r3("z"), bank(7)[:, 0:128].rearrange("p (a n) -> p a n", n=8), TE[:, 1:2], None, ALU.mult, None, t, t_r)
            t_inh = act(r3("inh"), r3("z"), ACT.Sigmoid, t)
            t = ts(V, r3("dist"), r3("inh"), CENTER, None, ALU.subtract, None, t_inh)
            t = act(r3("dist"), r3("dist"), ACT.Abs, t)
            t1 = act(r3("w"), r3("dist"), ACT.Exp, t, scale=-1.0 / 0.1)
            t2 = act(r3("fb"), r3("dist"), ACT.Exp, t, scale=-1.0 / 0.3)
            t = sst(V, r3("w"), r3("inh"), LOWER, r3("w"), ALU.is_ge, ALU.mult, t1)
            t = sst(V, r3("w"), r3("inh"), UPPER, r3("w"), ALU.is_le, ALU.mult, t)
            t_w8 = red(rs[:, 0, :], r3("w"), ALU.add, t)
            a = R["fb"][:, :, :].unsqueeze(2).broadcast_to([128, 16, 8, 8])
            b_ = R["fb"][:, :, :].unsqueeze(3).broadcast_to([128, 16, 8, 8])
            t = two(V, R8[0][:, :, :, :], a, b_, ALU.is_gt, t2)
            t = two(V, R8[1][:, :, :, :], a, b_, ALU.is_equal, t)
            t = two(V, R8[1][:, :, :, :], R8[1][:, :, :, :], LT[:, :, :].unsqueeze(1).broadcast_to([128, 16, 8, 8]), ALU.mult, t, t_lt)
            t = two(V, R8[0][:, :, :, :], R8[0][:, :, :, :], R8[1][:, :, :, :], ALU.add, t)
            t = red(r3("rank"), R8[0][:, :, :, :], ALU.add, t)
            t = sst(V, r3("fb"), r3("rank"), 2.0, r3("fb"), ALU.is_lt, ALU.mult, t)

            def share(n, k, tok):
                tok = red(rs[:, k, :], r3(n), ALU.add, tok)
                tok = ts(V, rs[:, k, :], rs[:, k, :], 1e-8, None, ALU.max, None, tok)
                tok = rec(rs[:, k, :], rs[:, k, :], tok)
                return two(V, r3(n), r3(n), rs[:, k, :].unsqueeze(2).broadcast_to([128, 16, 8]), ALU.mult, tok)

            t = share("fb", 1, t)
            t = ts(V, rs[:, 0, :], rs[:, 0, :], 1e-8, None, ALU.is_lt, None, t, t_w8)
            pick = rs[:, 0, :].unsqueeze(2).broadcast_to([128, 16, 8])
            t = two(V, r3("fb"), r3("fb"), pick, ALU.mult, t)
            t = two(V, r3("z"), r3("w"), pick, ALU.mult, t)
            t = two(V, r3("w"), r3("w"), r3("z"), ALU.subtract, t)
            t = two(V, r3("w"), r3("w"), r3("fb"), ALU.add, t)
            t_rw = share("w", 0, t)
            fr = {}
            t_acc = [None] * 16
            n = 0
            jobs = [(e, tb) for e in range(8) for tb in range(4)]
            t_h = {}

            def up(n):
                e, tb = jobs[n]
                ends = []
                for i in range(2):
                    for w in range(2):
                        bk = w + 2 * i
                        PE.wait(t_ws[e], t_xs[tb], free[bk])
                        parts = [(W, x, k) for k in range(2) for W, x in ((WH, XH), (WL, XH), (WH, XLo))]
                        for q, (W, x, k) in enumerate(parts):
                            t = mm(bank(bk), W[e % 2][:, w, k, 128 * i:128 * i + 128], x[:, k, 512 * tb:512 * tb + 512],
                                   q == 0, q == 5, PE.do if q == 5 else PE.raw)
                        if w == 0:
                            free[bk] = t1 = act(SL[:, i, :], bank(bk), ACT.Silu, t, fr.get(("sl", i)))
                    free[bk] = fr[("sl", i)] = t = two(V, HT[n % 2][:, i, :], bank(bk), SL[:, i, :], ALU.mult, t, t1,
                                                       fr.get(("ht", n - 2)))
                    ends.append(t)
                t_h[n] = ends

            def down(n):
                e, tb = jobs[n]
                for i in range(4):
                    tt_ = 4 * tb + i
                    bk = 4 + i
                    PE.wait(t_h[n], free[bk])
                    for k in range(2):
                        t = mm(bank(bk)[:, 0:256], HT[n % 2][:, k, 128 * i:128 * i + 128], WD[e % 2][:, k, :], k == 0, k == 1, PE.do)
                    free[bk] = t_acc[tt_] = sst(V, X[:, tt_, :], bank(bk)[:, 0:256], R["w"][:, tt_, e:e + 1], X[:, tt_, :],
                                                ALU.mult, ALU.add, t, t_rw, t_acc[tt_])
                fr[("ht", n)] = t
                if tb == 3 and e + 2 < 8:
                    load_moe(e + 2, t)

            for n in range(33):
                if n < 32:
                    up(n)
                if n % 4 == 1 and n // 4 + 1 < 8:
                    split_moe(n // 4 + 1, PE.here())
                if n:
                    down(n - 1)
            t_fin = norm_all(t_acc)

        Y.wait([P.dma(Y, out.rearrange("b (t p) d -> p (b t) d", p=128)[:, 4 * i:4 * i + 4, :], X[:, 4 * i:4 * i + 4, :],
                      t_fin[4 * i:4 * i + 4]) for i in range(4)])

        block = ctx.enter_context(nc.Block())

        @block.sync
        def _(e):
            Y.run(e)

        @block.tensor
        def _(e):
            PE.run(e)

        @block.vector
        def _(e):
            V.run(e)

        @block.scalar
        def _(e):
            S.run(e)

        @block.gpsimd
        def _(e):
            G.run(e)


_T = {"L0_attn_Wq": "L0_attn_WqT", "L0_attn_Wk": "L0_attn_WkT", "L0_attn_Wv": "L0_attn_WvT", "L0_attn_Wff": "L0_attn_WffT"}
_UNUSED = ("L0_ffn_gate_w",)


def kernel(**inputs):
    import concourse.bacc as _bacc
    from concourse.bass_utils import run_bass_kernel_spmd as _run

    nc = _bacc.Bacc("TRN2", target_bir_lowering=False, num_devices=1)
    arrays, A = {}, {}
    for name in inputs:
        if name in _UNUSED:
            continue
        if name == "L1_attn_conv_w":
            w = np.asarray(inputs[name])[:, 0, :, 0]
            a = np.zeros((128, 8, 160), w.dtype)
            for p in range(128):
                for j in range(33):
                    a[p, :, p + 32 - j] = w[:, j]
            arrays["in_conv"] = a
            A["conv_toeplitz"] = nc.dram_tensor("in_conv", a.shape, F32, kind="ExternalInput").ap()
            continue
        a = np.asarray(inputs[name])
        key = name
        if name in _T:
            a, key = a.T, _T[name]
        if name in ("L0_attn_Wq", "L0_attn_Wk"):
            a = a.reshape(256, 4, 4, 16).transpose(0, 1, 3, 2).reshape(256, 256)
        a = np.ascontiguousarray(a)
        arrays[f"in_{key}"] = a
        A[key] = nc.dram_tensor(f"in_{key}", a.shape, mybir.dt.from_np(a.dtype), kind="ExternalInput").ap()
    out = nc.dram_tensor("out_0", (2, 1024, 256), F32, kind="ExternalOutput").ap()
    build(nc, A, out)
    r = _run(nc, [arrays], core_ids=[0])
    return r.results[0]["out_0"]
```
